# Optimizing a Trainium2 kernel written in Bass

```python
import numpy as np
import jax
import jax.numpy as jnp

def _softmax(x, axis=-1):
    return jax.nn.softmax(x, axis=axis)

def _gelu(x):
    return jax.nn.gelu(x, approximate=True)

def _silu(x):
    return jax.nn.silu(x)

def _sigmoid(x):
    return jax.nn.sigmoid(x)

def _layernorm(x, axis=-1, eps=1e-05):
    m = jnp.mean(x, axis=axis, keepdims=True)
    v = jnp.var(x, axis=axis, keepdims=True)
    return (x - m) / jnp.sqrt(v + eps)

def _scatter_add(tgt, idx, src, axis=0):
    return tgt.at[idx].add(src)

def _segment_sum(src, seg, n):
    return jax.ops.segment_sum(src, seg, n)
kernel_name = 'mk_adaln_d1_jaxref_r4_b55f51'

def setup_inputs(seed: int=0):
    np.random.seed(seed)
    _w = jnp.asarray

    def _L0_attn_setup():
        import jax, jax.numpy as jnp
        import numpy as np
        B, L, H, I, K, G = (2, 1024, 256, 512, 4, 8)
        EPS = 1e-05

        def _layernorm(x, g, b):
            m = x.mean(-1, keepdims=True)
            v = jnp.var(x, axis=-1, keepdims=True)
            return (x - m) * jax.lax.rsqrt(v + EPS) * g + b
        key = jax.random.key(seed)
        ks = jax.random.split(key, 8)
        s = 0.02
        return {'hidden_states': jax.random.normal(ks[0], (B, L, H), jnp.float32), 'in_proj_w': jax.random.normal(ks[1], (2 * I, H), jnp.float32) * s, 'conv_w': jax.random.normal(ks[2], (I, I // G, K), jnp.float32) * s, 'conv_b': jax.random.normal(ks[3], (I,), jnp.float32) * s, 'ln_g': jnp.ones((I,), jnp.float32), 'ln_b': jnp.zeros((I,), jnp.float32), 'fc_w': jax.random.normal(ks[4], (H, I), jnp.float32) * s, 'fc_b': jnp.zeros((H,), jnp.float32), 'cproj_w': jax.random.normal(ks[5], (I, H), jnp.float32) * s, 'cproj_b': jnp.zeros((I,), jnp.float32), 'out_w': jax.random.normal(ks[6], (H, I), jnp.float32) * s}
    _L0_attn_in = _L0_attn_setup()

    def _L0_ffn_setup():
        import jax, jax.numpy as jnp
        import numpy as np
        B, S, D, F, E = (2, 512, 256, 1024, 8)
        LN_EPS = 1e-05

        def _layer_norm(x, gamma, beta):
            mu = jnp.mean(x, axis=-1, keepdims=True)
            var = jnp.mean(jnp.square(x - mu), axis=-1, keepdims=True)
            return (x - mu) * jax.lax.rsqrt(var + LN_EPS) * gamma + beta
        key = jax.random.key(seed)
        ks = jax.random.split(key, 8)

        def xavier(k, shape):
            fan_in, fan_out = (shape[-1], shape[-2])
            a = jnp.sqrt(6.0 / (fan_in + fan_out))
            return jax.random.uniform(k, shape, jnp.float32, -a, a)
        return {'tgt': jax.random.normal(ks[0], (B, S, D), jnp.float32), 'Wr': xavier(ks[1], (E, D)), 'br': jnp.zeros((E,), jnp.float32), 'W1': xavier(ks[2], (E, F, D)), 'b1': jnp.zeros((E, F), jnp.float32), 'W2': xavier(ks[3], (E, D, F)), 'b2': jnp.zeros((E, D), jnp.float32), 'gamma': jnp.ones((D,), jnp.float32), 'beta': jnp.zeros((D,), jnp.float32)}
    _L0_ffn_in = _L0_ffn_setup()
    _L0_c = _w((lambda *s: np.random.randn(*s).astype(np.float32) * 0.05)(8, 256))
    _L0_wmod = _w((lambda *s: np.random.randn(*s).astype(np.float32) * 0.05)(256, 6 * 256) * 256 ** (-0.5))
    _d = {'L0_attn_hidden_states': _L0_attn_in['hidden_states'], 'L0_attn_in_proj_w': _L0_attn_in['in_proj_w'], 'L0_attn_conv_w': _L0_attn_in['conv_w'], 'L0_attn_conv_b': _L0_attn_in['conv_b'], 'L0_attn_ln_g': _L0_attn_in['ln_g'], 'L0_attn_ln_b': _L0_attn_in['ln_b'], 'L0_attn_fc_w': _L0_attn_in['fc_w'], 'L0_attn_fc_b': _L0_attn_in['fc_b'], 'L0_attn_cproj_w': _L0_attn_in['cproj_w'], 'L0_attn_cproj_b': _L0_attn_in['cproj_b'], 'L0_attn_out_w': _L0_attn_in['out_w'], 'L0_ffn_Wr': _L0_ffn_in['Wr'], 'L0_ffn_br': _L0_ffn_in['br'], 'L0_ffn_W1': _L0_ffn_in['W1'], 'L0_ffn_b1': _L0_ffn_in['b1'], 'L0_ffn_W2': _L0_ffn_in['W2'], 'L0_ffn_b2': _L0_ffn_in['b2'], 'L0_ffn_gamma': _L0_ffn_in['gamma'], 'L0_ffn_beta': _L0_ffn_in['beta'], 'L0_c': _L0_c, 'L0_wmod': _L0_wmod}
    _x0 = _d['L0_attn_hidden_states']
    _d['L0_attn_hidden_states'] = jax.random.normal(jax.random.fold_in(jax.random.key(seed), 1), (8, 512, 256), dtype=_x0.dtype)
    del _x0
    return _d

def reference(L0_attn_hidden_states, L0_attn_in_proj_w, L0_attn_conv_w, L0_attn_conv_b, L0_attn_ln_g, L0_attn_ln_b, L0_attn_fc_w, L0_attn_fc_b, L0_attn_cproj_w, L0_attn_cproj_b, L0_attn_out_w, L0_ffn_Wr, L0_ffn_br, L0_ffn_W1, L0_ffn_b1, L0_ffn_W2, L0_ffn_b2, L0_ffn_gamma, L0_ffn_beta, L0_c, L0_wmod):

    def _L0_attn_ref(hidden_states, in_proj_w, conv_w, conv_b, ln_g, ln_b, fc_w, fc_b, cproj_w, cproj_b, out_w):
        import jax, jax.numpy as jnp
        import numpy as np
        B, L, H, I, K, G = (2, 1024, 256, 512, 4, 8)
        EPS = 1e-05

        def _layernorm(x, g, b):
            m = x.mean(-1, keepdims=True)
            v = jnp.var(x, axis=-1, keepdims=True)
            return (x - m) * jax.lax.rsqrt(v + EPS) * g + b
        p = hidden_states @ in_proj_w.T
        h, gate = (p[..., :I], p[..., I:])
        gate = jax.nn.silu(gate)
        hc = jnp.transpose(h, (0, 2, 1))
        conv = jax.lax.conv_general_dilated(hc, conv_w, window_strides=(1,), padding=[(K - 1, 0)], feature_group_count=G, dimension_numbers=('NCH', 'OIH', 'NCH'))
        conv = conv + conv_b[None, :, None]
        h = jnp.transpose(conv, (0, 2, 1)) * gate
        residual = h
        hn = _layernorm(h, ln_g, ln_b)
        m = jax.nn.silu(hn @ fc_w.T + fc_b) @ cproj_w.T + cproj_b
        h = m + residual
        return h @ out_w.T

    def _L0_ffn_ref(tgt, Wr, br, W1, b1, W2, b2, gamma, beta):
        import jax, jax.numpy as jnp
        import numpy as np
        B, S, D, F, E = (2, 512, 256, 1024, 8)
        LN_EPS = 1e-05

        def _layer_norm(x, gamma, beta):
            mu = jnp.mean(x, axis=-1, keepdims=True)
            var = jnp.mean(jnp.square(x - mu), axis=-1, keepdims=True)
            return (x - mu) * jax.lax.rsqrt(var + LN_EPS) * gamma + beta
        logits = jnp.einsum('bsd,ed->bse', tgt, Wr) + br
        top_v, top_i = jax.lax.top_k(logits, 2)
        top_w = jax.nn.softmax(top_v, axis=-1)
        n_exp = logits.shape[-1]
        router_w = jnp.sum(jax.nn.one_hot(top_i, n_exp, dtype=top_w.dtype) * top_w[..., None], axis=-2)
        h = jnp.einsum('bsd,efd->bsef', tgt, W1) + b1
        h = jax.nn.relu(h)
        o = jnp.einsum('bsef,edf->bsed', h, W2) + b2
        tgt2 = jnp.einsum('bsed,bse->bsd', o, router_w)
        return _layer_norm(tgt + tgt2, gamma, beta)
    x = L0_attn_hidden_states
    mod = (_silu(L0_c) @ L0_wmod).reshape(L0_c.shape[0], 6, 1, -1)
    sa, ca, ga, sb, cb, gb = (mod[:, 0], mod[:, 1], mod[:, 2], mod[:, 3], mod[:, 4], mod[:, 5])
    ga = (2 * (ga >= 0) - 1) * jnp.maximum(jnp.abs(ga), 0.25)
    gb = (2 * (gb >= 0) - 1) * jnp.maximum(jnp.abs(gb), 0.25)
    h = _layernorm(x, axis=-1) * (1 + ca) + sa
    x = x + ga * _L0_attn_ref(h, L0_attn_in_proj_w, L0_attn_conv_w, L0_attn_conv_b, L0_attn_ln_g, L0_attn_ln_b, L0_attn_fc_w, L0_attn_fc_b, L0_attn_cproj_w, L0_attn_cproj_b, L0_attn_out_w)
    h = _layernorm(x, axis=-1) * (1 + cb) + sb
    x = x + gb * _L0_ffn_ref(h, L0_ffn_Wr, L0_ffn_br, L0_ffn_W1, L0_ffn_b1, L0_ffn_W2, L0_ffn_b2, L0_ffn_gamma, L0_ffn_beta)
    return x

_drawn_inputs = setup_inputs


def setup_inputs(seed=0):
    import zlib

    import numpy as np

    out = dict(_drawn_inputs(seed))
    spreads = {'L0_attn_ln_g': (1.0, 0.6),
     'L0_attn_ln_b': (0.0, 0.8),
     'L0_attn_fc_b': (0.0, 0.8),
     'L0_attn_cproj_b': (0.0, 0.534),
     'L0_ffn_br': (0.0, 0.79),
     'L0_ffn_b1': (0.0, 1.445),
     'L0_ffn_b2': (0.0, 0.46),
     'L0_ffn_gamma': (1.0, 0.6),
     'L0_ffn_beta': (0.0, 0.335)}
    factors = {'L0_attn_in_proj_w': 5.441,
     'L0_attn_conv_w': 5.545,
     'L0_attn_conv_b': 8.0,
     'L0_attn_fc_w': 5.545,
     'L0_attn_cproj_w': 5.253,
     'L0_attn_out_w': 3.331}
    for name, (base, spread) in spreads.items():
        noise = np.random.default_rng([zlib.crc32(name.encode()), seed]).standard_normal(out[name].shape)
        drawn = base * np.exp(spread * noise) if base else spread * noise
        out[name] = jnp.asarray(drawn.astype(out[name].dtype))
    for name, factor in factors.items():
        out[name] = (out[name] * factor).astype(out[name].dtype)
    return out
```

```python
from contextlib import ExitStack

import concourse.bass as bass
from concourse import mybir

F32 = mybir.dt.float32
F16 = mybir.dt.float16
I32 = mybir.dt.int32
U32 = mybir.dt.uint32
ALU = mybir.AluOpType
ACT = mybir.ActivationFunctionType
AX = mybir.AxisListType.X

P = 128
EPS = 1e-5
WS = 16.0
GATE_MIN = 0.25
RSQRT_MAGIC = float(0x5F3759DF)
NEWTON = 3
MASKED = -3.0e38


def adaln_kernel(nc, x, in_wT, convT, conv_b, ln_g, ln_b, fcT, fc_b, cproj, cproj_b, outT,
                 WrT, br, W1T, b1, W2T, b2, gamma, beta, cT, wmod, out):
    NB, SEQ, D = x.shape
    INNER = outT.shape[0]
    NE, _, FF = W1T.shape
    TAPS = convT.shape[3]
    G = convT.shape[2]
    KD, KI, KF, SUB = D // P, INNER // P, FF // P, SEQ // P
    PAD = TAPS - 1
    TOKENS = NB * SEQ
    T = 256
    TS = T // P
    REGION = TOKENS + T
    MAXT = 48
    ROWS = 2 * MAXT
    assert 2 * TOKENS // T + NE <= MAXT and KF * T * 4 == 4 * 2048
    C_ID, C_NUM, C_DEN, RW = D, D + 1, D + 2, D + 8
    WE = KD * FF + KF * D
    BIAS_K = 33

    gathered = nc.dram_tensor("expert_lists", (NE * REGION, RW), F32, kind="Internal").ap()
    moe_acc = nc.dram_tensor("moe_sum", (TOKENS + T, D), F32, kind="Internal").ap()
    resid = nc.dram_tensor("residual_rows", (TOKENS, D), F32, kind="Internal").ap()
    modd = nc.dram_tensor("modulation_rows", (NB, 5, D), F32, kind="Internal").ap()

    with ExitStack() as ctx:
        def sb(name, shape, dt=F32):
            return ctx.enter_context(nc.sbuf_tensor(name, shape, dt))

        def sem(name):
            return ctx.enter_context(nc.semaphore(name))

        bank = [ctx.enter_context(nc.psum_tensor(f"bank{i}", [P, 512], F32)) for i in range(8)]

        pool_f = sb("weight_pool", [P, WE + 2 * WE])
        at = 0

        def part(n):
            nonlocal at
            at += n
            return pool_f[:, at - n:at]

        in_f = part(KD * 2 * INNER)
        conv_f = part(KI * TAPS * P)
        fc_f = part(KI * D)
        out_f = part(KI * D)
        cproj_f = part(KI * D)
        wmod_f = part(KD * 6 * D)
        convb_f = part(INNER)
        cpb_rep = part(KI * 64)
        assert at <= 3 * WE
        stage_w = pool_f[:, 0:WE]
        split_w = pool_f[:, WE:3 * WE].bitcast(F16).rearrange("p (b h n) -> p b h n", b=2, h=2)

        in_w = sb("in_w", [P, 2, KD * 2 * INNER], F16)
        conv_w = sb("conv_w", [P, 2, KI * TAPS * P], F16)
        fc_w = sb("fc_w", [P, 2, KI * D], F16)
        out_w = sb("out_w", [P, 2, KI * D], F16)
        comp_w = sb("comp_w", [P, 2, KD * D], F16)
        bias_rows = sb("bias_rows", [64, INNER + D], F16)
        bias_hi = sb("bias_hi", [64, INNER + D], F16)
        bias_lo = sb("bias_lo", [64, INNER + D], F16)
        router_w = sb("router_w", [P, KD, NE])
        cols = sb("cols", [P, 3 * KI + KD])
        g16 = sb("g16", [P, KI])
        fc_bias = sb("fc_bias", [P, KD])
        b1c = sb("b1c", [P, NE * KF])
        b2r = sb("b2r", [P, NE, D])
        br4 = sb("br4", [P, SUB, NE])
        silu_c = sb("silu_c", [P, KD * NB])
        c_sb = sb("c_sb", [P, KD * NB])
        shiftT = sb("shiftT", [P, KD, NB])
        scaleT = sb("scaleT", [P, KD, NB])
        modrow = sb("modrow", [NB, 5, D])
        mtmp = sb("mtmp", [NB, 4, D])
        gb_row = sb("gamma_beta", [NB, 2, D])
        colsum = sb("colsum", [P, D])

        ident = sb("ident", [P, P])
        ones_f = sb("ones_f", [P, P])
        ones16 = sb("ones16", [P, P], F16)
        before = sb("before", [P, P], F16)
        iota_i = sb("iota_i", [P, SUB * NE + NE + SUB + ROWS + TS], I32)
        iota_f = sb("iota_f", [P, SUB * NE + NE + SUB + ROWS + TS])
        rev = iota_f[:, 0:SUB * NE].rearrange("p (j e) -> p j e", j=SUB)
        region0 = iota_f[:, SUB * NE:SUB * NE + NE]
        token0 = iota_f[:, SUB * NE + NE:SUB * NE + NE + SUB]
        tile_no = iota_f[:, SUB * NE + NE + SUB:SUB * NE + NE + SUB + ROWS]
        fill_id = iota_f[:, SUB * NE + NE + SUB + ROWS:]
        filler = sb("filler", [P, TS, RW])

        xa = sb("xa", [P, SUB, D])
        xr = sb("xr", [P, SUB, D])
        xn = sb("xn", [P, SUB, D])
        xT_f = sb("xT_f", [P, KD, SEQ])
        xT = sb("xT", [P, 2, KD, SEQ], F16)
        hT = sb("hT", [P, 2, KI, PAD + SEQ], F16)
        gate_sb = sb("gate_sb", [P, INNER])
        r_sb = sb("r_sb", [P, SUB, INNER])
        hnT = sb("hnT", [P, 2, KI, SEQ], F16)
        s_f = sb("s_f", [P, KD, SEQ])
        sT = sb("sT", [P, 2, KD, SEQ], F16)
        tmp = sb("tmp", [P, SUB, D])
        x1 = sb("x1", [P, SUB, D])
        xn2 = sb("xn2", [P, SUB, D])
        x1p = sb("x1p", [P, SUB, D])
        h2x = sb("h2x", [P, SUB, RW])
        h2T = sb("h2T", [P, KD, SEQ])
        ga_row = sb("ga_row", [P, D])
        rt_row = sb("rt_row", [P, 3, D])
        st = [sb(f"bn_{n}", [P, SUB, 6]) for n in range(3)]
        mv = [sb(f"mv_{n}", [P, SUB, 2]) for n in range(3)]
        nw = [sb(f"nw_{n}", [P, 4, SUB]) for n in range(3)]
        rstd = [sb(f"rstd_{n}", [P, SUB]) for n in range(3)]
        nbias = [sb(f"nbias_{n}", [P, SUB]) for n in range(3)]
        std = sb("std", [P, SUB])
        m16 = sb("m16", [P, SUB])
        lg = sb("lg", [P, SUB, NE])
        lg2 = sb("lg2", [P, SUB, NE])
        eq = sb("eq", [P, SUB, NE])
        sc = sb("sc", [P, SUB, NE])
        top = sb("top", [P, 4, SUB])
        onehot = sb("onehot", [P, 2, SUB, NE])
        chosen = sb("chosen", [P, SUB, NE], F16)
        rank = sb("rank", [P, SUB, NE])
        pick = sb("pick", [P, 2, SUB, NE])
        slot_f = sb("slot_f", [P, 2, SUB])
        slot_u = sb("slot_u", [P, 2, SUB], U32)
        dlt = sb("dlt", [P, SUB])
        base = sb("base", [P, NE])
        ids = sb("ids", [P, SUB])
        cnt = sb("cnt", [P, NE])
        cnt_i = sb("cnt_i", [P, NE], I32)
        cnt_s = sb("cnt_s", [P, NE], I32)
        nt = sb("nt", [P, NE])
        g0 = sb("g0", [P, NE + 1])
        step = sb("step", [P, NE])
        row_f = sb("row_f", [P, ROWS])
        row_t = sb("row_t", [P, ROWS])
        tab_nt = sb("tab_nt", [P, NE], I32)
        tab_g0 = sb("tab_g0", [P, NE + 1], I32)
        tab_end = sb("tab_end", [P, NE], I32)
        tab_row = sb("tab_row", [P, ROWS], I32)
        xm = sb("xm", [P, TS, RW])
        xmT = sb("xmT", [P, 2, KD, T], F16)
        hf = r_sb[:, :, :].rearrange("p j (a t) -> p (j a) t", t=T)
        hm = hnT[:, :, :, :].rearrange("p h k (a t) -> p h (k a) t", t=T)
        meta = sb("meta", [P, TS, 3])
        ew = sb("ew", [P, TS, 2])
        wt = sb("wt", [P, 2, TS])
        wcur = sb("wcur", [P, TS])
        idcur = sb("idcur", [P, TS], U32)
        y_f = sb("y_f", [P, TS, D])
        y_w = sb("y_w", [P, TS, D])

        fin_v = [xr[:, :, :], xn[:, :, :]]
        fin_x = [xa[:, :, :], tmp[:, :, :]]
        fin_g = [ga_row[:, :], rt_row[:, 0, :]]
        fin_z = [x1[:, :, :], xn2[:, :, :]]
        fin_o = [x1p[:, :, :], xT_f[:, :, :].rearrange("p k (a d) -> p (k a) d", d=D)]

        names = """zeroed ident_ready consts_ready iota_ready iota_conv cond_loaded cols_loaded
        in_loaded conv_loaded fc_loaded out_loaded cproj_loaded rows_loaded router_loaded
        g16_ready cpb_ready silu_c_done modT_ps modT_read modrow_ps modrow_step modrow_done
        mod_stored colsum_ps fb_ps comp_ps comp_read w_hi w_lo bias_tmp
        xa_loaded ln1_step ln1_ready xn_done xT_ps xT_f32 xT_hi xT_lo
        h_ps h_hi h_lo gate_ps gate_done conv_ps r_done bn_in_step lnin_step lnin_ready hn_done
        hnT_ps hnT_hi hnT_lo u_ps s_f32 s_hi s_lo o_ps o_step t_done xr_loaded ga_loaded
        x1_step x1_done bn2_step ln2_step ln2_ready xn2_done rt_loaded h2_step row_done row_stored
        h2T_ps h2T_done lg_ps mask_step mask_done rank_ps slot_step slots_done
        payload scattered base_ready
        table_step tables_ready filled xm_loaded x_taken xmT_ps xmT_hi xmT_lo
        w_loaded w_conv w_ready b2_loaded l1_ps hf_done hm_hi hm_lo y_ps y_step meta_done exp_done
        wcur_step wcur_done y_done yw_done acc_added rows_added wait_passed acc_filled
        fin_loaded_even fin_loaded_odd fin_step fin_var fin_sqrt fin_norm fin_ready fin_mul fin_sum fin_stored
        """.split()
        S = {n: sem(n) for n in names}
        FIN_LOADED = (S["fin_loaded_even"], S["fin_loaded_odd"])

        def rows_of(t, b):
            if isinstance(b, int):
                return t[b * SEQ:(b + 1) * SEQ, :].rearrange("(j p) d -> p j d", p=P)
            return t[bass.ds(b * SEQ, SEQ), :].rearrange("(j p) d -> p j d", p=P)

        x_rows = x.rearrange("b s d -> (b s) d")
        out_rows = out.rearrange("b s d -> (b s) d")

        def mod_bc(b, lo, hi):
            src = modd[b:b + 1, lo:hi, :] if isinstance(b, int) else modd[bass.ds(b, 1), lo:hi, :]
            return src.rearrange("a r d -> a (r d)").partition_broadcast(P)

        def col(t, b):
            return t[:, b:b + 1] if isinstance(b, int) else t[:, bass.ds(b, 1)]

        def three(pe, ps, stat, mov, first, last, lo_first=False):
            sh, sl = stat
            mh, ml = mov
            pe.matmul(ps, sh, mh, start=first, stop=False)
            pe.matmul(ps, sh, ml, start=False, stop=False)
            return pe.matmul(ps, sl, mh, start=False, stop=last)

        block = ctx.enter_context(nc.Block())

        STAGES = [(i, 0 <= i < NB, 0 <= i - 1 < NB, 0 <= i - 2 < NB, i + 1 < NB)
                  for i in range(NB + 2)]

        def run(eng, body):
            full = [s[0] for s in STAGES if all(s[1:]) and s[0] > 2]
            for s in STAGES:
                if s[0] == full[0]:
                    with eng.Fori(full[0], full[-1] + 1) as i:
                        body(i, True, True, True, True)
                elif s[0] not in full:
                    body(*s)

        def wait_alone(eng, semaphore, value):
            eng.wait_ge(semaphore, value)
            eng.nop().then_inc(S["wait_passed"], 1)

        def expert_pairs(eng, expert):
            with eng.Fori(0, NE // 2 - 1) as pair:
                expert(pair * 2, 0, True, True)
                expert(pair * 2 + 1, 1, True, True)
            expert(NE - 2, 0, True, False)
            expert(NE - 1, 1, False, False)

        @block.sync
        def _(sp):
            sp.dma_start(xa[:, :, :], rows_of(x_rows, 0)).then_inc(S["xa_loaded"], 16)
            sp.dma_start(c_sb[:, :], cT).then_inc(S["cond_loaded"], 16)
            sp.dma_start(wmod_f.rearrange("p (k n) -> p k n", k=KD),
                         wmod.rearrange("(k p) n -> p k n", p=P)).then_inc(S["cond_loaded"], 16)
            sp.dma_start(in_f.rearrange("p (k n) -> p k n", k=KD),
                         in_wT.rearrange("(k p) n -> p k n", p=P)).then_inc(S["in_loaded"], 16)
            for n, (src, w) in enumerate([(ln_g, KI), (ln_b, KI), (cproj_b, KI), (fc_b, KD)]):
                sp.dma_start(cols[:, n * KI:n * KI + w], src).then_inc(S["cols_loaded"], 16)
            sp.dma_start(b1c[:, :], b1).then_inc(S["cols_loaded"], 16)
            sp.wait_ge(S["zeroed"], 1)
            for g in range(P // G):
                for c in range(KI):
                    dst = conv_f[g * G:(g + 1) * G, :].rearrange(
                        "p (c t m) -> p c t m", c=KI, t=TAPS)[:, c, :, g * G:(g + 1) * G]
                    sp.dma_start(dst, convT[c, g]).then_inc(S["conv_loaded"], 16)
            sp.dma_start(convb_f[0:64, :], conv_b.partition_broadcast(64)).then_inc(S["rows_loaded"], 16)
            for n, src in enumerate([gamma, beta]):
                sp.dma_start(gb_row[:, n, :], src.partition_broadcast(NB)).then_inc(S["rows_loaded"], 16)
            for dst, src, s in [(out_f, outT, "out_loaded"), (cproj_f, cproj, "cproj_loaded"),
                                (fc_f, fcT, "fc_loaded")]:
                sp.dma_start(dst.rearrange("p (k n) -> p k n", k=KI),
                             src.rearrange("(k p) n -> p k n", p=P)).then_inc(S[s], 16)
            sp.dma_start(router_w[:, :, :], WrT.rearrange("(k p) e -> p k e", p=P)).then_inc(S["router_loaded"], 16)
            for j in range(SUB):
                sp.dma_start(br4[:, j, :], br.partition_broadcast(P)).then_inc(S["router_loaded"], 16)
            sp.dma_start(b2r[:, :, :].rearrange("p e d -> p (e d)"),
                         b2.partition_broadcast(P)).then_inc(S["b2_loaded"], 16)
            sp.wait_ge(S["modrow_done"], 1)
            sp.dma_start(modd, modrow[:, :, :]).then_inc(S["mod_stored"], 16)
            sp.wait_ge(S["mod_stored"], 16)
            sp.dma_start(rt_row[:, :, :].rearrange("p r d -> p (r d)"), mod_bc(0, 1, 4)).then_inc(S["rt_loaded"], 16)
            sp.wait_ge(S["consts_ready"], 3)
            sp.dma_start(moe_acc[TOKENS:TOKENS + T, :].rearrange("(p j) d -> p j d", j=TS),
                         filler[:, :, 0:D]).then_inc(S["acc_filled"], 16)

            def body(i, front, mid, route, pre):
                if mid:
                    if not (isinstance(i, int) and i == 1):
                        sp.wait_ge(S["x1_done"], (i - 1) * SUB)
                    sp.dma_start(xr[:, :, :], rows_of(x_rows, i - 1)).then_inc(S["xr_loaded"], 16)
                    sp.dma_start(ga_row[:, :], mod_bc(i - 1, 0, 1)).then_inc(S["ga_loaded"], 16)
                if pre:
                    sp.wait_ge(S["xn_done"], i + 1)
                    sp.dma_start(xa[:, :, :], rows_of(x_rows, i + 1)).then_inc(S["xa_loaded"], 16)
                if route:
                    b = i - 2
                    sp.wait_ge(S["row_done"], b * SUB + SUB)
                    sp.dma_start(rows_of(resid, b), x1p[:, :, :]).then_inc(S["row_stored"], 16)
                    sp.dma_start(rows_of(moe_acc, b), h2x[:, :, 0:D]).then_inc(S["row_stored"], 16)
                    if not (isinstance(b, int) and b == NB - 1):
                        sp.dma_start(rt_row[:, :, :].rearrange("p r d -> p (r d)"),
                                     mod_bc(b + 1, 1, 4)).then_inc(S["rt_loaded"], 16)
                if isinstance(i, int) and i == NB:
                    sp.dma_start(stage_w[:, 0:KD * FF].rearrange("p (k n) -> p k n", k=KD),
                                 W1T[0].rearrange("(k p) n -> p k n", p=P)).then_inc(S["w_loaded"], 16)
                    sp.dma_start(stage_w[:, KD * FF:WE].rearrange("p (k n) -> p k n", k=KF),
                                 W2T[0].rearrange("(k p) n -> p k n", p=P)).then_inc(S["w_loaded"], 16)

            run(sp, body)

            def load_w(e):
                w1 = W1T[e:e + 1] if isinstance(e, int) else W1T[bass.ds(e, 1)]
                w2 = W2T[e:e + 1] if isinstance(e, int) else W2T[bass.ds(e, 1)]
                sp.dma_start(stage_w[:, 0:KD * FF].rearrange("p (k n) -> p k n", k=KD),
                             w1.rearrange("a (k p) n -> p (a k) n", p=P)).then_inc(S["w_loaded"], 16)
                sp.dma_start(stage_w[:, KD * FF:WE].rearrange("p (k n) -> p k n", k=KF),
                             w2.rearrange("a (k p) n -> p (a k) n", p=P)).then_inc(S["w_loaded"], 16)

            def load_tile(g):
                r = sp.value_load(tab_row[0:1, g:g + 1] if isinstance(g, int) else tab_row[0:1, bass.ds(g, 1)],
                                  min_val=0, max_val=NE * REGION - T)
                sp.dma_start(xm[:, :, :], gathered[bass.ds(r, T), :].rearrange("(p j) c -> p j c", j=TS))\
                  .then_inc(S["xm_loaded"], 16)

            sp.wait_ge(S["w_ready"], 1)
            load_w(1)
            sp.wait_ge(S["tables_ready"], 1)
            sp.wait_ge(S["scattered"], 16 * 2 * SUB * NB)
            for e in range(NE):
                r = sp.value_load(tab_end[0:1, e:e + 1], min_val=0, max_val=NE * REGION - T)
                sp.dma_start(gathered[bass.ds(r, T), :].rearrange("(p j) c -> p j c", j=TS),
                             filler[:, :, :]).then_inc(S["filled"], 16)
            sp.wait_ge(S["filled"], 16 * NE)
            load_tile(0)

            def expert(e, buf, has_next, has_after):
                first = sp.value_load(tab_g0[0:1, e:e + 1] if isinstance(e, int) else tab_g0[0:1, bass.ds(e, 1)],
                                      min_val=0, max_val=MAXT - 2)
                n = sp.value_load(tab_nt[0:1, e:e + 1] if isinstance(e, int) else tab_nt[0:1, bass.ds(e, 1)],
                                  min_val=1, max_val=MAXT - 2)
                if has_after:
                    sp.wait_ge(S["w_ready"], e + 2)
                    load_w(e + 2)
                with sp.Fori(0, n) as t:
                    g = sp.snap(first + t)
                    sp.wait_ge(S["x_taken"], g + 1)
                    load_tile(g + 1)

            expert_pairs(sp, expert)
            total = sp.value_load(tab_g0[0:1, NE:NE + 1], min_val=1, max_val=MAXT - 2)
            wait_alone(sp, S["xm_loaded"], total * 16 + 16)
            sp.wait_ge(S["acc_added"], total * (16 * TS))

            def fin(b, q):
                lo = b * SEQ
                if isinstance(b, int) and b < 2:
                    pass
                else:
                    sp.wait_ge(S["fin_sum"], b - 1)
                rows = lambda t: (t[lo:lo + SEQ, :] if isinstance(b, int) else t[bass.ds(lo, SEQ), :])\
                    .rearrange("(p j) d -> p j d", j=SUB)
                sp.dma_start(fin_v[q], rows(moe_acc)).then_inc(FIN_LOADED[q], 16)
                sp.dma_start(fin_x[q], rows(resid)).then_inc(FIN_LOADED[q], 16)
                sp.dma_start(fin_g[q], mod_bc(b, 4, 5)).then_inc(FIN_LOADED[q], 16)

            def fin_store(b, q):
                lo = b * SEQ
                sp.wait_ge(S["fin_sum"], b + 1)
                rows = (out_rows[lo:lo + SEQ, :] if isinstance(b, int) else out_rows[bass.ds(lo, SEQ), :])
                sp.dma_start(rows.rearrange("(p j) d -> p j d", j=SUB), fin_o[q]).then_inc(S["fin_stored"], 16)

            fin(0, 0)
            fin(1, 1)
            for b in range(NB):
                fin_store(b, b % 2)
                if b + 2 < NB:
                    fin(b + 2, b % 2)
            sp.wait_ge(S["fin_stored"], 16 * NB)
            sp.wait_ge(S["acc_filled"], 16)
            sp.wait_ge(S["row_stored"], 32 * NB)

        @block.gpsimd
        def _(pool):
            pool.memset(ident[:, :], 0.0).then_inc(S["ident_ready"], 1)
            pool.memset(before[:, :], 0.0).then_inc(S["ident_ready"], 1)
            pool.wait_ge(S["ident_ready"], 2)
            pool.affine_select(out=ident[:, :], in_=ident[:, :], compare_op=ALU.not_equal, fill=1.0,
                               base=0, pattern=[[-1, P]], channel_multiplier=1).then_inc(S["ident_ready"], 1)
            pool.affine_select(out=before[:, :], in_=before[:, :], compare_op=ALU.is_ge, fill=1.0,
                               base=0, pattern=[[-1, P]], channel_multiplier=1).then_inc(S["ident_ready"], 1)
            o = 0
            for pattern, base_, mult, n in [([[0, SUB], [-1, NE]], NE, 0, SUB * NE),
                                            ([[REGION, NE]], 0, 0, NE), ([[P, SUB]], 0, 1, SUB),
                                            ([[1, ROWS]], 0, 0, ROWS), ([[1, TS]], TOKENS, TS, TS)]:
                pool.iota(iota_i[:, o:o + n], pattern, base=base_, channel_multiplier=mult)\
                    .then_inc(S["iota_ready"], 1)
                o += n
            pool.wait_ge(S["iota_ready"], 5)
            pool.tensor_copy(iota_f[:, :], iota_i[:, :]).then_inc(S["iota_conv"], 1)
            pool.memset(filler[:, :, :], 0.0).then_inc(S["consts_ready"], 1)
            pool.memset(h2x[:, :, C_DEN + 1:RW], 0.0).then_inc(S["consts_ready"], 1)
            pool.wait_ge(S["consts_ready"], 2)
            pool.wait_ge(S["iota_conv"], 1)
            pool.tensor_copy(filler[:, :, C_ID], fill_id).then_inc(S["consts_ready"], 1)
            pool.tensor_copy(ids[:, :], token0).then_inc(S["consts_ready"], 1)
            pool.tensor_copy(base[:, :], region0).then_inc(S["base_ready"], 1)
            pool.wait_ge(S["consts_ready"], 4)

            def xT_lo(b):
                for k in range(KD):
                    pool.wait_ge(S["xT_hi"], b * KD + k + 1)
                    pool.tensor_tensor(xT[:, 1, k, :], xT_f[:, k, :], xT[:, 0, k, :], ALU.subtract)\
                        .then_inc(S["xT_lo"], 1)

            def x1_add(b, j):
                pool.wait_ge(S["t_done"], b * SUB + j + 1)
                if j == 0:
                    pool.wait_ge(S["ga_loaded"], (b + 1) * 16)
                    pool.wait_ge(S["xr_loaded"], (b + 1) * 16)
                    if not (isinstance(b, int) and b == 0):
                        pool.wait_ge(S["xn2_done"], b * SUB)
                pool.tensor_tensor(tmp[:, j, :], tmp[:, j, :], ga_row[:, :], ALU.mult).then_inc(S["x1_step"], 1)
                pool.wait_ge(S["x1_step"], b * SUB + j + 1)
                pool.tensor_tensor(x1[:, j, :], tmp[:, j, :], xr[:, j, :], ALU.add).then_inc(S["x1_done"], 1)

            def scatter(b, k):
                if k == 0:
                    wait_alone(pool, S["slots_done"], b + 1)
                    pool.tensor_copy(h2x[:, :, C_ID], ids[:, :]).then_inc(S["payload"], 1)
                    pool.tensor_copy(h2x[:, :, C_DEN], dlt[:, :]).then_inc(S["payload"], 1)
                    pool.memset(h2x[:, :, C_NUM], 0.0).then_inc(S["payload"], 1)
                    wait_alone(pool, S["payload"], b * 5 + 3)
                    pool.tensor_scalar(ids[:, :], ids[:, :], float(SEQ), None, ALU.add).then_inc(S["payload"], 1)
                else:
                    wait_alone(pool, S["scattered"], (b * 2 + 1) * (16 * SUB))
                    pool.tensor_copy(h2x[:, :, C_NUM], dlt[:, :]).then_inc(S["payload"], 1)
                    wait_alone(pool, S["payload"], b * 5 + 5)
                for j in range(SUB):
                    pool.indirect_dma_start(
                        out=gathered, out_offset=bass.IndirectOffsetOnAxis(ap=slot_u[:, k, j:j + 1], axis=0),
                        in_=h2x[:, j, :], in_offset=None).then_inc(S["scattered"], 16)

            def body(i, front, mid, route, pre):
                if route:
                    b = i - 2
                    pool.wait_ge(S["rt_loaded"], (b + 1) * 16)
                    for j in range(SUB):
                        pool.wait_ge(S["xn2_done"], b * SUB + j + 1)
                        if j == 0 and not (isinstance(b, int) and b == 0):
                            pool.wait_ge(S["row_stored"], b * 32)
                            pool.wait_ge(S["scattered"], b * (32 * SUB))
                        pool.tensor_tensor(h2x[:, j, 0:D], xn2[:, j, :], rt_row[:, 0, :], ALU.mult)\
                            .then_inc(S["h2_step"], 1)
                        pool.tensor_tensor(x1p[:, j, :], x1[:, j, :], rt_row[:, 2, :], ALU.add)\
                            .then_inc(S["h2_step"], 1)
                        pool.wait_ge(S["h2_step"], (b * SUB + j) * 2 + 2)
                        pool.tensor_tensor(h2x[:, j, 0:D], h2x[:, j, 0:D], rt_row[:, 1, :], ALU.add)\
                            .then_inc(S["row_done"], 1)
                if mid:
                    b = i - 1
                    for m in range(KD):
                        pool.wait_ge(S["s_hi"], b * KD + m + 1)
                        pool.tensor_tensor(sT[:, 1, m, :], s_f[:, m, :], sT[:, 0, m, :], ALU.subtract)\
                            .then_inc(S["s_lo"], 1)
                    x1_add(b, 0)
                    x1_add(b, 1)
                if route:
                    scatter(i - 2, 0)
                if mid:
                    x1_add(i - 1, 2)
                if pre:
                    xT_lo(i + 1)
                if mid:
                    x1_add(i - 1, 3)
                if route:
                    scatter(i - 2, 1)

            xT_lo(0)
            run(pool, body)

            pool.nop().then_inc(S["rows_added"], 1)
            pool.wait_ge(S["row_stored"], 32 * NB)
            pool.wait_ge(S["acc_filled"], 16)
            pool.wait_ge(S["tables_ready"], 1)
            total = pool.value_load(tab_g0[0:1, NE:NE + 1], min_val=1, max_val=MAXT - 2)

            def add_rows(g, j):
                pool.indirect_dma_start(
                    out=moe_acc, out_offset=bass.IndirectOffsetOnAxis(ap=idcur[:, j:j + 1], axis=0),
                    in_=y_w[:, j, :], in_offset=None, compute_op=ALU.add).then_inc(S["acc_added"], 16)

            with pool.Fori(0, total) as g:
                wait_alone(pool, S["yw_done"], g * TS + TS + 1)
                for j in range(TS):
                    add_rows(g, j)
                pool.wait_ge(S["acc_added"], (g + 1) * (16 * TS))
                pool.nop().then_inc(S["rows_added"], 1)

        @block.scalar
        def _(act):
            def split_hi(dst, src, scale=WS):
                act.activation(dst, src, ACT.Copy, scale=scale).then_inc(S["w_hi"], 1)

            def xn_norm(b):
                act.wait_ge(S["ln1_ready"], b + 1)
                if not (isinstance(b, int) and b == 0):
                    act.wait_ge(S["xT_ps"], b * KD)
                for j in range(SUB):
                    a = act.activation(xn[:, j, :], xa[:, j, :], ACT.Identity,
                                       bias=nbias[0][:, j:j + 1], scale=rstd[0][:, j:j + 1])
                a.then_inc(S["xn_done"], 1)

            def xT_split(b):
                for k in range(KD):
                    act.wait_ge(S["xT_ps"], b * KD + k + 1)
                    if k == 0 and not (isinstance(b, int) and b == 0):
                        act.wait_ge(S["xT_lo"], b * KD)
                    act.activation(xT_f[:, k, :], bank[6 + k][:, :], ACT.Identity,
                                   bias=col(shiftT[:, k, :], b), scale=col(scaleT[:, k, :], b))\
                        .then_inc(S["xT_f32"], 1)
                    act.wait_ge(S["xT_f32"], b * KD + k + 1)
                    act.activation(xT[:, 0, k, :], xT_f[:, k, :], ACT.Copy).then_inc(S["xT_hi"], 1)

            def h_hi(b, m):
                act.wait_ge(S["h_ps"], b * KI + m + 1)
                act.activation(hT[:, 0, m, PAD:], bank[m % 2][:, :], ACT.Copy, scale=1 / WS)\
                    .then_inc(S["h_hi"], 1)

            def gate(b, j):
                act.wait_ge(S["gate_ps"], b * SUB + j + 1)
                if not (isinstance(b, int) and b * SUB + j == 0):
                    act.wait_ge(S["r_done"], b * SUB + j)
                act.activation(gate_sb[:, :], bank[2][:, :], ACT.Silu, scale=1 / WS).then_inc(S["gate_done"], 1)

            def hnT_hi(b, j):
                act.wait_ge(S["hnT_ps"], b * SUB + j + 1)
                act.activation(hnT[:, 0, :, j * P:(j + 1) * P],
                               bank[6 + j % 2][:, :].rearrange("p (k t) -> p k t", k=KI), ACT.Copy)\
                    .then_inc(S["hnT_hi"], 1)

            def body(i, front, mid, route, pre):
                if front:
                    h_hi(i, 0)
                    h_hi(i, 1)
                    gate(i, 0)
                if mid:
                    hnT_hi(i - 1, 0)
                    hnT_hi(i - 1, 1)
                if front:
                    h_hi(i, 2)
                if mid:
                    hnT_hi(i - 1, 2)
                if front:
                    h_hi(i, 3)
                if mid:
                    hnT_hi(i - 1, 3)
                if route:
                    b = i - 2
                    act.wait_ge(S["ln2_ready"], b + 1)
                    if not (isinstance(b, int) and b == 0):
                        act.wait_ge(S["row_done"], b * SUB)
                    for j in range(SUB):
                        act.activation(xn2[:, j, :], x1[:, j, :], ACT.Identity,
                                       bias=nbias[2][:, j:j + 1], scale=rstd[2][:, j:j + 1])\
                            .then_inc(S["xn2_done"], 1)
                if mid:
                    b = i - 1
                    for m in range(KD):
                        act.wait_ge(S["u_ps"], b * KD + m + 1)
                        if m == 0 and not (isinstance(b, int) and b == 0):
                            act.wait_ge(S["s_lo"], b * KD)
                        act.activation(s_f[:, m, :], bank[m][:, :], ACT.Silu, bias=fc_bias[:, m:m + 1],
                                       scale=1 / WS).then_inc(S["s_f32"], 1)
                        act.wait_ge(S["s_f32"], b * KD + m + 1)
                        act.activation(sT[:, 0, m, :], s_f[:, m, :], ACT.Copy).then_inc(S["s_hi"], 1)
                if front:
                    gate(i, 1)
                if route:
                    for k in range(KD):
                        act.wait_ge(S["h2T_ps"], (i - 2) * KD + k + 1)
                        act.activation(h2T[:, k, :], bank[6 + k][:, :], ACT.Copy).then_inc(S["h2T_done"], 1)
                if pre:
                    xn_norm(i + 1)
                if front:
                    gate(i, 2)
                    gate(i, 3)
                if pre:
                    xT_split(i + 1)
                if front:
                    act.wait_ge(S["lnin_ready"], i + 1)
                    for j in range(SUB):
                        act.activation(r_sb[:, j, :], r_sb[:, j, :], ACT.Identity,
                                       bias=nbias[1][:, j:j + 1], scale=rstd[1][:, j:j + 1])\
                            .then_inc(S["hn_done"], 1)

            act.wait_ge(S["cond_loaded"], 32)
            act.activation(silu_c[:, :], c_sb[:, :], ACT.Silu).then_inc(S["silu_c_done"], 1)
            xn_norm(0)
            act.wait_ge(S["in_loaded"], 16)
            split_hi(in_w[:, 0, :], in_f)
            act.wait_ge(S["modT_read"], 2)
            xT_split(0)
            act.wait_ge(S["conv_loaded"], 16 * KI * (P // G))
            split_hi(conv_w[:, 0, :], conv_f)
            act.wait_ge(S["rows_loaded"], 48)
            split_hi(bias_hi[:, 0:INNER], convb_f[0:64, :])
            act.wait_ge(S["g16_ready"], 1)
            act.wait_ge(S["fc_loaded"], 16)
            for k in range(KI):
                a = act.activation(fc_w[:, 0, k * D:(k + 1) * D], fc_f[:, k * D:(k + 1) * D], ACT.Copy,
                                   scale=g16[:, k:k + 1])
            a.then_inc(S["w_hi"], 1)
            act.wait_ge(S["out_loaded"], 16)
            split_hi(out_w[:, 0, :], out_f)
            act.wait_ge(S["comp_ps"], 1)
            split_hi(comp_w[:, 0, :], bank[1][:, :])
            act.wait_ge(S["colsum_ps"], 1)
            split_hi(bias_hi[:, INNER:], bank[0][0:64, D:2 * D])

            run(act, body)

            def w_split(n, buf):
                act.wait_ge(S["w_loaded"], n * 32)
                act.activation(split_w[:, buf, 0, :], stage_w, ACT.Copy, scale=WS).then_inc(S["w_conv"], 1)

            def xmT_hi(g):
                act.wait_ge(S["xmT_ps"], g + 1)
                act.activation(xmT[:, 0, :, :].rearrange("p k t -> p (k t)"), bank[6][:, :], ACT.Copy)\
                    .then_inc(S["xmT_hi"], 1)

            act.nop().then_inc(S["hf_done"], 1)
            act.nop().then_inc(S["yw_done"], 1)
            w_split(1, 0)
            act.wait_ge(S["tables_ready"], 1)
            xmT_hi(0)

            def expert(e, buf, has_next, has_after):
                first = act.value_load(tab_g0[0:1, e:e + 1] if isinstance(e, int) else tab_g0[0:1, bass.ds(e, 1)],
                                       min_val=0, max_val=MAXT - 2)
                n = act.value_load(tab_nt[0:1, e:e + 1] if isinstance(e, int) else tab_nt[0:1, bass.ds(e, 1)],
                                   min_val=1, max_val=MAXT - 2)
                if has_next:
                    act.wait_ge(S["y_ps"], first + 1)
                    w_split(e + 2, 1 - buf)
                with act.Fori(0, n) as t:
                    g = act.snap(first + t)
                    for c in range(KF):
                        if c % 2 == 0:
                            if c == 0:
                                act.wait_ge(S["hm_lo"], g * (KF // 2) + 1)
                            act.wait_ge(S["l1_ps"], g * (KF // 2) + c // 2 + 1)
                        act.activation(hf[:, c, :], bank[c // 2][:, (c % 2) * T:(c % 2 + 1) * T], ACT.Relu,
                                       bias=col(b1c, e * KF + c), scale=1 / WS).then_inc(S["hf_done"], 1)
                    act.wait_ge(S["meta_done"], g + 1)
                    act.activation(ew[:, :, :], meta[:, :, 1:3], ACT.Exp).then_inc(S["exp_done"], 1)
                    xmT_hi(g + 1)
                    act.wait_ge(S["wcur_done"], g + 1)
                    act.wait_ge(S["rows_added"], g + 1)
                    for j in range(TS):
                        act.wait_ge(S["y_done"], g * TS + j + 2)
                        act.activation(y_w[:, j, :], y_f[:, j, :], ACT.Copy, scale=wcur[:, j:j + 1])\
                            .then_inc(S["yw_done"], 1)

            expert_pairs(act, expert)

            for b in range(NB):
                q = b % 2
                act.wait_ge(S["fin_var"], b + 1)
                act.activation(rstd[1][:, :], mv[q][:, :, 1], ACT.Sqrt).then_inc(S["fin_sqrt"], 1)
                act.wait_ge(S["fin_ready"], b + 1)
                if b >= 2:
                    act.wait_ge(S["fin_mul"], b - 1)
                for j in range(SUB):
                    a = act.activation(fin_z[q][:, j, :], fin_v[q][:, j, :], ACT.Identity,
                                       bias=nbias[q][:, j:j + 1], scale=nw[q][:, 0, j:j + 1])
                a.then_inc(S["fin_norm"], 1)

        @block.vector
        def _(dve):
            def rsqrt(n, s, at):
                ve, y, a, yi = (nw[n][:, k, :] for k in range(4))
                var, mean = mv[n][:, :, 1], mv[n][:, :, 0]
                c = 0

                def do(ins, last=False):
                    nonlocal c
                    c += 1
                    ins.then_inc(S[s], 1)
                    if not last:
                        dve.wait_ge(S[s], at + c)

                do(dve.tensor_scalar(ve, var, EPS, None, ALU.add))
                do(dve.tensor_scalar(yi.bitcast(I32), ve.bitcast(I32), 1, None, ALU.logical_shift_right))
                do(dve.tensor_scalar(y.bitcast(I32), yi.bitcast(I32), -1.0, RSQRT_MAGIC, ALU.mult, ALU.add))
                for it in range(NEWTON):
                    do(dve.scalar_tensor_tensor(out=a, in0=y, scalar=-0.5, in1=y, op0=ALU.mult, op1=ALU.mult))
                    do(dve.tensor_tensor(a, a, ve, ALU.mult))
                    to = rstd[n][:, :] if it == NEWTON - 1 else y
                    do(dve.scalar_tensor_tensor(out=to, in0=a, scalar=1.5, in1=y, op0=ALU.add, op1=ALU.mult))
                do(dve.scalar_tensor_tensor(out=nbias[n][:, :], in0=mean, scalar=-1.0, in1=rstd[n][:, :],
                                            op0=ALU.mult, op1=ALU.mult))
                return c

            RSQRT_STEPS = 4 + 3 * NEWTON

            def ln1(b):
                dve.wait_ge(S["xa_loaded"], (b + 1) * 16)
                at = b * (2 * SUB + RSQRT_STEPS)
                for j in range(SUB):
                    dve.bn_stats(st[0][:, j, :], xa[:, j, :]).then_inc(S["ln1_step"], 1)
                for j in range(SUB):
                    wait_alone(dve, S["ln1_step"], at + j + 1)
                    dve.bn_aggr(mv[0][:, j, :], st[0][:, j, :]).then_inc(S["ln1_step"], 1)
                dve.wait_ge(S["ln1_step"], at + 2 * SUB)
                if not (isinstance(b, int) and b == 0):
                    dve.wait_ge(S["xn_done"], b)
                rsqrt(0, "ln1_step", at + 2 * SUB)
                dve.wait_ge(S["ln1_step"], at + 2 * SUB + RSQRT_STEPS)
                dve.nop().then_inc(S["ln1_ready"], 1)

            def split_lo(dst, src, hi, n, scale=WS):
                dve.wait_ge(S["w_hi"], n)
                dve.scalar_tensor_tensor(out=dst, in0=src, scalar=scale, in1=hi, op0=ALU.mult,
                                         op1=ALU.subtract)

            def h_lo(b, m):
                dve.wait_ge(S["h_hi"], b * KI + m + 1)
                dve.scalar_tensor_tensor(out=hT[:, 1, m, PAD:], in0=bank[m % 2][:, :], scalar=1 / WS,
                                         in1=hT[:, 0, m, PAD:], op0=ALU.mult, op1=ALU.subtract)\
                    .then_inc(S["h_lo"], 1)

            def hnT_lo(b, j):
                dve.wait_ge(S["hnT_hi"], b * SUB + j + 1)
                dve.tensor_tensor(hnT[:, 1, :, j * P:(j + 1) * P],
                                  bank[6 + j % 2][:, :].rearrange("p (k t) -> p k t", k=KI),
                                  hnT[:, 0, :, j * P:(j + 1) * P], ALU.subtract).then_inc(S["hnT_lo"], 1)

            def r_tile(b, j):
                dve.wait_ge(S["conv_ps"], b * SUB + j + 1)
                dve.wait_ge(S["gate_done"], b * SUB + j + 1)
                if not (isinstance(b, int) and b == 0):
                    dve.wait_ge(S["hnT_ps"], (b - 1) * SUB + j + 1)
                dve.scalar_tensor_tensor(out=r_sb[:, j, :], in0=bank[3][:, :], scalar=1 / WS, in1=gate_sb[:, :],
                                         op0=ALU.mult, op1=ALU.mult).then_inc(S["r_done"], 1)
                dve.wait_ge(S["r_done"], b * SUB + j + 1)
                dve.bn_stats(st[1][:, j, :], r_sb[:, j, :]).then_inc(S["bn_in_step"], 1)

            def ln_inner(b):
                for j in range(SUB):
                    wait_alone(dve, S["bn_in_step"], b * (2 * SUB) + SUB + j)
                    dve.bn_aggr(mv[1][:, j, :], st[1][:, j, :]).then_inc(S["bn_in_step"], 1)
                dve.wait_ge(S["bn_in_step"], (b + 1) * (2 * SUB))
                if not (isinstance(b, int) and b == 0):
                    dve.wait_ge(S["hn_done"], b * SUB)
                at = b * RSQRT_STEPS
                rsqrt(1, "lnin_step", at)
                dve.wait_ge(S["lnin_step"], at + RSQRT_STEPS)
                dve.nop().then_inc(S["lnin_ready"], 1)

            def inner_stats(b):
                dve.tensor_tensor(std[:, :], nw[1][:, 0, :], rstd[1][:, :], ALU.mult).then_inc(S["o_step"], 1)
                dve.tensor_scalar(m16[:, :], mv[1][:, :, 0], WS, None, ALU.mult).then_inc(S["o_step"], 1)

            def o_tile(b, j):
                if j == 0:
                    dve.wait_ge(S["o_step"], b * (2 + SUB) + 2)
                    if not (isinstance(b, int) and b == 0):
                        dve.wait_ge(S["x1_done"], b * SUB)
                dve.wait_ge(S["o_ps"], b * SUB + j + 1)
                dve.scalar_tensor_tensor(out=tmp[:, j, :], in0=colsum[:, :], scalar=m16[:, j:j + 1],
                                         in1=bank[5][:, D:2 * D], op0=ALU.mult, op1=ALU.add)\
                    .then_inc(S["o_step"], 1)
                dve.wait_ge(S["o_step"], b * (2 + SUB) + 3 + j)
                dve.scalar_tensor_tensor(out=tmp[:, j, :], in0=bank[5][:, 0:D], scalar=std[:, j:j + 1],
                                         in1=tmp[:, j, :], op0=ALU.mult, op1=ALU.add).then_inc(S["t_done"], 1)

            def ln2(b):
                for j in range(SUB):
                    dve.wait_ge(S["x1_done"], b * SUB + j + 1)
                    dve.bn_stats(st[2][:, j, :], x1[:, j, :]).then_inc(S["bn2_step"], 1)
                for j in range(SUB):
                    wait_alone(dve, S["bn2_step"], b * (2 * SUB) + SUB + j)
                    dve.bn_aggr(mv[2][:, j, :], st[2][:, j, :]).then_inc(S["bn2_step"], 1)
                dve.wait_ge(S["bn2_step"], (b + 1) * (2 * SUB))
                if not (isinstance(b, int) and b == 0):
                    dve.wait_ge(S["xn2_done"], b * SUB)
                at = b * RSQRT_STEPS
                rsqrt(2, "ln2_step", at)
                dve.wait_ge(S["ln2_step"], at + RSQRT_STEPS)
                dve.nop().then_inc(S["ln2_ready"], 1)

            MASK_STEPS = 14

            def top2(b):
                c = 0

                def do(ins):
                    nonlocal c
                    c += 1
                    ins.then_inc(S["mask_step"], 1)
                    dve.wait_ge(S["mask_step"], b * MASK_STEPS + c)

                def bc(a):
                    return a.unsqueeze(2).to_broadcast([P, SUB, NE])

                dve.wait_ge(S["lg_ps"], b + 1)
                do(dve.tensor_tensor(lg[:, :, :], bank[4][:, 0:SUB * NE].rearrange("p (j e) -> p j e", j=SUB),
                                     br4[:, :, :], ALU.add))
                src = lg
                for k in range(2):
                    v, mx = top[:, k, :], top[:, 2 + k, :]
                    do(dve.tensor_reduce(v, src[:, :, :], AX, ALU.max))
                    do(dve.tensor_tensor(eq[:, :, :], src[:, :, :], bc(v), ALU.is_equal))
                    do(dve.tensor_tensor(sc[:, :, :], eq[:, :, :], rev, ALU.mult))
                    do(dve.tensor_reduce(mx, sc[:, :, :], AX, ALU.max))
                    do(dve.tensor_tensor(onehot[:, k, :, :], sc[:, :, :], bc(mx), ALU.is_equal))
                    if k == 0:
                        do(dve.scalar_tensor_tensor(out=lg2[:, :, :], in0=onehot[:, 0, :, :], scalar=MASKED,
                                                    in1=lg[:, :, :], op0=ALU.mult, op1=ALU.add))
                        src = lg2
                if not (isinstance(b, int) and b == 0):
                    dve.wait_ge(S["payload"], b * 5)
                do(dve.tensor_tensor(dlt[:, :], top[:, 1, :], top[:, 0, :], ALU.subtract))
                do(dve.tensor_tensor(chosen[:, :, :], onehot[:, 0, :, :], onehot[:, 1, :, :], ALU.add))
                assert c == MASK_STEPS
                dve.nop().then_inc(S["mask_done"], 1)

            def slots(b):
                c = 0

                def do(ins):
                    nonlocal c
                    c += 1
                    ins.then_inc(S["slot_step"], 1)
                    dve.wait_ge(S["slot_step"], b * 5 + c)

                dve.wait_ge(S["rank_ps"], b + 1)
                R0 = SUB * NE
                do(dve.tensor_tensor(rank[:, :, :], bank[4][:, R0:2 * R0].rearrange("p (j e) -> p j e", j=SUB),
                                     base[:, :].unsqueeze(1).to_broadcast([P, SUB, NE]), ALU.add))
                do(dve.tensor_tensor(base[:, :], bank[4][:, 2 * R0:2 * R0 + NE], base[:, :], ALU.add))
                for k in range(2):
                    ins = dve.tensor_tensor(pick[:, k, :, :], onehot[:, k, :, :], rank[:, :, :], ALU.mult)
                do(ins)
                do(dve.tensor_reduce(slot_f[:, :, :], pick[:, :, :, :], AX, ALU.add))
                if not (isinstance(b, int) and b == 0):
                    dve.wait_ge(S["scattered"], b * (32 * SUB))
                do(dve.tensor_copy(slot_u[:, :, :], slot_f[:, :, :]))
                dve.nop().then_inc(S["slots_done"], 1)

            def body(i, front, mid, route, pre):
                if mid:
                    inner_stats(i - 1)
                if front:
                    h_lo(i, 0)
                    h_lo(i, 1)
                if mid:
                    hnT_lo(i - 1, 0)
                    hnT_lo(i - 1, 1)
                if front:
                    h_lo(i, 2)
                if mid:
                    hnT_lo(i - 1, 2)
                if front:
                    h_lo(i, 3)
                if mid:
                    hnT_lo(i - 1, 3)
                if front:
                    r_tile(i, 0)
                if pre:
                    ln1(i + 1)
                if front:
                    r_tile(i, 1)
                if mid:
                    o_tile(i - 1, 0)
                if route:
                    top2(i - 2)
                if front:
                    r_tile(i, 2)
                if mid:
                    o_tile(i - 1, 1)
                if route:
                    slots(i - 2)
                if front:
                    r_tile(i, 3)
                if mid:
                    o_tile(i - 1, 2)
                if front:
                    ln_inner(i)
                if mid:
                    o_tile(i - 1, 3)
                    ln2(i - 1)

            dve.memset(conv_f, 0.0).then_inc(S["zeroed"], 1)
            dve.memset(hT[:, :, :, 0:PAD], 0.0)
            dve.memset(ones_f[:, :], 1.0)
            dve.memset(ones16[:, :], 1.0)
            dve.memset(bias_rows[:, :], 0.0).then_inc(S["zeroed"], 1)
            ln1(0)
            dve.wait_ge(S["cols_loaded"], 80)
            dve.wait_ge(S["zeroed"], 2)
            dve.tensor_scalar(g16[:, :], cols[:, 0:KI], WS, None, ALU.mult).then_inc(S["g16_ready"], 1)
            for k in range(KI):
                ins = dve.tensor_scalar(cpb_rep[:, k * 64:(k + 1) * 64], ones_f[:, 0:64],
                                        cols[:, 2 * KI + k:2 * KI + k + 1], None, ALU.mult)
            ins.then_inc(S["cpb_ready"], 1)
            dve.wait_ge(S["modT_ps"], 1)
            modT = bank[4][:, 0:4 * NB].rearrange("p (s k b) -> p s k b", s=2, k=KD)
            dve.tensor_copy(shiftT[:, :, :], modT[:, 0]).then_inc(S["modT_read"], 1)
            dve.tensor_scalar(scaleT[:, :, :], modT[:, 1], 1.0, None, ALU.add).then_inc(S["modT_read"], 1)
            split_lo(in_w[:, 1, :], in_f, in_w[:, 0, :], 1)
            dve.nop()
            dve.drain().then_inc(S["w_lo"], 1)
            split_lo(conv_w[:, 1, :], conv_f, conv_w[:, 0, :], 2)
            split_lo(bias_lo[:, 0:INNER], convb_f[0:64, :], bias_hi[:, 0:INNER], 3)
            dve.drain().then_inc(S["w_lo"], 1)
            dve.wait_ge(S["w_lo"], 2)
            dve.tensor_copy(bias_rows[0:1, 0:INNER], bias_hi[0:1, 0:INNER])
            dve.tensor_copy(bias_rows[32:33, 0:INNER], bias_lo[32:33, 0:INNER]).then_inc(S["w_lo"], 1)

            dve.wait_ge(S["modrow_ps"], 1)
            c = 0

            def do(ins):
                nonlocal c
                c += 1
                ins.then_inc(S["modrow_step"], 1)
                dve.wait_ge(S["modrow_step"], c)

            do(dve.tensor_copy(mtmp[:, 0, :], bank[5][0:NB, 0:D]))
            do(dve.tensor_copy(modrow[:, 2, :], bank[5][0:NB, D:2 * D]))
            do(dve.tensor_scalar(modrow[:, 1, :], bank[3][0:NB, 0:D], 1.0, None, ALU.add))
            do(dve.tensor_copy(mtmp[:, 1, :], bank[3][0:NB, D:2 * D]))
            gates = mtmp[:, 0:2, :]
            work = mtmp[:, 2:4, :]
            do(dve.scalar_tensor_tensor(out=work, in0=gates, scalar=-1.0, in1=gates, op0=ALU.mult, op1=ALU.max))
            do(dve.tensor_scalar(work, work, GATE_MIN, None, ALU.max))
            do(dve.tensor_scalar(gates, gates, 0.0, 2.0, ALU.is_ge, ALU.mult))
            do(dve.scalar_tensor_tensor(out=gates, in0=gates, scalar=-1.0, in1=work, op0=ALU.add, op1=ALU.mult))
            do(dve.tensor_scalar(modrow[:, 0, :], mtmp[:, 0, :], 1 / WS, None, ALU.mult))
            dve.wait_ge(S["rows_loaded"], 48)
            do(dve.tensor_tensor(modrow[:, 4, :], mtmp[:, 1, :], gb_row[:, 0, :], ALU.mult))
            do(dve.tensor_tensor(modrow[:, 3, :], mtmp[:, 1, :], gb_row[:, 1, :], ALU.mult))
            dve.nop().then_inc(S["modrow_done"], 1)

            for k in range(KI):
                split_lo(fc_w[:, 1, k * D:(k + 1) * D], fc_f[:, k * D:(k + 1) * D],
                         fc_w[:, 0, k * D:(k + 1) * D], 4, g16[:, k:k + 1])
            dve.wait_ge(S["fb_ps"], 1)
            dve.tensor_tensor(fc_bias[:, :], bank[2][:, 0:KD], cols[:, 3 * KI:3 * KI + KD], ALU.add)
            dve.drain().then_inc(S["w_lo"], 1)
            split_lo(out_w[:, 1, :], out_f, out_w[:, 0, :], 5)
            split_lo(comp_w[:, 1, :], bank[1][:, :], comp_w[:, 0, :], 6)
            split_lo(bias_lo[:, INNER:], bank[0][0:64, D:2 * D], bias_hi[:, INNER:], 7)
            dve.tensor_copy(colsum[:, :], bank[0][:, 0:D])
            dve.drain().then_inc(S["w_lo"], 1)
            dve.wait_ge(S["w_lo"], 5)
            dve.tensor_copy(bias_rows[0:1, INNER:], bias_hi[0:1, INNER:])
            dve.tensor_copy(bias_rows[32:33, INNER:], bias_lo[32:33, INNER:]).then_inc(S["w_lo"], 1)
            dve.wait_ge(S["base_ready"], 1)
            dve.wait_ge(S["router_loaded"], 16 * (1 + SUB))

            run(dve, body)

            c2 = 0

            def do2(ins):
                nonlocal c2
                c2 += 1
                ins.then_inc(S["table_step"], 1)
                dve.wait_ge(S["table_step"], c2)

            do2(dve.tensor_copy(tab_end[:, :], base[:, :]))
            do2(dve.tensor_tensor(cnt[:, :], base[:, :], region0, ALU.subtract))
            do2(dve.tensor_scalar(cnt[:, :], cnt[:, :], float(T - 1), None, ALU.add))
            do2(dve.tensor_copy(cnt_i[:, :], cnt[:, :]))
            do2(dve.tensor_scalar(cnt_s[:, :], cnt_i[:, :], T.bit_length() - 1, None, ALU.logical_shift_right))
            do2(dve.tensor_copy(nt[:, :], cnt_s[:, :]))
            do2(dve.tensor_scalar(nt[:, :], nt[:, :], 1.0, None, ALU.max))
            do2(dve.memset(g0[:, 0:1], 0.0))
            for e in range(NE):
                do2(dve.tensor_tensor(g0[:, e + 1:e + 2], g0[:, e:e + 1], nt[:, e:e + 1], ALU.add))
            do2(dve.tensor_scalar(step[:, :], nt[:, :], -float(T), float(REGION), ALU.mult, ALU.add))
            do2(dve.tensor_scalar(row_f[:, :], tile_no, float(T), None, ALU.mult))
            for e in range(1, NE):
                do2(dve.tensor_scalar(row_t[:, :], tile_no, g0[:, e:e + 1], step[:, e - 1:e],
                                      ALU.is_ge, ALU.mult))
                do2(dve.tensor_tensor(row_f[:, :], row_f[:, :], row_t[:, :], ALU.add))
            do2(dve.tensor_scalar(row_t[:, :], tile_no, g0[:, NE:NE + 1], None, ALU.is_lt))
            do2(dve.tensor_tensor(row_f[:, :], row_f[:, :], row_t[:, :], ALU.mult))
            do2(dve.tensor_copy(tab_row[:, :], row_f[:, :]))
            do2(dve.tensor_copy(tab_nt[:, :], nt[:, :]))
            do2(dve.tensor_copy(tab_g0[:, :], g0[:, :]))
            dve.nop().then_inc(S["tables_ready"], 1)

            def w_split(n, buf):
                dve.wait_ge(S["w_conv"], n)
                dve.scalar_tensor_tensor(out=split_w[:, buf, 1, :], in0=stage_w, scalar=WS,
                                         in1=split_w[:, buf, 0, :], op0=ALU.mult, op1=ALU.subtract)\
                    .then_inc(S["w_ready"], 1)

            def xmT_lo(g):
                dve.wait_ge(S["xmT_hi"], g + 1)
                dve.tensor_copy(meta[:, :, :], xm[:, :, D:D + 3]).then_inc(S["meta_done"], 1)
                dve.tensor_tensor(xmT[:, 1, :, :].rearrange("p k t -> p (k t)"), bank[6][:, :],
                                  xmT[:, 0, :, :].rearrange("p k t -> p (k t)"), ALU.subtract)\
                    .then_inc(S["xmT_lo"], 1)
                dve.wait_ge(S["meta_done"], g + 1)
                dve.nop().then_inc(S["x_taken"], 1)

            dve.nop().then_inc(S["hm_lo"], 1)
            dve.nop().then_inc(S["y_done"], 1)
            w_split(1, 0)
            xmT_lo(0)

            def expert(e, buf, has_next, has_after):
                first = dve.value_load(tab_g0[0:1, e:e + 1] if isinstance(e, int) else tab_g0[0:1, bass.ds(e, 1)],
                                       min_val=0, max_val=MAXT - 2)
                n = dve.value_load(tab_nt[0:1, e:e + 1] if isinstance(e, int) else tab_nt[0:1, bass.ds(e, 1)],
                                   min_val=1, max_val=MAXT - 2)
                if has_next:
                    w_split(e + 2, 1 - buf)
                b2e = (b2r[:, e:e + 1, :] if isinstance(e, int) else b2r[:, bass.ds(e, 1), :])\
                    .rearrange("p a d -> p (a d)")
                with dve.Fori(0, n) as t:
                    g = dve.snap(first + t)
                    for q in range(KF // 2):
                        dve.wait_ge(S["hf_done"], g * KF + 2 * q + 3)
                        pair = hf[:, 2 * q:2 * q + 2, :]
                        dve.tensor_copy(hm[:, 0, 2 * q:2 * q + 2, :], pair).then_inc(S["hm_hi"], 1)
                        dve.wait_ge(S["hm_hi"], g * (KF // 2) + q + 1)
                        dve.tensor_tensor(hm[:, 1, 2 * q:2 * q + 2, :], pair, hm[:, 0, 2 * q:2 * q + 2, :],
                                          ALU.subtract).then_inc(S["hm_lo"], 1)
                    dve.wait_ge(S["exp_done"], g + 1)
                    dve.wait_ge(S["rows_added"], g + 1)
                    dve.tensor_scalar(wt[:, 0, :], ew[:, :, 1], 1.0, None, ALU.add).then_inc(S["wcur_step"], 1)
                    dve.tensor_copy(idcur[:, :], meta[:, :, 0]).then_inc(S["wcur_step"], 1)
                    dve.wait_ge(S["wcur_step"], g * 3 + 2)
                    dve.reciprocal(wt[:, 1, :], wt[:, 0, :]).then_inc(S["wcur_step"], 1)
                    dve.wait_ge(S["wcur_step"], g * 3 + 3)
                    dve.tensor_tensor(wcur[:, :], wt[:, 1, :], ew[:, :, 0], ALU.mult).then_inc(S["wcur_done"], 1)
                    xmT_lo(g + 1)
                    dve.wait_ge(S["yw_done"], g * TS + 1)
                    dve.wait_ge(S["y_ps"], g + 2)
                    for j in range(TS):
                        dve.scalar_tensor_tensor(out=y_f[:, j, :], in0=bank[4 + j][:, 0:D], scalar=1 / WS,
                                                 in1=b2e, op0=ALU.mult, op1=ALU.add).then_inc(S["y_done"], 1)

            dve.wait_ge(S["b2_loaded"], 16)
            expert_pairs(dve, expert)

            for b in range(NB):
                q = b % 2
                dve.wait_ge(FIN_LOADED[q], 48 * (b // 2 + 1))
                if b >= 1:
                    dve.wait_ge(S["fin_norm"], b)
                c = b * (3 * SUB)
                for j in range(SUB):
                    dve.bn_stats(st[q][:, j, :], fin_v[q][:, j, :]).then_inc(S["fin_step"], 1)
                for j in range(SUB):
                    dve.wait_ge(S["fin_step"], b * (2 * SUB + 2) + j + 1)
                    dve.bn_aggr(mv[q][:, j, :], st[q][:, j, :]).then_inc(S["fin_step"], 1)
                dve.wait_ge(S["fin_step"], b * (2 * SUB + 2) + 2 * SUB)
                dve.tensor_scalar(mv[q][:, :, 1], mv[q][:, :, 1], EPS, None, ALU.add).then_inc(S["fin_var"], 1)
                dve.wait_ge(S["fin_sqrt"], b + 1)
                dve.reciprocal(nw[q][:, 0, :], rstd[1][:, :]).then_inc(S["fin_step"], 1)
                dve.wait_ge(S["fin_step"], b * (2 * SUB + 2) + 2 * SUB + 1)
                dve.scalar_tensor_tensor(out=nbias[q][:, :], in0=mv[q][:, :, 0], scalar=-1.0,
                                         in1=nw[q][:, 0, :], op0=ALU.mult, op1=ALU.mult)\
                    .then_inc(S["fin_step"], 1)
                dve.wait_ge(S["fin_step"], b * (2 * SUB + 2) + 2 * SUB + 2)
                dve.nop().then_inc(S["fin_ready"], 1)
                dve.wait_ge(S["fin_norm"], b + 1)
                z = fin_z[q]
                dve.tensor_tensor(z, z, fin_g[q].unsqueeze(1).to_broadcast([P, SUB, D]), ALU.mult)\
                    .then_inc(S["fin_mul"], 1)
                dve.wait_ge(S["fin_mul"], b + 1)
                if b >= 2:
                    dve.wait_ge(S["fin_stored"], 16 * (b - 1))
                dve.tensor_tensor(fin_o[q], z, fin_x[q], ALU.add).then_inc(S["fin_sum"], 1)

        @block.tensor
        def _(pe):
            def win(hl, k, lo, n):
                return in_w[:, hl, k * 2 * INNER + lo:k * 2 * INNER + lo + n]

            def turn_x(b):
                for k in range(KD):
                    if not (isinstance(b, int) and b == 0):
                        if isinstance(b, int) and b <= 1:
                            pe.wait_ge(S["xT_f32"], KD * b)
                        elif isinstance(b, int) and b == 2:
                            pe.wait_ge(S["hnT_lo"], SUB)
                        else:
                            pe.wait_ge(S["h2T_done"], (b - 3) * KD + k + 1)
                    if k == 0:
                        pe.wait_ge(S["xn_done"], b + 1)
                    for j in range(SUB):
                        mm = pe.transpose(bank[6 + k][:, j * P:(j + 1) * P], xn[:, j, k * P:(k + 1) * P],
                                          ident[:, :])
                    mm.then_inc(S["xT_ps"], 1)

            def proj_h(b, m):
                if m == 0:
                    pe.wait_ge(S["xT_lo"], (b + 1) * KD)
                if m < 2:
                    if isinstance(b, int) and b == 1:
                        pe.wait_ge(S["h_lo"], KI)
                    elif not (isinstance(b, int) and b == 0):
                        pe.wait_ge(S["s_f32"], (b - 2) * KD + m + 1)
                else:
                    pe.wait_ge(S["h_lo"], b * KI + m - 1)
                for k in range(KD):
                    mm = three(pe, bank[m % 2][:, :], (win(0, k, m * P, P), win(1, k, m * P, P)),
                               (xT[:, 0, k, :], xT[:, 1, k, :]), k == 0, k == KD - 1)
                mm.then_inc(S["h_ps"], 1)

            def proj_gate(b, j):
                if not (isinstance(b, int) and b * SUB + j == 0):
                    pe.wait_ge(S["gate_done"], b * SUB + j)
                t = slice(j * P, (j + 1) * P)
                for k in range(KD):
                    mm = three(pe, bank[2][:, :], (xT[:, 0, k, t], xT[:, 1, k, t]),
                               (win(0, k, INNER, INNER), win(1, k, INNER, INNER)), k == 0, k == KD - 1)
                mm.then_inc(S["gate_ps"], 1)

            def conv(b, j):
                if not (isinstance(b, int) and b * SUB + j == 0):
                    pe.wait_ge(S["r_done"], b * SUB + j)
                pe.matmul(bank[3][:, :], ones16[0:BIAS_K, :], bias_rows[0:BIAS_K, 0:INNER],
                          start=True, stop=False)
                for c in range(KI):
                    if j == 0:
                        pe.wait_ge(S["h_lo"], b * KI + c + 1)
                    for t in range(TAPS):
                        w = (c * TAPS + t) * P
                        tt = slice(j * P + t, j * P + t + P)
                        mm = three(pe, bank[3][:, c * P:(c + 1) * P], (hT[:, 0, c, tt], hT[:, 1, c, tt]),
                                   (conv_w[:, 0, w:w + P], conv_w[:, 1, w:w + P]), False,
                                   c == KI - 1 and t == TAPS - 1)
                mm.then_inc(S["conv_ps"], 1)

            def turn_hn(b, j, front):
                if j < 2:
                    if isinstance(b, int) and b == NB - 1:
                        pe.wait_ge(S["h2T_done"], (b - 1) * KD)
                    else:
                        pe.wait_ge(S["xT_f32"], (b + 1) * KD + j + 1)
                else:
                    pe.wait_ge(S["hnT_lo"], b * SUB + j - 1)
                pe.wait_ge(S["hn_done"], b * SUB + j + 1)
                for k in range(KI):
                    mm = pe.transpose(bank[6 + j % 2][:, k * P:(k + 1) * P], r_sb[:, j, k * P:(k + 1) * P],
                                      ident[:, :])
                mm.then_inc(S["hnT_ps"], 1)

            def fc(b, m, front):
                if m == 0:
                    pe.wait_ge(S["hnT_lo"], (b + 1) * SUB)
                if front:
                    pe.wait_ge(S["h_lo"], (b + 1) * KI + 3 + m)
                for k in range(KI):
                    w = k * D + m * P
                    mm = three(pe, bank[m][:, :], (fc_w[:, 0, w:w + P], fc_w[:, 1, w:w + P]),
                               (hnT[:, 0, k, :], hnT[:, 1, k, :]), k == 0, k == KI - 1)
                mm.then_inc(S["u_ps"], 1)

            def out_proj(b, j):
                if not (isinstance(b, int) and b * SUB + j == 0):
                    pe.wait_ge(S["t_done"], b * SUB + j)
                if j == 0:
                    pe.wait_ge(S["s_lo"], (b + 1) * KD)
                t = slice(j * P, (j + 1) * P)
                for k in range(KI):
                    three(pe, bank[5][:, 0:D], (hnT[:, 0, k, t], hnT[:, 1, k, t]),
                          (out_w[:, 0, k * D:(k + 1) * D], out_w[:, 1, k * D:(k + 1) * D]), k == 0, k == KI - 1)
                pe.matmul(bank[5][:, D:2 * D], ones16[0:BIAS_K, :], bias_rows[0:BIAS_K, INNER:],
                          start=True, stop=False)
                for k in range(KD):
                    mm = three(pe, bank[5][:, D:2 * D], (sT[:, 0, k, t], sT[:, 1, k, t]),
                               (comp_w[:, 0, k * D:(k + 1) * D], comp_w[:, 1, k * D:(k + 1) * D]),
                               False, k == KD - 1)
                mm.then_inc(S["o_ps"], 1)

            def turn_h2(b, mid):
                pe.wait_ge(S["row_done"], (b + 1) * SUB)
                for k in range(KD):
                    if mid:
                        pe.wait_ge(S["hnT_lo"], (b + 1) * SUB + 3 + k)
                    else:
                        pe.wait_ge(S["h2T_done"], b * KD)
                    for j in range(SUB):
                        mm = pe.transpose(bank[6 + k][:, j * P:(j + 1) * P], h2x[:, j, k * P:(k + 1) * P],
                                          ident[:, :])
                    mm.then_inc(S["h2T_ps"], 1)

            def logits(b):
                pe.wait_ge(S["h2T_done"], (b + 1) * KD)
                if not (isinstance(b, int) and b == 0):
                    pe.wait_ge(S["slots_done"], b)
                for j in range(SUB):
                    for k in range(KD):
                        mm = pe.matmul(bank[4][:, j * NE:(j + 1) * NE], h2T[:, k, j * P:(j + 1) * P],
                                       router_w[:, k, :], start=(k == 0), stop=(k == KD - 1))
                mm.then_inc(S["lg_ps"], 1)

            def ranks(b):
                pe.wait_ge(S["mask_done"], b + 1)
                R0 = SUB * NE
                pe.matmul(bank[4][:, R0:2 * R0], before[:, :], chosen[:, :, :].rearrange("p j e -> p (j e)"),
                          start=True, stop=False)
                for j in range(SUB - 1):
                    pe.matmul(bank[4][:, R0 + (j + 1) * NE:2 * R0], ones16[:, :],
                              chosen[:, j:j + 1, :].to_broadcast([P, SUB - 1 - j, NE]),
                              start=False, stop=(j == SUB - 2))
                for j in range(SUB):
                    mm = pe.matmul(bank[4][:, 2 * R0:2 * R0 + NE], ones16[:, :], chosen[:, j, :],
                                   start=(j == 0), stop=(j == SUB - 1))
                mm.then_inc(S["rank_ps"], 1)

            def body(i, front, mid, route, pre):
                if front:
                    proj_h(i, 0)
                    proj_h(i, 1)
                    proj_gate(i, 0)
                if mid:
                    turn_hn(i - 1, 0, front)
                    turn_hn(i - 1, 1, front)
                if front:
                    proj_h(i, 2)
                if mid:
                    turn_hn(i - 1, 2, front)
                if front:
                    proj_h(i, 3)
                if mid:
                    turn_hn(i - 1, 3, front)
                if front:
                    if isinstance(i, int) and i == 0:
                        pe.wait_ge(S["w_lo"], 3)
                    conv(i, 0)
                if mid:
                    if isinstance(i, int) and i == 1:
                        pe.wait_ge(S["w_lo"], 6)
                    fc(i - 1, 0, front)
                    fc(i - 1, 1, front)
                if route:
                    turn_h2(i - 2, mid)
                if front:
                    proj_gate(i, 1)
                    conv(i, 1)
                if mid:
                    out_proj(i - 1, 0)
                if route:
                    logits(i - 2)
                if front:
                    proj_gate(i, 2)
                    conv(i, 2)
                if mid:
                    out_proj(i - 1, 1)
                if route:
                    ranks(i - 2)
                if front:
                    proj_gate(i, 3)
                    conv(i, 3)
                if mid:
                    out_proj(i - 1, 2)
                if pre:
                    turn_x(i + 1)
                if mid:
                    out_proj(i - 1, 3)

            pe.wait_ge(S["silu_c_done"], 1)
            pe.wait_ge(S["ident_ready"], 4)
            for s in range(2):
                for m in range(KD):
                    o = (s * KD + m) * NB
                    for k in range(KD):
                        w = k * 6 * D + s * D + m * P
                        mm = pe.matmul(bank[4][:, o:o + NB], wmod_f[:, w:w + P], silu_c[:, k * NB:(k + 1) * NB],
                                       start=(k == 0), stop=(k == KD - 1))
            mm.then_inc(S["modT_ps"], 1)
            for r, bk in ((0, 5), (1, 3)):
                for k in range(KD):
                    w = k * 6 * D + (2 + 2 * r) * D
                    mm = pe.matmul(bank[bk][0:NB, 0:2 * D], silu_c[:, k * NB:(k + 1) * NB], wmod_f[:, w:w + 2 * D],
                                   start=(k == 0), stop=(k == KD - 1))
            mm.then_inc(S["modrow_ps"], 1)
            turn_x(0)
            pe.wait_ge(S["out_loaded"], 16)
            pe.wait_ge(S["cpb_ready"], 1)
            for k in range(KI):
                pe.matmul(bank[0][:, 0:D], ones_f[:, :], out_f[:, k * D:(k + 1) * D], start=(k == 0), stop=(k == KI - 1))
            for k in range(KI):
                mm = pe.matmul(bank[0][0:64, D:2 * D], cpb_rep[:, k * 64:(k + 1) * 64], out_f[:, k * D:(k + 1) * D],
                               start=(k == 0), stop=(k == KI - 1))
            mm.then_inc(S["colsum_ps"], 1)
            pe.wait_ge(S["cproj_loaded"], 16)
            for m in range(KD):
                for k in range(KI):
                    w = k * D + m * P
                    mm = pe.matmul(bank[1][:, m * D:(m + 1) * D], cproj_f[:, w:w + P], out_f[:, k * D:(k + 1) * D],
                                   start=(k == 0), stop=(k == KI - 1))
            mm.then_inc(S["comp_ps"], 1)
            pe.wait_ge(S["fc_loaded"], 16)
            for m in range(KD):
                for k in range(KI):
                    w = k * D + m * P
                    mm = pe.matmul(bank[2][:, m:m + 1], fc_f[:, w:w + P], cols[:, KI + k:KI + k + 1],
                                   start=(k == 0), stop=(k == KI - 1))
            mm.then_inc(S["fb_ps"], 1)
            pe.wait_ge(S["w_lo"], 6)
            pe.wait_ge(S["modrow_done"], 1)
            run(pe, body)

            def turn_m(g):
                pe.wait_ge(S["xm_loaded"], (g + 1) * 16)
                for j in range(TS):
                    for k in range(KD):
                        o = k * T + j * P
                        mm = pe.transpose(bank[6][:, o:o + P], xm[:, j, k * P:(k + 1) * P], ident[:, :])
                mm.then_inc(S["xmT_ps"], 1)

            pe.nop().then_inc(S["y_ps"], 1)
            pe.wait_ge(S["tables_ready"], 1)
            turn_m(0)

            def expert(e, buf, has_next, has_after):
                first = pe.value_load(tab_g0[0:1, e:e + 1] if isinstance(e, int) else tab_g0[0:1, bass.ds(e, 1)],
                                      min_val=0, max_val=MAXT - 2)
                n = pe.value_load(tab_nt[0:1, e:e + 1] if isinstance(e, int) else tab_nt[0:1, bass.ds(e, 1)],
                                  min_val=1, max_val=MAXT - 2)
                wait_alone(pe, S["w_ready"], e + 1)

                def w1(hl, k, c):
                    o = k * FF + c * P
                    return split_w[:, buf, hl, o:o + P]

                def w2(hl, c):
                    o = KD * FF + c * D
                    return split_w[:, buf, hl, o:o + D]

                with pe.Fori(0, n) as t:
                    g = pe.snap(first + t)
                    pe.wait_ge(S["xmT_lo"], g + 1)
                    for c in range(KF):
                        if c == 0:
                            pe.wait_ge(S["hf_done"], g * KF + 1)
                        for k in range(KD):
                            mm = three(pe, bank[c // 2][:, (c % 2) * T:(c % 2 + 1) * T],
                                       (w1(0, k, c), w1(1, k, c)), (xmT[:, 0, k, :], xmT[:, 1, k, :]),
                                       k == 0, k == KD - 1)
                        if c % 2 == 1:
                            mm.then_inc(S["l1_ps"], 1)
                    turn_m(g + 1)
                    pe.wait_ge(S["y_done"], g * TS + 1)
                    for c in range(KF):
                        pe.wait_ge(S["hm_lo"], g * (KF // 2) + c // 2 + 2)
                        for j in range(TS):
                            mm = three(pe, bank[4 + j][:, 0:D],
                                       (hm[:, 0, c, j * P:(j + 1) * P], hm[:, 1, c, j * P:(j + 1) * P]),
                                       (w2(0, c), w2(1, c)), c == 0, c == KF - 1)
                    mm.then_inc(S["y_ps"], 1)

            expert_pairs(pe, expert)


_LAYOUT = {
    "x": lambda d: d["L0_attn_hidden_states"],
    "in_wT": lambda d: d["L0_attn_in_proj_w"].T,
    "convT": lambda d: d["L0_attn_conv_w"].reshape(4, 2, 64, 64, 4).transpose(0, 1, 3, 4, 2),
    "conv_b": lambda d: d["L0_attn_conv_b"],
    "ln_g": lambda d: d["L0_attn_ln_g"].reshape(-1, 128).T,
    "ln_b": lambda d: d["L0_attn_ln_b"].reshape(-1, 128).T,
    "fcT": lambda d: d["L0_attn_fc_w"].T,
    "fc_b": lambda d: d["L0_attn_fc_b"].reshape(-1, 128).T,
    "cproj": lambda d: d["L0_attn_cproj_w"],
    "cproj_b": lambda d: d["L0_attn_cproj_b"].reshape(-1, 128).T,
    "outT": lambda d: d["L0_attn_out_w"].T,
    "WrT": lambda d: d["L0_ffn_Wr"].T,
    "br": lambda d: d["L0_ffn_br"],
    "W1T": lambda d: d["L0_ffn_W1"].transpose(0, 2, 1),
    "b1": lambda d: d["L0_ffn_b1"].reshape(-1, 128).T,
    "W2T": lambda d: d["L0_ffn_W2"].transpose(0, 2, 1),
    "b2": lambda d: d["L0_ffn_b2"].reshape(-1),
    "gamma": lambda d: d["L0_ffn_gamma"],
    "beta": lambda d: d["L0_ffn_beta"],
    "cT": lambda d: d["L0_c"].T.reshape(2, 128, 8).transpose(1, 0, 2).reshape(128, 16),
    "wmod": lambda d: d["L0_wmod"],
}


def kernel(**inputs):
    import numpy as np
    import concourse.bacc as bacc
    from concourse.bass_utils import run_bass_kernel_spmd

    nc = bacc.Bacc("TRN2", target_bir_lowering=False, num_devices=1)
    arrays, args = {}, {}
    for name, lay in _LAYOUT.items():
        a = np.ascontiguousarray(lay({k: np.asarray(v) for k, v in inputs.items()}))
        arrays[f"in_{name}"] = a
        args[name] = nc.dram_tensor(f"in_{name}", a.shape, F32, kind="ExternalInput").ap()
    shape = tuple(inputs["L0_attn_hidden_states"].shape)
    args["out"] = nc.dram_tensor("out_x", shape, F32, kind="ExternalOutput").ap()
    adaln_kernel(nc, **args)
    r = run_bass_kernel_spmd(nc, [arrays], core_ids=[0])
    return r.results[0]["out_x"]
```

```python
from contextlib import ExitStack

import concourse.bass as bass
from concourse import mybir

F32 = mybir.dt.float32
F16 = mybir.dt.float16
I32 = mybir.dt.int32
U32 = mybir.dt.uint32
ALU = mybir.AluOpType
ACT = mybir.ActivationFunctionType
AX = mybir.AxisListType.X

P = 128
EPS = 1e-5
WS = 16.0
GATE_MIN = 0.25
RSQRT_MAGIC = float(0x5F3759DF)
NEWTON = 3
MASKED = -3.0e38


def adaln_kernel(nc, x, in_wT, convT, conv_b, ln_g, ln_b, fcT, fc_b, cproj, cproj_b, outT,
                 WrT, br, W1T, b1, W2T, b2, gamma, beta, cT, wmod, out):
    NB, SEQ, D = x.shape
    INNER = outT.shape[0]
    NE, _, FF = W1T.shape
    TAPS = convT.shape[3]
    G = convT.shape[2]
    KD, KI, KF, SUB = D // P, INNER // P, FF // P, SEQ // P
    PAD = TAPS - 1
    TOKENS = NB * SEQ
    T = 256
    TS = T // P
    REGION = TOKENS + T
    MAXT = 48
    ROWS = 2 * MAXT
    assert 2 * TOKENS // T + NE <= MAXT and KF * T * 4 == 4 * 2048
    C_ID, C_W, RW = D, D + 1, D + 8
    WE = KD * FF + KF * D
    WQ = 4
    BIAS_K = 33

    gathered = nc.dram_tensor("expert_lists", (NE * REGION, RW), F32, kind="Internal").ap()
    moe_acc = nc.dram_tensor("moe_sum", (TOKENS + T, D), F32, kind="Internal").ap()
    resid = nc.dram_tensor("residual_rows", (TOKENS, D), F32, kind="Internal").ap()
    modd = nc.dram_tensor("modulation_rows", (NB, 5, D), F32, kind="Internal").ap()

    with ExitStack() as ctx:
        def sb(name, shape, dt=F32):
            return ctx.enter_context(nc.sbuf_tensor(name, shape, dt))

        def sem(name):
            return ctx.enter_context(nc.semaphore(name))

        bank = [ctx.enter_context(nc.psum_tensor(f"bank{i}", [P, 512], F32)) for i in range(8)]

        pool_f = sb("weight_pool", [P, WE + 2 * WE])
        at = 0

        def part(n):
            nonlocal at
            at += n
            return pool_f[:, at - n:at]

        in_f = part(KD * 2 * INNER)
        conv_f = part(KI * TAPS * P)
        fc_f = part(KI * D)
        out_f = part(KI * D)
        cproj_f = part(KI * D)
        wmod_f = part(KD * 6 * D)
        convb_f = part(INNER)
        cpb_rep = part(KI * 64)
        assert at <= 3 * WE
        stage_w = pool_f[:, 0:WE]
        split_w = pool_f[:, WE:3 * WE].bitcast(F16).rearrange("p (b h n) -> p b h n", b=2, h=2)

        in_w = sb("in_w", [P, 2, KD * 2 * INNER], F16)
        conv_w = sb("conv_w", [P, 2, KI * TAPS * P], F16)
        fc_w = sb("fc_w", [P, 2, KI * D], F16)
        out_w = sb("out_w", [P, 2, KI * D], F16)
        comp_w = sb("comp_w", [P, 2, KD * D], F16)
        bias_rows = sb("bias_rows", [64, INNER + D], F16)
        bias_hi = sb("bias_hi", [64, INNER + D], F16)
        bias_lo = sb("bias_lo", [64, INNER + D], F16)
        router_w = sb("router_w", [P, KD, NE])
        cols = sb("cols", [P, 3 * KI + KD])
        g16 = sb("g16", [P, KI])
        fc_bias = sb("fc_bias", [P, KD])
        b1c = sb("b1c", [P, NE * KF])
        b2r = sb("b2r", [P, NE, D])
        br4 = sb("br4", [P, SUB, NE])
        silu_c = sb("silu_c", [P, KD * NB])
        c_sb = sb("c_sb", [P, KD * NB])
        shiftT = sb("shiftT", [P, KD, NB])
        scaleT = sb("scaleT", [P, KD, NB])
        modrow = sb("modrow", [NB, 5, D])
        mtmp = sb("mtmp", [NB, 4, D])
        gb_row = sb("gamma_beta", [NB, 2, D])
        colsum = sb("colsum", [P, D])

        ident = sb("ident", [P, P])
        ones_f = sb("ones_f", [P, P])
        ones16 = sb("ones16", [P, P], F16)
        before = sb("before", [P, P], F16)
        iota_i = sb("iota_i", [P, SUB * NE + NE + SUB + ROWS + TS], I32)
        iota_f = sb("iota_f", [P, SUB * NE + NE + SUB + ROWS + TS])
        rev = iota_f[:, 0:SUB * NE].rearrange("p (j e) -> p j e", j=SUB)
        region0 = iota_f[:, SUB * NE:SUB * NE + NE]
        token0 = iota_f[:, SUB * NE + NE:SUB * NE + NE + SUB]
        tile_no = iota_f[:, SUB * NE + NE + SUB:SUB * NE + NE + SUB + ROWS]
        fill_id = iota_f[:, SUB * NE + NE + SUB + ROWS:]
        filler = sb("filler", [P, TS, RW])

        xa = sb("xa", [P, SUB, D])
        xr = sb("xr", [P, SUB, D])
        xn = sb("xn", [P, SUB, D])
        xT_f = sb("xT_f", [P, KD, SEQ])
        xT = sb("xT", [P, 2, KD, SEQ], F16)
        hT_all = sb("hT", [P, 2 * KI * (PAD + SEQ)], F16)
        hT = hT_all[:, :].rearrange("p (h k n) -> p h k n", h=2, k=KI)
        gate_sb = sb("gate_sb", [P, INNER])
        r_sb = sb("r_sb", [P, SUB, INNER])
        hnT = sb("hnT", [P, 2, KI, SEQ], F16)
        s_f = sb("s_f", [P, KD, SEQ])
        sT = sb("sT", [P, 2, KD, SEQ], F16)
        tmp = sb("tmp", [P, SUB, D])
        x1 = sb("x1", [P, SUB, D])
        xn2 = sb("xn2", [P, SUB, D])
        x1p = sb("x1p", [P, SUB, D])
        h2x = sb("h2x", [P, SUB, RW])
        h2T = sb("h2T", [P, KD, SEQ])
        ga_row = sb("ga_row", [P, D])
        rt_row = sb("rt_row", [P, 3, D])
        st_in = sb("bn_inner", [P, SUB, 6])
        mv_in = sb("mv_inner", [P, SUB, 2])
        nw_in = sb("newton_inner", [P, 4, SUB])
        rstd_in = sb("rstd_inner", [P, SUB])
        nbias_in = sb("nbias_inner", [P, SUB])
        st_12 = sb("bn_12", [P, 2, SUB, 6])
        mv_12 = sb("mv_12", [P, 2 * SUB, 2])
        nw_12 = sb("newton_12", [P, 4, 2 * SUB])
        rstd_12 = sb("rstd_12", [P, 2 * SUB])
        nbias_12 = sb("nbias_12", [P, 2 * SUB])
        std = sb("std", [P, SUB])
        m16 = sb("m16", [P, SUB])
        lg = sb("lg", [P, SUB, NE])
        lg2 = sb("lg2", [P, SUB, NE])
        eq = sb("eq", [P, SUB, NE])
        sc = sb("sc", [P, SUB, NE])
        top = sb("top", [P, 4, SUB])
        onehot = sb("onehot", [P, 2, SUB, NE])
        chosen = sb("chosen", [P, SUB, NE], F16)
        rank = sb("rank", [P, SUB, NE])
        pick = sb("pick", [P, 2, SUB, NE])
        slot_f = sb("slot_f", [P, 2, SUB])
        slot_u = sb("slot_u", [P, 2, SUB], U32)
        dlt = sb("dlt", [P, SUB])
        weights = sb("weights", [P, 2, SUB])
        base = sb("base", [P, NE])
        ids = sb("ids", [P, SUB])
        cnt = sb("cnt", [P, NE])
        cnt_i = sb("cnt_i", [P, NE], I32)
        cnt_s = sb("cnt_s", [P, NE], I32)
        nt = sb("nt", [P, NE])
        g0 = sb("g0", [P, NE + 1])
        step = sb("step", [P, NE])
        row_f = sb("row_f", [P, ROWS])
        row_t = sb("row_t", [P, ROWS])
        tab_nt = sb("tab_nt", [P, NE], I32)
        tab_g0 = sb("tab_g0", [P, NE + 1], I32)
        tab_end = sb("tab_end", [P, NE], I32)
        tab_row = sb("tab_row", [P, ROWS], I32)
        xm = sb("xm", [P, TS, RW])
        xmT = sb("xmT", [P, 2, KD, T], F16)
        hf = r_sb[:, :, :].rearrange("p j (a t) -> p (j a) t", t=T)
        hm = hnT[:, :, :, :].rearrange("p h k (a t) -> p h (k a) t", t=T)
        meta = sb("meta", [P, TS, 2])
        wcur = sb("wcur", [P, TS])
        idcur = sb("idcur", [P, TS], U32)
        b2w = sb("b2w", [P, TS, D])
        y_w = sb("y_w", [P, TS, D])

        fin_x = [t[:, :, :] for t in (xa, xr, xn, tmp, x1, xn2, x1p)]
        fin_x.append(xT_f[:, :, :].rearrange("p k (a d) -> p (k a) d", d=D))
        fin_v = [t.rearrange("p (j d) -> p j d", j=SUB) for t in (
            s_f[:, :, :].rearrange("p k n -> p (k n)"), h2T[:, :, :].rearrange("p k n -> p (k n)"),
            *(in_w[:, h, :].bitcast(F32) for h in range(2)), *(conv_w[:, h, :].bitcast(F32) for h in range(2)),
            fc_w[:, :, :].rearrange("p h n -> p (h n)").bitcast(F32),
            out_w[:, :, :].rearrange("p h n -> p (h n)").bitcast(F32))]
        fin_g = hT_all[:, 0:2 * NB * D].bitcast(F32).rearrange("p (b d) -> p b d", b=NB)
        fin_std = sb("fin_std", [P, NB, SUB])
        fin_rstd = sb("fin_rstd", [P, NB, SUB])
        fin_nbias = sb("fin_nbias", [P, NB, SUB])
        fin_st = sb("fin_st", [P, NB, SUB, 6])
        fin_mv = sb("fin_mv", [P, NB, SUB, 2])

        names = """zeroed ident_ready consts_ready iota_ready iota_conv cond_loaded cols_loaded
        in_loaded conv_loaded fc_loaded out_loaded cproj_loaded rows_loaded router_loaded
        g16_ready cpb_ready silu_c_done modT_ps modT_read modrow_ps modrow_step modrow_done
        mod_stored colsum_ps fb_ps comp_ps comp_read w_hi w_lo bias_tmp
        xa_loaded ln1_step ln2_step ln_aggr ln_step ln_ready xn_done xT_ps xT_f32 xT_hi xT_lo
        h_ps h_hi h_lo gate_ps gate_done conv_ps r_done bn_in_step lnin_step lnin_ready hn_done
        hnT_ps hnT_hi hnT_lo u_ps s_f32 s_hi s_lo o_ps o_step t_done xr_loaded ga_loaded
        x1_step x1_done xn2_done rt_loaded h2_step h2_last_step x1p_done row_done row_stored
        h2T_ps h2T_done lg_ps mask_step mask_done weights_done rank_ps slot_step slots_done
        payload scattered base_ready
        table_step tables_ready filled xm_loaded xmT_ps xmT_hi xmT_lo
        w_loaded w_conv w_ready b2_loaded l1_ps hf_done hm_hi hm_lo y_ps meta_done meta_used b2_scaled b2w_done
        yw_done acc_added rows_added wait_passed acc_filled
        fin_prefetched fin_step fin_var fin_sqrt fin_recip fin_norm fin_ready fin_mul fin_sum fin_stored
        """.split()
        S = {n: sem(n) for n in names}
        FIN_LOADED = [sem(f"fin_loaded_{b}") for b in range(NB)]

        def rows_of(t, b):
            if isinstance(b, int):
                return t[b * SEQ:(b + 1) * SEQ, :].rearrange("(j p) d -> p j d", p=P)
            return t[bass.ds(b * SEQ, SEQ), :].rearrange("(j p) d -> p j d", p=P)

        x_rows = x.rearrange("b s d -> (b s) d")
        out_rows = out.rearrange("b s d -> (b s) d")

        def mod_bc(b, lo, hi):
            src = modd[b:b + 1, lo:hi, :] if isinstance(b, int) else modd[bass.ds(b, 1), lo:hi, :]
            return src.rearrange("a r d -> a (r d)").partition_broadcast(P)

        def col(t, b):
            return t[:, b:b + 1] if isinstance(b, int) else t[:, bass.ds(b, 1)]

        def three(pe, ps, stat, mov, first, last, lo_first=False):
            sh, sl = stat
            mh, ml = mov
            pe.matmul(ps, sh, mh, start=first, stop=False)
            pe.matmul(ps, sh, ml, start=False, stop=False)
            return pe.matmul(ps, sl, mh, start=False, stop=last)

        block = ctx.enter_context(nc.Block())

        STAGES = [(i, 0 <= i < NB, 0 <= i - 1 < NB, 0 <= i - 2 < NB, i + 1 < NB)
                  for i in range(NB + 2)]

        def run(eng, body):
            full = [s[0] for s in STAGES if all(s[1:]) and s[0] > 2]
            for s in STAGES:
                if s[0] == full[0]:
                    with eng.Fori(full[0], full[-1] + 1) as i:
                        body(i, True, True, True, True)
                elif s[0] not in full:
                    body(*s)

        def load_w(eng, e):
            w1, w2 = (W1T[e:e + 1], W2T[e:e + 1]) if isinstance(e, int) else (W1T[bass.ds(e, 1)], W2T[bass.ds(e, 1)])
            eng.dma_start(stage_w[:, 0:KD * FF].rearrange("p (k n) -> p k n", k=KD),
                          w1.rearrange("a (k p) n -> p (a k) n", p=P)).then_inc(S["w_loaded"], 16)
            eng.dma_start(stage_w[:, KD * FF:WE].rearrange("p (k n) -> p k n", k=KF),
                          w2.rearrange("a (k p) n -> p (a k) n", p=P)).then_inc(S["w_loaded"], 16)

        def wait_alone(eng, semaphore, value):
            eng.wait_ge(semaphore, value)
            eng.nop().then_inc(S["wait_passed"], 1)

        def expert_pairs(eng, expert):
            with eng.Fori(0, NE // 2 - 1) as pair:
                expert(pair * 2, 0, True, True)
                expert(pair * 2 + 1, 1, True, True)
            expert(NE - 2, 0, True, False)
            expert(NE - 1, 1, False, False)

        @block.sync
        def _(sp):
            sp.dma_start(xa[:, :, :], rows_of(x_rows, 0)).then_inc(S["xa_loaded"], 16)
            sp.dma_start(c_sb[:, :], cT).then_inc(S["cond_loaded"], 16)
            sp.dma_start(wmod_f.rearrange("p (k n) -> p k n", k=KD),
                         wmod.rearrange("(k p) n -> p k n", p=P)).then_inc(S["cond_loaded"], 16)
            sp.dma_start(in_f.rearrange("p (k n) -> p k n", k=KD),
                         in_wT.rearrange("(k p) n -> p k n", p=P)).then_inc(S["in_loaded"], 16)
            for n, (src, w) in enumerate([(ln_g, KI), (ln_b, KI), (cproj_b, KI), (fc_b, KD)]):
                sp.dma_start(cols[:, n * KI:n * KI + w], src).then_inc(S["cols_loaded"], 16)
            sp.dma_start(b1c[:, :], b1).then_inc(S["cols_loaded"], 16)
            sp.wait_ge(S["zeroed"], 1)
            for g in range(P // G):
                for c in range(KI):
                    dst = conv_f[g * G:(g + 1) * G, :].rearrange(
                        "p (c t m) -> p c t m", c=KI, t=TAPS)[:, c, :, g * G:(g + 1) * G]
                    sp.dma_start(dst, convT[c, g]).then_inc(S["conv_loaded"], 16)
            sp.dma_start(convb_f[0:64, :], conv_b.partition_broadcast(64)).then_inc(S["rows_loaded"], 16)
            for n, src in enumerate([gamma, beta]):
                sp.dma_start(gb_row[:, n, :], src.partition_broadcast(NB)).then_inc(S["rows_loaded"], 16)
            for dst, src, s in [(out_f, outT, "out_loaded"), (cproj_f, cproj, "cproj_loaded"),
                                (fc_f, fcT, "fc_loaded")]:
                sp.dma_start(dst.rearrange("p (k n) -> p k n", k=KI),
                             src.rearrange("(k p) n -> p k n", p=P)).then_inc(S[s], 16)
            sp.dma_start(router_w[:, :, :], WrT.rearrange("(k p) e -> p k e", p=P)).then_inc(S["router_loaded"], 16)
            for j in range(SUB):
                sp.dma_start(br4[:, j, :], br.partition_broadcast(P)).then_inc(S["router_loaded"], 16)
            sp.dma_start(b2r[:, :, :].rearrange("p e d -> p (e d)"),
                         b2.partition_broadcast(P)).then_inc(S["b2_loaded"], 16)
            sp.wait_ge(S["modrow_done"], 1)
            sp.dma_start(modd, modrow[:, :, :]).then_inc(S["mod_stored"], 16)
            sp.wait_ge(S["mod_stored"], 16)
            sp.dma_start(rt_row[:, :, :].rearrange("p r d -> p (r d)"), mod_bc(0, 1, 4)).then_inc(S["rt_loaded"], 16)
            sp.wait_ge(S["consts_ready"], 3)
            sp.dma_start(moe_acc[TOKENS:TOKENS + T, :].rearrange("(p j) d -> p j d", j=TS),
                         filler[:, :, 0:D]).then_inc(S["acc_filled"], 16)

            def body(i, front, mid, route, pre):
                if mid:
                    if not (isinstance(i, int) and i == 1):
                        sp.wait_ge(S["x1_done"], (i - 1) * SUB)
                    sp.dma_start(xr[:, :, :], rows_of(x_rows, i - 1)).then_inc(S["xr_loaded"], 16)
                    sp.dma_start(ga_row[:, :], mod_bc(i - 1, 0, 1)).then_inc(S["ga_loaded"], 16)
                if pre:
                    sp.wait_ge(S["xn_done"], i + 1)
                    sp.dma_start(xa[:, :, :], rows_of(x_rows, i + 1)).then_inc(S["xa_loaded"], 16)
                if route:
                    b = i - 2
                    sp.wait_ge(S["row_done"], b * SUB + SUB)
                    sp.dma_start(rows_of(moe_acc, b), h2x[:, :, 0:D]).then_inc(S["row_stored"], 16)
                    sp.wait_ge(S["x1p_done"], b * SUB + SUB)
                    sp.dma_start(rows_of(resid, b), x1p[:, :, :]).then_inc(S["row_stored"], 16)
                    if not (isinstance(b, int) and b == NB - 1):
                        sp.dma_start(rt_row[:, :, :].rearrange("p r d -> p (r d)"),
                                     mod_bc(b + 1, 1, 4)).then_inc(S["rt_loaded"], 16)
                if isinstance(i, int) and i == NB:
                    load_w(sp, 0)

            run(sp, body)

            def load_tile(g):
                r = sp.value_load(tab_row[0:1, g:g + 1] if isinstance(g, int) else tab_row[0:1, bass.ds(g, 1)],
                                  min_val=0, max_val=NE * REGION - T)
                sp.dma_start(xm[:, :, :], gathered[bass.ds(r, T), :].rearrange("(p j) c -> p j c", j=TS))\
                  .then_inc(S["xm_loaded"], 16)

            def fill(e):
                r = sp.value_load(tab_end[0:1, e:e + 1], min_val=0, max_val=NE * REGION - T)
                sp.dma_start(gathered[bass.ds(r, T), :].rearrange("(p j) c -> p j c", j=TS),
                             filler[:, :, :]).then_inc(S["filled"], 16)

            sp.wait_ge(S["tables_ready"], 1)
            sp.wait_ge(S["scattered"], 16 * 2 * SUB * NB)
            fill(0)
            sp.wait_ge(S["filled"], 16)
            load_tile(0)
            for e in range(1, NE):
                fill(e)
            sp.wait_ge(S["w_ready"], WQ)
            load_w(sp, 1)
            sp.wait_ge(S["filled"], 16 * NE)

            def expert(e, buf, has_next, has_after):
                first = sp.value_load(tab_g0[0:1, e:e + 1] if isinstance(e, int) else tab_g0[0:1, bass.ds(e, 1)],
                                      min_val=0, max_val=MAXT - 2)
                n = sp.value_load(tab_nt[0:1, e:e + 1] if isinstance(e, int) else tab_nt[0:1, bass.ds(e, 1)],
                                  min_val=1, max_val=MAXT - 2)
                with sp.Fori(0, n) as t:
                    g = sp.snap(first + t)
                    sp.wait_ge(S["xmT_ps"], g + 1)
                    sp.wait_ge(S["meta_done"], g + 1)
                    load_tile(g + 1)

            expert_pairs(sp, expert)
            total = sp.value_load(tab_g0[0:1, NE:NE + 1], min_val=1, max_val=MAXT - 2)
            wait_alone(sp, S["xm_loaded"], total * 16 + 16)

            def fin_rows(t, b):
                return t[b * SEQ:(b + 1) * SEQ, :].rearrange("(p j) d -> p j d", j=SUB)

            sp.wait_ge(S["row_stored"], 32 * NB)
            for b in range(NB):
                sp.dma_start(fin_x[b], fin_rows(resid, b)).then_inc(S["fin_prefetched"], 16)
            sp.dma_start(fin_g, modd[:, 4:5, :].rearrange("b r d -> r b d").partition_broadcast(P))\
                .then_inc(S["fin_prefetched"], 16)
            sp.wait_ge(S["acc_added"], total * (16 * TS))
            for b in range(NB):
                sp.dma_start(fin_v[b], fin_rows(moe_acc, b)).then_inc(FIN_LOADED[b], 16)
            for b in range(NB):
                sp.wait_ge(S["fin_sum"], b + 1)
                sp.dma_start(fin_rows(out_rows, b), fin_x[b]).then_inc(S["fin_stored"], 16)
            sp.wait_ge(S["fin_stored"], 16 * NB)
            sp.wait_ge(S["acc_filled"], 16)

        @block.gpsimd
        def _(pool):
            pool.memset(ident[:, :], 0.0).then_inc(S["ident_ready"], 1)
            pool.memset(before[:, :], 0.0).then_inc(S["ident_ready"], 1)
            pool.wait_ge(S["ident_ready"], 2)
            pool.affine_select(out=ident[:, :], in_=ident[:, :], compare_op=ALU.not_equal, fill=1.0,
                               base=0, pattern=[[-1, P]], channel_multiplier=1).then_inc(S["ident_ready"], 1)
            pool.affine_select(out=before[:, :], in_=before[:, :], compare_op=ALU.is_ge, fill=1.0,
                               base=0, pattern=[[-1, P]], channel_multiplier=1).then_inc(S["ident_ready"], 1)
            o = 0
            for pattern, base_, mult, n in [([[0, SUB], [-1, NE]], NE, 0, SUB * NE),
                                            ([[REGION, NE]], 0, 0, NE), ([[P, SUB]], 0, 1, SUB),
                                            ([[1, ROWS]], 0, 0, ROWS), ([[1, TS]], TOKENS, TS, TS)]:
                pool.iota(iota_i[:, o:o + n], pattern, base=base_, channel_multiplier=mult)\
                    .then_inc(S["iota_ready"], 1)
                o += n
            pool.wait_ge(S["iota_ready"], 5)
            pool.tensor_copy(iota_f[:, :], iota_i[:, :]).then_inc(S["iota_conv"], 1)
            pool.memset(filler[:, :, :], 0.0).then_inc(S["consts_ready"], 1)
            pool.memset(h2x[:, :, C_W + 1:RW], 0.0).then_inc(S["consts_ready"], 1)
            pool.wait_ge(S["consts_ready"], 2)
            pool.wait_ge(S["iota_conv"], 1)
            pool.tensor_copy(filler[:, :, C_ID], fill_id).then_inc(S["consts_ready"], 1)
            pool.tensor_copy(ids[:, :], token0).then_inc(S["consts_ready"], 1)
            pool.tensor_copy(base[:, :], region0).then_inc(S["base_ready"], 1)
            pool.wait_ge(S["consts_ready"], 4)

            def xT_lo(b):
                for k in range(KD):
                    pool.wait_ge(S["xT_hi"], b * KD + k + 1)
                    pool.tensor_tensor(xT[:, 1, k, :], xT_f[:, k, :], xT[:, 0, k, :], ALU.subtract)\
                        .then_inc(S["xT_lo"], 1)

            def x1_add(b, j):
                pool.wait_ge(S["t_done"], b * SUB + j + 1)
                if j == 0:
                    pool.wait_ge(S["ga_loaded"], (b + 1) * 16)
                    pool.wait_ge(S["xr_loaded"], (b + 1) * 16)
                    if not (isinstance(b, int) and b == 0):
                        pool.wait_ge(S["xn2_done"], b * SUB)
                        pool.wait_ge(S["x1p_done"], b * SUB)
                pool.tensor_tensor(tmp[:, j, :], tmp[:, j, :], ga_row[:, :], ALU.mult).then_inc(S["x1_step"], 1)
                pool.wait_ge(S["x1_step"], b * SUB + j + 1)
                pool.tensor_tensor(x1[:, j, :], tmp[:, j, :], xr[:, j, :], ALU.add).then_inc(S["x1_done"], 1)

            def scatter(b, k):
                if k == 0:
                    wait_alone(pool, S["slots_done"], b + 1)
                    pool.tensor_copy(h2x[:, :, C_ID], ids[:, :]).then_inc(S["payload"], 1)
                    wait_alone(pool, S["weights_done"], b + 1)
                    pool.tensor_scalar(h2x[:, :, C_W], weights[:, 0, :], 1 / WS, None, ALU.mult)\
                        .then_inc(S["payload"], 1)
                    wait_alone(pool, S["payload"], b * 4 + 2)
                    pool.tensor_scalar(ids[:, :], ids[:, :], float(SEQ), None, ALU.add).then_inc(S["payload"], 1)
                else:
                    wait_alone(pool, S["scattered"], (b * 2 + 1) * (16 * SUB))
                    pool.tensor_scalar(h2x[:, :, C_W], weights[:, 1, :], 1 / WS, None, ALU.mult)\
                        .then_inc(S["payload"], 1)
                    wait_alone(pool, S["payload"], b * 4 + 4)
                for j in range(SUB):
                    pool.indirect_dma_start(
                        out=gathered, out_offset=bass.IndirectOffsetOnAxis(ap=slot_u[:, k, j:j + 1], axis=0),
                        in_=h2x[:, j, :], in_offset=None).then_inc(S["scattered"], 16)

            def body(i, front, mid, route, pre):
                if route:
                    b = i - 2
                    pool.wait_ge(S["rt_loaded"], (b + 1) * 16)
                    if not (isinstance(b, int) and b == 0):
                        pool.wait_ge(S["row_stored"], b * 32)
                        pool.wait_ge(S["scattered"], b * (32 * SUB))
                    for j in range(SUB if mid else 0):
                        pool.wait_ge(S["xn2_done"], b * SUB + j + 1)
                        pool.tensor_tensor(h2x[:, j, 0:D], xn2[:, j, :], rt_row[:, 0, :], ALU.mult)\
                            .then_inc(S["h2_step"], 1)
                        pool.wait_ge(S["h2_step"], b * SUB + j + 1)
                        pool.tensor_tensor(h2x[:, j, 0:D], h2x[:, j, 0:D], rt_row[:, 1, :], ALU.add)\
                            .then_inc(S["row_done"], 1)
                    for j in range(SUB):
                        pool.tensor_tensor(x1p[:, j, :], x1[:, j, :], rt_row[:, 2, :], ALU.add)\
                            .then_inc(S["x1p_done"], 1)
                if mid:
                    x1_add(i - 1, 0)
                    x1_add(i - 1, 1)
                if route:
                    scatter(i - 2, 0)
                if pre:
                    xT_lo(i + 1)
                if mid:
                    x1_add(i - 1, 2)
                    x1_add(i - 1, 3)
                if route:
                    scatter(i - 2, 1)

            xT_lo(0)
            pool.wait_ge(S["b2_loaded"], 16)
            pool.tensor_scalar(b2r[:, :, :], b2r[:, :, :], WS, None, ALU.mult).then_inc(S["b2_scaled"], 1)
            run(pool, body)

            pool.wait_ge(S["b2_scaled"], 1)
            pool.nop().then_inc(S["rows_added"], 1)
            pool.wait_ge(S["row_stored"], 32 * NB)
            pool.wait_ge(S["acc_filled"], 16)
            pool.wait_ge(S["tables_ready"], 1)

            def take_meta(g):
                wait_alone(pool, S["xm_loaded"], (g + 1) * 16)
                pool.tensor_copy(meta[:, :, :], xm[:, :, C_ID:C_W + 1]).then_inc(S["meta_done"], 1)

            take_meta(0)

            def expert(e, buf, has_next, has_after):
                first = pool.value_load(tab_g0[0:1, e:e + 1] if isinstance(e, int) else tab_g0[0:1, bass.ds(e, 1)],
                                        min_val=0, max_val=MAXT - 2)
                n = pool.value_load(tab_nt[0:1, e:e + 1] if isinstance(e, int) else tab_nt[0:1, bass.ds(e, 1)],
                                    min_val=1, max_val=MAXT - 2)
                b2e = b2r[:, e:e + 1, :] if isinstance(e, int) else b2r[:, bass.ds(e, 1), :]
                with pool.Fori(0, n) as t:
                    g = pool.snap(first + t)
                    wait_alone(pool, S["meta_done"], g + 1)
                    pool.tensor_copy(idcur[:, :], meta[:, :, 0]).then_inc(S["meta_used"], 1)
                    pool.tensor_copy(wcur[:, :], meta[:, :, 1]).then_inc(S["meta_used"], 1)
                    pool.wait_ge(S["meta_used"], g * 2 + 2)
                    pool.tensor_tensor(b2w[:, :, :], b2e.to_broadcast([P, TS, D]),
                                       wcur[:, :].unsqueeze(2).to_broadcast([P, TS, D]), ALU.mult)\
                        .then_inc(S["b2w_done"], 1)
                    take_meta(g + 1)
                    wait_alone(pool, S["yw_done"], g * TS + TS + 1)
                    for j in range(TS):
                        pool.indirect_dma_start(
                            out=moe_acc, out_offset=bass.IndirectOffsetOnAxis(ap=idcur[:, j:j + 1], axis=0),
                            in_=y_w[:, j, :], in_offset=None, compute_op=ALU.add).then_inc(S["acc_added"], 16)
                    pool.wait_ge(S["acc_added"], (g + 1) * (16 * TS))
                    pool.nop().then_inc(S["rows_added"], 1)

            expert_pairs(pool, expert)

            pool.wait_ge(S["fin_prefetched"], 16 * (NB + 1))
            for b in range(NB):
                pool.wait_ge(S["fin_norm"], b + 1)
                pool.tensor_tensor(fin_v[b], fin_v[b], fin_g[:, b:b + 1, :].to_broadcast([P, SUB, D]), ALU.mult)\
                    .then_inc(S["fin_mul"], 1)

        @block.scalar
        def _(act):
            def split_hi(dst, src, scale=WS):
                act.activation(dst, src, ACT.Copy, scale=scale).then_inc(S["w_hi"], 1)

            def xn_norm(b):
                act.wait_ge(S["ln_ready"], b + 1)
                if not (isinstance(b, int) and b == 0):
                    act.wait_ge(S["xT_ps"], b * KD)
                for j in range(SUB):
                    a = act.activation(xn[:, j, :], xa[:, j, :], ACT.Identity,
                                       bias=nbias_12[:, j:j + 1], scale=rstd_12[:, j:j + 1])
                a.then_inc(S["xn_done"], 1)

            def xT_split(b):
                for k in range(KD):
                    act.wait_ge(S["xT_ps"], b * KD + k + 1)
                    if k == 0 and not (isinstance(b, int) and b == 0):
                        act.wait_ge(S["xT_lo"], b * KD)
                    act.activation(xT_f[:, k, :], bank[6 + k][:, :], ACT.Identity,
                                   bias=col(shiftT[:, k, :], b), scale=col(scaleT[:, k, :], b))\
                        .then_inc(S["xT_f32"], 1)
                    act.wait_ge(S["xT_f32"], b * KD + k + 1)
                    act.activation(xT[:, 0, k, :], xT_f[:, k, :], ACT.Copy).then_inc(S["xT_hi"], 1)

            def h_hi(b, m):
                act.wait_ge(S["h_ps"], b * KI + m + 1)
                act.activation(hT[:, 0, m, PAD:], bank[m % 2][:, :], ACT.Copy, scale=1 / WS)\
                    .then_inc(S["h_hi"], 1)

            def gate(b, j):
                act.wait_ge(S["gate_ps"], b * SUB + j + 1)
                if not (isinstance(b, int) and b * SUB + j == 0):
                    act.wait_ge(S["r_done"], b * SUB + j)
                act.activation(gate_sb[:, :], bank[2][:, :], ACT.Silu, scale=1 / WS).then_inc(S["gate_done"], 1)

            def hnT_hi(b, j):
                act.wait_ge(S["hnT_ps"], b * SUB + j + 1)
                act.activation(hnT[:, 0, :, j * P:(j + 1) * P],
                               bank[6 + j % 2][:, :].rearrange("p (k t) -> p k t", k=KI), ACT.Copy)\
                    .then_inc(S["hnT_hi"], 1)

            def body(i, front, mid, route, pre):
                if front:
                    h_hi(i, 0)
                    h_hi(i, 1)
                    gate(i, 0)
                if mid:
                    hnT_hi(i - 1, 0)
                    hnT_hi(i - 1, 1)
                if front:
                    h_hi(i, 2)
                if mid:
                    hnT_hi(i - 1, 2)
                if front:
                    h_hi(i, 3)
                if mid:
                    hnT_hi(i - 1, 3)
                if route:
                    b = i - 2
                    act.wait_ge(S["ln_ready"], b + 4)
                    if not (isinstance(b, int) and b == 0):
                        act.wait_ge(S["row_done"], b * SUB)
                    for j in range(SUB):
                        act.activation(xn2[:, j, :], x1[:, j, :], ACT.Identity,
                                       bias=nbias_12[:, SUB + j:SUB + j + 1],
                                       scale=rstd_12[:, SUB + j:SUB + j + 1])\
                            .then_inc(S["xn2_done"], 1)
                if mid:
                    b = i - 1
                    for m in range(KD):
                        act.wait_ge(S["u_ps"], b * KD + m + 1)
                        if m == 0 and not (isinstance(b, int) and b == 0):
                            act.wait_ge(S["s_lo"], b * KD)
                        act.activation(s_f[:, m, :], bank[m][:, :], ACT.Silu, bias=fc_bias[:, m:m + 1],
                                       scale=1 / WS).then_inc(S["s_f32"], 1)
                        act.wait_ge(S["s_f32"], b * KD + m + 1)
                        act.activation(sT[:, 0, m, :], s_f[:, m, :], ACT.Copy).then_inc(S["s_hi"], 1)
                if front:
                    gate(i, 1)
                if route:
                    for k in range(KD):
                        act.wait_ge(S["h2T_ps"], (i - 2) * KD + k + 1)
                        act.activation(h2T[:, k, :], bank[6 + k][:, :], ACT.Copy).then_inc(S["h2T_done"], 1)
                if pre:
                    xn_norm(i + 1)
                if front:
                    gate(i, 2)
                if front:
                    gate(i, 3)
                if route:
                    b = i - 2
                    act.wait_ge(S["mask_done"], b + 1)
                    if not (isinstance(b, int) and b == 0):
                        act.wait_ge(S["payload"], b * 4)
                    act.activation(weights[:, 0, :], dlt[:, :], ACT.Sigmoid, scale=-1.0)
                    act.activation(weights[:, 1, :], dlt[:, :], ACT.Sigmoid).then_inc(S["weights_done"], 1)
                if pre:
                    xT_split(i + 1)
                if front:
                    act.wait_ge(S["lnin_ready"], i + 1)
                    for j in range(SUB):
                        act.activation(r_sb[:, j, :], r_sb[:, j, :], ACT.Identity,
                                       bias=nbias_in[:, j:j + 1], scale=rstd_in[:, j:j + 1])\
                            .then_inc(S["hn_done"], 1)

            act.wait_ge(S["cond_loaded"], 32)
            act.activation(silu_c[:, :], c_sb[:, :], ACT.Silu).then_inc(S["silu_c_done"], 1)
            xn_norm(0)
            act.wait_ge(S["in_loaded"], 16)
            split_hi(in_w[:, 0, :], in_f)
            act.wait_ge(S["modT_read"], 2)
            xT_split(0)
            act.wait_ge(S["conv_loaded"], 16 * KI * (P // G))
            split_hi(conv_w[:, 0, :], conv_f)
            act.wait_ge(S["rows_loaded"], 48)
            split_hi(bias_hi[:, 0:INNER], convb_f[0:64, :])
            act.wait_ge(S["g16_ready"], 1)
            act.wait_ge(S["fc_loaded"], 16)
            for k in range(KI):
                a = act.activation(fc_w[:, 0, k * D:(k + 1) * D], fc_f[:, k * D:(k + 1) * D], ACT.Copy,
                                   scale=g16[:, k:k + 1])
            a.then_inc(S["w_hi"], 1)
            act.wait_ge(S["out_loaded"], 16)
            split_hi(out_w[:, 0, :], out_f)
            act.wait_ge(S["comp_ps"], 1)
            split_hi(comp_w[:, 0, :], bank[1][:, :])
            act.wait_ge(S["colsum_ps"], 1)
            split_hi(bias_hi[:, INNER:], bank[0][0:64, D:2 * D])

            run(act, body)

            def w_split(n, buf):
                act.wait_ge(S["w_loaded"], n * 32)
                for q in range(WQ):
                    c = slice(q * (WE // WQ), (q + 1) * (WE // WQ))
                    act.activation(split_w[:, buf, 0, c], stage_w[:, c], ACT.Copy, scale=WS)\
                        .then_inc(S["w_conv"], 1)

            def xmT_hi(g):
                act.wait_ge(S["xmT_ps"], g + 1)
                act.activation(xmT[:, 0, :, :].rearrange("p k t -> p (k t)"), bank[6][:, :], ACT.Copy)\
                    .then_inc(S["xmT_hi"], 1)

            act.nop().then_inc(S["hf_done"], 1)
            w_split(1, 0)
            act.wait_ge(S["tables_ready"], 1)
            xmT_hi(0)

            def expert(e, buf, has_next, has_after):
                first = act.value_load(tab_g0[0:1, e:e + 1] if isinstance(e, int) else tab_g0[0:1, bass.ds(e, 1)],
                                       min_val=0, max_val=MAXT - 2)
                n = act.value_load(tab_nt[0:1, e:e + 1] if isinstance(e, int) else tab_nt[0:1, bass.ds(e, 1)],
                                   min_val=1, max_val=MAXT - 2)
                with act.Fori(0, n) as t:
                    g = act.snap(first + t)
                    for c in range(KF):
                        if c % 2 == 0:
                            if c == 0:
                                act.wait_ge(S["hm_lo"], g * (KF // 2) + 1)
                            act.wait_ge(S["l1_ps"], g * (KF // 2) + c // 2 + 1)
                        act.activation(hf[:, c, :], bank[c // 2][:, (c % 2) * T:(c % 2 + 1) * T], ACT.Relu,
                                       bias=col(b1c, e * KF + c), scale=1 / WS).then_inc(S["hf_done"], 1)
                    xmT_hi(g + 1)
                    if has_next:
                        with act.If(t == 0):
                            act.wait_ge(S["y_ps"], first + 1)
                            w_split(e + 2, 1 - buf)
                    if has_after:
                        with act.If(t == 0):
                            act.wait_ge(S["w_ready"], (e + 2) * WQ)
                            load_w(act, e + 2)

            expert_pairs(act, expert)

            def norm(b):
                act.wait_ge(S["fin_ready"], b + 1)
                for j in range(SUB):
                    a = act.activation(fin_v[b][:, j, :], fin_v[b][:, j, :], ACT.Identity,
                                       bias=fin_nbias[:, b, j:j + 1], scale=fin_rstd[:, b, j:j + 1])
                a.then_inc(S["fin_norm"], 1)

            for b in range(NB):
                act.wait_ge(S["fin_var"], b + 1)
                act.activation(fin_std[:, b, :], fin_mv[:, b, :, 1], ACT.Sqrt).then_inc(S["fin_sqrt"], 1)
                if b >= 1:
                    norm(b - 1)
            norm(NB - 1)

        @block.vector
        def _(dve):
            def rsqrt(mv, nw, rstd, nbias, s, at):
                ve, y, a, yi = (nw[:, k, :] for k in range(4))
                var, mean = mv[:, :, 1], mv[:, :, 0]
                c = 0

                def do(ins, last=False):
                    nonlocal c
                    c += 1
                    ins.then_inc(S[s], 1)
                    if not last:
                        dve.wait_ge(S[s], at + c)

                do(dve.tensor_scalar(ve, var, EPS, None, ALU.add))
                do(dve.tensor_scalar(yi.bitcast(I32), ve.bitcast(I32), 1, None, ALU.logical_shift_right))
                do(dve.tensor_scalar(y.bitcast(I32), yi.bitcast(I32), -1.0, RSQRT_MAGIC, ALU.mult, ALU.add))
                for it in range(NEWTON):
                    do(dve.scalar_tensor_tensor(out=a, in0=y, scalar=-0.5, in1=y, op0=ALU.mult, op1=ALU.mult))
                    do(dve.tensor_tensor(a, a, ve, ALU.mult))
                    to = rstd[:, :] if it == NEWTON - 1 else y
                    do(dve.scalar_tensor_tensor(out=to, in0=a, scalar=1.5, in1=y, op0=ALU.add, op1=ALU.mult))
                do(dve.scalar_tensor_tensor(out=nbias[:, :], in0=mean, scalar=-1.0, in1=rstd[:, :],
                                            op0=ALU.mult, op1=ALU.mult))
                return c

            RSQRT_STEPS = 4 + 3 * NEWTON

            def ln1_stats(b):
                dve.wait_ge(S["xa_loaded"], (b + 1) * 16)
                for j in range(SUB):
                    dve.bn_stats(st_12[:, 0, j, :], xa[:, j, :]).then_inc(S["ln1_step"], 1)

            def ln2_stats(b, j):
                dve.wait_ge(S["x1_done"], b * SUB + j + 1)
                dve.bn_stats(st_12[:, 1, j, :], x1[:, j, :]).then_inc(S["ln2_step"], 1)

            def ln12(i, pre, route):
                if pre:
                    wait_alone(dve, S["ln1_step"], (i + 2) * SUB)
                    for j in range(SUB):
                        dve.bn_aggr(mv_12[:, j, :], st_12[:, 0, j, :]).then_inc(S["ln_aggr"], 1)
                if route:
                    wait_alone(dve, S["ln2_step"], (i - 1) * SUB)
                    for j in range(SUB):
                        dve.bn_aggr(mv_12[:, SUB + j, :], st_12[:, 1, j, :]).then_inc(S["ln_aggr"], 1)
                dve.wait_ge(S["ln_aggr"], (min(i + 2, NB) + max(i - 1, 0)) * SUB if isinstance(i, int)
                            else i * (2 * SUB) + SUB)
                if not (isinstance(i, int) and i < 0):
                    dve.wait_ge(S["xn_done"], min(i + 1, NB) if isinstance(i, int) else i + 1)
                if not (isinstance(i, int) and i <= 2):
                    dve.wait_ge(S["xn2_done"], (i - 2) * SUB)
                at = (i + 1) * RSQRT_STEPS
                rsqrt(mv_12, nw_12, rstd_12, nbias_12, "ln_step", at)
                dve.wait_ge(S["ln_step"], at + RSQRT_STEPS)
                dve.nop().then_inc(S["ln_ready"], 1)

            def split_lo(dst, src, hi, n, scale=WS):
                dve.wait_ge(S["w_hi"], n)
                dve.scalar_tensor_tensor(out=dst, in0=src, scalar=scale, in1=hi, op0=ALU.mult,
                                         op1=ALU.subtract)

            def h_lo(b, m):
                dve.wait_ge(S["h_hi"], b * KI + m + 1)
                dve.scalar_tensor_tensor(out=hT[:, 1, m, PAD:], in0=bank[m % 2][:, :], scalar=1 / WS,
                                         in1=hT[:, 0, m, PAD:], op0=ALU.mult, op1=ALU.subtract)\
                    .then_inc(S["h_lo"], 1)

            def hnT_lo(b, j):
                dve.wait_ge(S["hnT_hi"], b * SUB + j + 1)
                dve.tensor_tensor(hnT[:, 1, :, j * P:(j + 1) * P],
                                  bank[6 + j % 2][:, :].rearrange("p (k t) -> p k t", k=KI),
                                  hnT[:, 0, :, j * P:(j + 1) * P], ALU.subtract).then_inc(S["hnT_lo"], 1)

            def r_tile(b, j):
                dve.wait_ge(S["conv_ps"], b * SUB + j + 1)
                dve.wait_ge(S["gate_done"], b * SUB + j + 1)
                if not (isinstance(b, int) and b == 0):
                    dve.wait_ge(S["hnT_ps"], (b - 1) * SUB + j + 1)
                dve.scalar_tensor_tensor(out=r_sb[:, j, :], in0=bank[3][:, :], scalar=1 / WS, in1=gate_sb[:, :],
                                         op0=ALU.mult, op1=ALU.mult).then_inc(S["r_done"], 1)
                dve.wait_ge(S["r_done"], b * SUB + j + 1)
                dve.bn_stats(st_in[:, j, :], r_sb[:, j, :]).then_inc(S["bn_in_step"], 1)

            def ln_inner(b):
                wait_alone(dve, S["bn_in_step"], b * (2 * SUB) + SUB)
                for j in range(SUB):
                    dve.bn_aggr(mv_in[:, j, :], st_in[:, j, :]).then_inc(S["bn_in_step"], 1)
                dve.wait_ge(S["bn_in_step"], (b + 1) * (2 * SUB))
                if not (isinstance(b, int) and b == 0):
                    dve.wait_ge(S["hn_done"], b * SUB)
                at = b * RSQRT_STEPS
                rsqrt(mv_in, nw_in, rstd_in, nbias_in, "lnin_step", at)
                dve.wait_ge(S["lnin_step"], at + RSQRT_STEPS)
                dve.nop().then_inc(S["lnin_ready"], 1)

            def inner_stats(b):
                if not (isinstance(b, int) and b == 0):
                    dve.wait_ge(S["t_done"], b * SUB)
                dve.tensor_tensor(std[:, :], nw_in[:, 0, :], rstd_in[:, :], ALU.mult).then_inc(S["o_step"], 1)
                dve.tensor_scalar(m16[:, :], mv_in[:, :, 0], WS, None, ALU.mult).then_inc(S["o_step"], 1)

            def o_tile(b, j):
                if j == 0:
                    dve.wait_ge(S["o_step"], b * (2 + SUB) + 2)
                    if not (isinstance(b, int) and b == 0):
                        dve.wait_ge(S["x1_done"], b * SUB)
                dve.wait_ge(S["o_ps"], b * SUB + j + 1)
                dve.scalar_tensor_tensor(out=tmp[:, j, :], in0=colsum[:, :], scalar=m16[:, j:j + 1],
                                         in1=bank[5][:, D:2 * D], op0=ALU.mult, op1=ALU.add)\
                    .then_inc(S["o_step"], 1)
                dve.wait_ge(S["o_step"], b * (2 + SUB) + 3 + j)
                dve.scalar_tensor_tensor(out=tmp[:, j, :], in0=bank[5][:, 0:D], scalar=std[:, j:j + 1],
                                         in1=tmp[:, j, :], op0=ALU.mult, op1=ALU.add).then_inc(S["t_done"], 1)

            MASK_STEPS = 14

            def top2(b):
                c = 0

                def do(ins):
                    nonlocal c
                    c += 1
                    ins.then_inc(S["mask_step"], 1)
                    dve.wait_ge(S["mask_step"], b * MASK_STEPS + c)

                def bc(a):
                    return a.unsqueeze(2).to_broadcast([P, SUB, NE])

                dve.wait_ge(S["lg_ps"], b + 1)
                do(dve.tensor_tensor(lg[:, :, :], bank[4][:, 0:SUB * NE].rearrange("p (j e) -> p j e", j=SUB),
                                     br4[:, :, :], ALU.add))
                src = lg
                for k in range(2):
                    v, mx = top[:, k, :], top[:, 2 + k, :]
                    do(dve.tensor_reduce(v, src[:, :, :], AX, ALU.max))
                    do(dve.tensor_tensor(eq[:, :, :], src[:, :, :], bc(v), ALU.is_equal))
                    do(dve.tensor_tensor(sc[:, :, :], eq[:, :, :], rev, ALU.mult))
                    do(dve.tensor_reduce(mx, sc[:, :, :], AX, ALU.max))
                    do(dve.tensor_tensor(onehot[:, k, :, :], sc[:, :, :], bc(mx), ALU.is_equal))
                    if k == 0:
                        do(dve.scalar_tensor_tensor(out=lg2[:, :, :], in0=onehot[:, 0, :, :], scalar=MASKED,
                                                    in1=lg[:, :, :], op0=ALU.mult, op1=ALU.add))
                        src = lg2
                if not (isinstance(b, int) and b == 0):
                    dve.wait_ge(S["weights_done"], b)
                do(dve.tensor_tensor(dlt[:, :], top[:, 1, :], top[:, 0, :], ALU.subtract))
                do(dve.tensor_tensor(chosen[:, :, :], onehot[:, 0, :, :], onehot[:, 1, :, :], ALU.add))
                assert c == MASK_STEPS
                dve.nop().then_inc(S["mask_done"], 1)

            def h2_last(b):
                dve.wait_ge(S["rt_loaded"], (b + 1) * 16)
                dve.wait_ge(S["row_stored"], b * 32)
                dve.wait_ge(S["scattered"], b * (32 * SUB))
                for j in range(SUB):
                    dve.wait_ge(S["xn2_done"], b * SUB + j + 1)
                    dve.tensor_tensor(h2x[:, j, 0:D], xn2[:, j, :], rt_row[:, 0, :], ALU.mult)\
                        .then_inc(S["h2_last_step"], 1)
                for j in range(SUB):
                    dve.wait_ge(S["h2_last_step"], j + 1)
                    dve.tensor_tensor(h2x[:, j, 0:D], h2x[:, j, 0:D], rt_row[:, 1, :], ALU.add)\
                        .then_inc(S["row_done"], 1)

            def slots(b):
                c = 0

                def do(ins):
                    nonlocal c
                    c += 1
                    ins.then_inc(S["slot_step"], 1)
                    dve.wait_ge(S["slot_step"], b * 5 + c)

                dve.wait_ge(S["rank_ps"], b + 1)
                R0 = SUB * NE
                do(dve.tensor_tensor(rank[:, :, :], bank[4][:, R0:2 * R0].rearrange("p (j e) -> p j e", j=SUB),
                                     base[:, :].unsqueeze(1).to_broadcast([P, SUB, NE]), ALU.add))
                do(dve.tensor_tensor(base[:, :], bank[4][:, 2 * R0:2 * R0 + NE], base[:, :], ALU.add))
                for k in range(2):
                    ins = dve.tensor_tensor(pick[:, k, :, :], onehot[:, k, :, :], rank[:, :, :], ALU.mult)
                do(ins)
                do(dve.tensor_reduce(slot_f[:, :, :], pick[:, :, :, :], AX, ALU.add))
                if not (isinstance(b, int) and b == 0):
                    dve.wait_ge(S["scattered"], b * (32 * SUB))
                do(dve.tensor_copy(slot_u[:, :, :], slot_f[:, :, :]))
                dve.nop().then_inc(S["slots_done"], 1)

            def body(i, front, mid, route, pre):
                if mid:
                    inner_stats(i - 1)
                if front:
                    h_lo(i, 0)
                    h_lo(i, 1)
                if mid:
                    hnT_lo(i - 1, 0)
                    hnT_lo(i - 1, 1)
                if pre:
                    ln1_stats(i + 1)
                if front:
                    h_lo(i, 2)
                if mid:
                    hnT_lo(i - 1, 2)
                if front:
                    h_lo(i, 3)
                if mid:
                    hnT_lo(i - 1, 3)
                if route:
                    ln2_stats(i - 2, 3)
                ln12(i, pre, route)
                if front:
                    r_tile(i, 0)
                if mid:
                    for m in range(KD):
                        dve.wait_ge(S["s_hi"], (i - 1) * KD + m + 1)
                        dve.tensor_tensor(sT[:, 1, m, :], s_f[:, m, :], sT[:, 0, m, :], ALU.subtract)\
                            .then_inc(S["s_lo"], 1)
                if front:
                    r_tile(i, 1)
                if mid:
                    o_tile(i - 1, 0)
                if front:
                    r_tile(i, 2)
                if route and not mid:
                    h2_last(i - 2)
                if route:
                    top2(i - 2)
                if mid:
                    o_tile(i - 1, 1)
                if route:
                    slots(i - 2)
                if front:
                    r_tile(i, 3)
                if mid:
                    ln2_stats(i - 1, 0)
                    o_tile(i - 1, 2)
                if front:
                    ln_inner(i)
                if mid:
                    ln2_stats(i - 1, 1)
                    o_tile(i - 1, 3)
                    ln2_stats(i - 1, 2)

            dve.memset(conv_f, 0.0).then_inc(S["zeroed"], 1)
            dve.memset(hT[:, :, :, 0:PAD], 0.0)
            dve.memset(ones_f[:, :], 1.0)
            dve.memset(ones16[:, :], 1.0)
            dve.memset(mv_12[:, :, :], 1.0).then_inc(S["zeroed"], 1)
            dve.memset(bias_rows[:, :], 0.0).then_inc(S["zeroed"], 1)
            ln1_stats(0)
            dve.wait_ge(S["zeroed"], 3)
            ln12(-1, True, False)
            dve.wait_ge(S["cols_loaded"], 80)
            dve.tensor_scalar(g16[:, :], cols[:, 0:KI], WS, None, ALU.mult).then_inc(S["g16_ready"], 1)
            for k in range(KI):
                ins = dve.tensor_scalar(cpb_rep[:, k * 64:(k + 1) * 64], ones_f[:, 0:64],
                                        cols[:, 2 * KI + k:2 * KI + k + 1], None, ALU.mult)
            ins.then_inc(S["cpb_ready"], 1)
            dve.wait_ge(S["modT_ps"], 1)
            modT = bank[4][:, 0:4 * NB].rearrange("p (s k b) -> p s k b", s=2, k=KD)
            dve.tensor_copy(shiftT[:, :, :], modT[:, 0]).then_inc(S["modT_read"], 1)
            dve.tensor_scalar(scaleT[:, :, :], modT[:, 1], 1.0, None, ALU.add).then_inc(S["modT_read"], 1)
            split_lo(in_w[:, 1, :], in_f, in_w[:, 0, :], 1)
            dve.nop()
            dve.drain().then_inc(S["w_lo"], 1)
            split_lo(conv_w[:, 1, :], conv_f, conv_w[:, 0, :], 2)
            split_lo(bias_lo[:, 0:INNER], convb_f[0:64, :], bias_hi[:, 0:INNER], 3)
            dve.drain().then_inc(S["w_lo"], 1)
            dve.wait_ge(S["w_lo"], 2)
            dve.tensor_copy(bias_rows[0:1, 0:INNER], bias_hi[0:1, 0:INNER])
            dve.tensor_copy(bias_rows[32:33, 0:INNER], bias_lo[32:33, 0:INNER]).then_inc(S["w_lo"], 1)

            dve.wait_ge(S["modrow_ps"], 1)
            c = 0

            def do(ins):
                nonlocal c
                c += 1
                ins.then_inc(S["modrow_step"], 1)
                dve.wait_ge(S["modrow_step"], c)

            do(dve.tensor_copy(mtmp[:, 0, :], bank[5][0:NB, 0:D]))
            do(dve.tensor_copy(modrow[:, 2, :], bank[5][0:NB, D:2 * D]))
            do(dve.tensor_scalar(modrow[:, 1, :], bank[3][0:NB, 0:D], 1.0, None, ALU.add))
            do(dve.tensor_copy(mtmp[:, 1, :], bank[3][0:NB, D:2 * D]))
            gates = mtmp[:, 0:2, :]
            work = mtmp[:, 2:4, :]
            do(dve.scalar_tensor_tensor(out=work, in0=gates, scalar=-1.0, in1=gates, op0=ALU.mult, op1=ALU.max))
            do(dve.tensor_scalar(work, work, GATE_MIN, None, ALU.max))
            do(dve.tensor_scalar(gates, gates, 0.0, 2.0, ALU.is_ge, ALU.mult))
            do(dve.scalar_tensor_tensor(out=gates, in0=gates, scalar=-1.0, in1=work, op0=ALU.add, op1=ALU.mult))
            do(dve.tensor_scalar(modrow[:, 0, :], mtmp[:, 0, :], 1 / WS, None, ALU.mult))
            dve.wait_ge(S["rows_loaded"], 48)
            do(dve.tensor_tensor(modrow[:, 4, :], mtmp[:, 1, :], gb_row[:, 0, :], ALU.mult))
            do(dve.tensor_tensor(modrow[:, 3, :], mtmp[:, 1, :], gb_row[:, 1, :], ALU.mult))
            dve.nop().then_inc(S["modrow_done"], 1)

            for k in range(KI):
                split_lo(fc_w[:, 1, k * D:(k + 1) * D], fc_f[:, k * D:(k + 1) * D],
                         fc_w[:, 0, k * D:(k + 1) * D], 4, g16[:, k:k + 1])
            dve.wait_ge(S["fb_ps"], 1)
            dve.tensor_tensor(fc_bias[:, :], bank[2][:, 0:KD], cols[:, 3 * KI:3 * KI + KD], ALU.add)
            dve.drain().then_inc(S["w_lo"], 1)
            split_lo(out_w[:, 1, :], out_f, out_w[:, 0, :], 5)
            split_lo(comp_w[:, 1, :], bank[1][:, :], comp_w[:, 0, :], 6)
            split_lo(bias_lo[:, INNER:], bank[0][0:64, D:2 * D], bias_hi[:, INNER:], 7)
            dve.tensor_copy(colsum[:, :], bank[0][:, 0:D])
            dve.drain().then_inc(S["w_lo"], 1)
            dve.wait_ge(S["w_lo"], 5)
            dve.tensor_copy(bias_rows[0:1, INNER:], bias_hi[0:1, INNER:])
            dve.tensor_copy(bias_rows[32:33, INNER:], bias_lo[32:33, INNER:]).then_inc(S["w_lo"], 1)
            dve.wait_ge(S["base_ready"], 1)
            dve.wait_ge(S["router_loaded"], 16 * (1 + SUB))

            run(dve, body)

            c2 = 0

            def do2(ins):
                nonlocal c2
                c2 += 1
                ins.then_inc(S["table_step"], 1)
                dve.wait_ge(S["table_step"], c2)

            do2(dve.tensor_copy(tab_end[:, :], base[:, :]))
            do2(dve.tensor_tensor(cnt[:, :], base[:, :], region0, ALU.subtract))
            do2(dve.tensor_scalar(cnt[:, :], cnt[:, :], float(T - 1), None, ALU.add))
            do2(dve.tensor_copy(cnt_i[:, :], cnt[:, :]))
            do2(dve.tensor_scalar(cnt_s[:, :], cnt_i[:, :], T.bit_length() - 1, None, ALU.logical_shift_right))
            do2(dve.tensor_copy(nt[:, :], cnt_s[:, :]))
            do2(dve.tensor_scalar(nt[:, :], nt[:, :], 1.0, None, ALU.max))
            do2(dve.memset(g0[:, 0:1], 0.0))
            for e in range(NE):
                do2(dve.tensor_tensor(g0[:, e + 1:e + 2], g0[:, e:e + 1], nt[:, e:e + 1], ALU.add))
            do2(dve.tensor_scalar(step[:, :], nt[:, :], -float(T), float(REGION), ALU.mult, ALU.add))
            do2(dve.tensor_scalar(row_f[:, :], tile_no, float(T), None, ALU.mult))
            for e in range(1, NE):
                do2(dve.tensor_scalar(row_t[:, :], tile_no, g0[:, e:e + 1], step[:, e - 1:e],
                                      ALU.is_ge, ALU.mult))
                do2(dve.tensor_tensor(row_f[:, :], row_f[:, :], row_t[:, :], ALU.add))
            do2(dve.tensor_scalar(row_t[:, :], tile_no, g0[:, NE:NE + 1], None, ALU.is_lt))
            do2(dve.tensor_tensor(row_f[:, :], row_f[:, :], row_t[:, :], ALU.mult))
            do2(dve.tensor_copy(tab_row[:, :], row_f[:, :]))
            do2(dve.tensor_copy(tab_nt[:, :], nt[:, :]))
            do2(dve.tensor_copy(tab_g0[:, :], g0[:, :]))
            dve.nop().then_inc(S["tables_ready"], 1)

            def w_split(n, buf):
                for q in range(WQ):
                    c = slice(q * (WE // WQ), (q + 1) * (WE // WQ))
                    dve.wait_ge(S["w_conv"], (n - 1) * WQ + q + 1)
                    dve.scalar_tensor_tensor(out=split_w[:, buf, 1, c], in0=stage_w[:, c], scalar=WS,
                                             in1=split_w[:, buf, 0, c], op0=ALU.mult, op1=ALU.subtract)\
                        .then_inc(S["w_ready"], 1)

            def xmT_lo(g):
                dve.wait_ge(S["xmT_hi"], g + 1)
                dve.tensor_tensor(xmT[:, 1, :, :].rearrange("p k t -> p (k t)"), bank[6][:, :],
                                  xmT[:, 0, :, :].rearrange("p k t -> p (k t)"), ALU.subtract)\
                    .then_inc(S["xmT_lo"], 1)

            dve.nop().then_inc(S["hm_lo"], 1)
            dve.nop().then_inc(S["yw_done"], 1)
            w_split(1, 0)
            xmT_lo(0)

            def expert(e, buf, has_next, has_after):
                first = dve.value_load(tab_g0[0:1, e:e + 1] if isinstance(e, int) else tab_g0[0:1, bass.ds(e, 1)],
                                       min_val=0, max_val=MAXT - 2)
                n = dve.value_load(tab_nt[0:1, e:e + 1] if isinstance(e, int) else tab_nt[0:1, bass.ds(e, 1)],
                                   min_val=1, max_val=MAXT - 2)
                with dve.Fori(0, n) as t:
                    g = dve.snap(first + t)
                    for q in range(KF // 2):
                        dve.wait_ge(S["hf_done"], g * KF + 2 * q + 3)
                        pair = hf[:, 2 * q:2 * q + 2, :]
                        dve.tensor_copy(hm[:, 0, 2 * q:2 * q + 2, :], pair).then_inc(S["hm_hi"], 1)
                        dve.wait_ge(S["hm_hi"], g * (KF // 2) + q + 1)
                        dve.tensor_tensor(hm[:, 1, 2 * q:2 * q + 2, :], pair, hm[:, 0, 2 * q:2 * q + 2, :],
                                          ALU.subtract).then_inc(S["hm_lo"], 1)
                    xmT_lo(g + 1)
                    if has_next:
                        with dve.If(t == 0):
                            w_split(e + 2, 1 - buf)
                    dve.wait_ge(S["b2w_done"], g + 1)
                    dve.wait_ge(S["rows_added"], g + 1)
                    dve.wait_ge(S["y_ps"], g + 2)
                    for j in range(TS):
                        dve.scalar_tensor_tensor(out=y_w[:, j, :], in0=bank[4 + j][:, 0:D],
                                                 scalar=wcur[:, j:j + 1], in1=b2w[:, j, :],
                                                 op0=ALU.mult, op1=ALU.add).then_inc(S["yw_done"], 1)

            expert_pairs(dve, expert)

            def stats(b):
                dve.wait_ge(FIN_LOADED[b], 16)
                for j in range(SUB):
                    dve.bn_stats(fin_st[:, b, j, :], fin_v[b][:, j, :]).then_inc(S["fin_step"], 1)
                for j in range(SUB):
                    dve.wait_ge(S["fin_step"], b * (2 * SUB) + j + 1)
                    dve.bn_aggr(fin_mv[:, b, j, :], fin_st[:, b, j, :]).then_inc(S["fin_step"], 1)
                dve.wait_ge(S["fin_step"], (b + 1) * (2 * SUB))
                dve.tensor_scalar(fin_mv[:, b, :, 1], fin_mv[:, b, :, 1], EPS, None, ALU.add)\
                    .then_inc(S["fin_var"], 1)

            def scale(b):
                dve.wait_ge(S["fin_sqrt"], b + 1)
                dve.reciprocal(fin_rstd[:, b, :], fin_std[:, b, :]).then_inc(S["fin_recip"], 1)
                dve.wait_ge(S["fin_recip"], b + 1)
                dve.scalar_tensor_tensor(out=fin_nbias[:, b, :], in0=fin_mv[:, b, :, 0], scalar=-1.0,
                                         in1=fin_rstd[:, b, :], op0=ALU.mult, op1=ALU.mult)\
                    .then_inc(S["fin_ready"], 1)

            def add(b):
                dve.wait_ge(S["fin_mul"], b + 1)
                if b == 0:
                    dve.wait_ge(S["fin_prefetched"], 16 * (NB + 1))
                dve.tensor_tensor(fin_x[b], fin_v[b], fin_x[b], ALU.add).then_inc(S["fin_sum"], 1)

            stats(0)
            for b in range(NB):
                if b + 1 < NB:
                    stats(b + 1)
                scale(b)
                if b >= 2:
                    add(b - 2)
            add(NB - 2)
            add(NB - 1)

        @block.tensor
        def _(pe):
            def win(hl, k, lo, n):
                return in_w[:, hl, k * 2 * INNER + lo:k * 2 * INNER + lo + n]

            def turn_x(b, chunks=range(KD)):
                for k in chunks:
                    if not (isinstance(b, int) and b == 0):
                        if isinstance(b, int) and b <= 1:
                            pe.wait_ge(S["xT_f32"], KD * b)
                        elif isinstance(b, int) and b == 2:
                            pe.wait_ge(S["hnT_lo"], SUB)
                        else:
                            pe.wait_ge(S["h2T_done"], (b - 3) * KD + k + 1)
                    if k == 0:
                        pe.wait_ge(S["xn_done"], b + 1)
                    for j in range(SUB):
                        mm = pe.transpose(bank[6 + k][:, j * P:(j + 1) * P], xn[:, j, k * P:(k + 1) * P],
                                          ident[:, :])
                    mm.then_inc(S["xT_ps"], 1)

            def proj_h(b, m):
                if m == 0:
                    pe.wait_ge(S["xT_lo"], (b + 1) * KD)
                if m < 2:
                    if isinstance(b, int) and b == 1:
                        pe.wait_ge(S["h_lo"], KI)
                    elif not (isinstance(b, int) and b == 0):
                        pe.wait_ge(S["s_f32"], (b - 2) * KD + m + 1)
                else:
                    pe.wait_ge(S["h_lo"], b * KI + m - 1)
                for k in range(KD):
                    mm = three(pe, bank[m % 2][:, :], (win(0, k, m * P, P), win(1, k, m * P, P)),
                               (xT[:, 0, k, :], xT[:, 1, k, :]), k == 0, k == KD - 1)
                mm.then_inc(S["h_ps"], 1)

            def proj_gate(b, j):
                if not (isinstance(b, int) and b * SUB + j == 0):
                    pe.wait_ge(S["gate_done"], b * SUB + j)
                t = slice(j * P, (j + 1) * P)
                for k in range(KD):
                    mm = three(pe, bank[2][:, :], (xT[:, 0, k, t], xT[:, 1, k, t]),
                               (win(0, k, INNER, INNER), win(1, k, INNER, INNER)), k == 0, k == KD - 1)
                mm.then_inc(S["gate_ps"], 1)

            def conv(b, j):
                if not (isinstance(b, int) and b * SUB + j == 0):
                    pe.wait_ge(S["r_done"], b * SUB + j)
                pe.matmul(bank[3][:, :], ones16[0:BIAS_K, :], bias_rows[0:BIAS_K, 0:INNER],
                          start=True, stop=False)
                for c in range(KI):
                    if j == 0:
                        pe.wait_ge(S["h_lo"], b * KI + c + 1)
                    for t in range(TAPS):
                        w = (c * TAPS + t) * P
                        tt = slice(j * P + t, j * P + t + P)
                        mm = three(pe, bank[3][:, c * P:(c + 1) * P], (hT[:, 0, c, tt], hT[:, 1, c, tt]),
                                   (conv_w[:, 0, w:w + P], conv_w[:, 1, w:w + P]), False,
                                   c == KI - 1 and t == TAPS - 1)
                mm.then_inc(S["conv_ps"], 1)

            def turn_hn(b, j, front):
                if j < 2:
                    if isinstance(b, int) and b == NB - 1:
                        pe.wait_ge(S["h2T_done"], (b - 1) * KD)
                    else:
                        pe.wait_ge(S["xT_f32"], (b + 1) * KD + j + 1)
                else:
                    pe.wait_ge(S["hnT_lo"], b * SUB + j - 1)
                pe.wait_ge(S["hn_done"], b * SUB + j + 1)
                for k in range(KI):
                    mm = pe.transpose(bank[6 + j % 2][:, k * P:(k + 1) * P], r_sb[:, j, k * P:(k + 1) * P],
                                      ident[:, :])
                mm.then_inc(S["hnT_ps"], 1)

            def fc(b, m, front):
                if m == 0:
                    pe.wait_ge(S["hnT_lo"], (b + 1) * SUB)
                if front:
                    pe.wait_ge(S["h_lo"], (b + 1) * KI + 3 + m)
                for k in range(KI):
                    w = k * D + m * P
                    mm = three(pe, bank[m][:, :], (fc_w[:, 0, w:w + P], fc_w[:, 1, w:w + P]),
                               (hnT[:, 0, k, :], hnT[:, 1, k, :]), k == 0, k == KI - 1)
                mm.then_inc(S["u_ps"], 1)

            def out_proj(b, j):
                if not (isinstance(b, int) and b * SUB + j == 0):
                    pe.wait_ge(S["t_done"], b * SUB + j)
                if j == 0:
                    pe.wait_ge(S["s_lo"], (b + 1) * KD)
                t = slice(j * P, (j + 1) * P)
                for k in range(KI):
                    three(pe, bank[5][:, 0:D], (hnT[:, 0, k, t], hnT[:, 1, k, t]),
                          (out_w[:, 0, k * D:(k + 1) * D], out_w[:, 1, k * D:(k + 1) * D]), k == 0, k == KI - 1)
                pe.matmul(bank[5][:, D:2 * D], ones16[0:BIAS_K, :], bias_rows[0:BIAS_K, INNER:],
                          start=True, stop=False)
                for k in range(KD):
                    mm = three(pe, bank[5][:, D:2 * D], (sT[:, 0, k, t], sT[:, 1, k, t]),
                               (comp_w[:, 0, k * D:(k + 1) * D], comp_w[:, 1, k * D:(k + 1) * D]),
                               False, k == KD - 1)
                mm.then_inc(S["o_ps"], 1)

            def turn_h2(b, mid):
                pe.wait_ge(S["row_done"], (b + 1) * SUB)
                for k in range(KD):
                    if mid:
                        pe.wait_ge(S["hnT_lo"], (b + 1) * SUB + 3 + k)
                    else:
                        pe.wait_ge(S["h2T_done"], b * KD)
                    for j in range(SUB):
                        mm = pe.transpose(bank[6 + k][:, j * P:(j + 1) * P], h2x[:, j, k * P:(k + 1) * P],
                                          ident[:, :])
                    mm.then_inc(S["h2T_ps"], 1)

            def logits(b):
                pe.wait_ge(S["h2T_done"], (b + 1) * KD)
                if not (isinstance(b, int) and b == 0):
                    pe.wait_ge(S["slots_done"], b)
                for j in range(SUB):
                    for k in range(KD):
                        mm = pe.matmul(bank[4][:, j * NE:(j + 1) * NE], h2T[:, k, j * P:(j + 1) * P],
                                       router_w[:, k, :], start=(k == 0), stop=(k == KD - 1))
                mm.then_inc(S["lg_ps"], 1)

            def ranks(b):
                pe.wait_ge(S["mask_done"], b + 1)
                R0 = SUB * NE
                pe.matmul(bank[4][:, R0:2 * R0], before[:, :], chosen[:, :, :].rearrange("p j e -> p (j e)"),
                          start=True, stop=False)
                for j in range(SUB - 1):
                    pe.matmul(bank[4][:, R0 + (j + 1) * NE:2 * R0], ones16[:, :],
                              chosen[:, j:j + 1, :].to_broadcast([P, SUB - 1 - j, NE]),
                              start=False, stop=(j == SUB - 2))
                for j in range(SUB):
                    mm = pe.matmul(bank[4][:, 2 * R0:2 * R0 + NE], ones16[:, :], chosen[:, j, :],
                                   start=(j == 0), stop=(j == SUB - 1))
                mm.then_inc(S["rank_ps"], 1)

            def body(i, front, mid, route, pre):
                if front:
                    proj_h(i, 0)
                    proj_h(i, 1)
                    proj_gate(i, 0)
                if mid:
                    turn_hn(i - 1, 0, front)
                    turn_hn(i - 1, 1, front)
                if front:
                    proj_h(i, 2)
                if mid:
                    turn_hn(i - 1, 2, front)
                if front:
                    proj_h(i, 3)
                if mid:
                    turn_hn(i - 1, 3, front)
                if front:
                    if isinstance(i, int) and i == 0:
                        pe.wait_ge(S["w_lo"], 3)
                    conv(i, 0)
                if mid:
                    if isinstance(i, int) and i == 1:
                        pe.wait_ge(S["w_lo"], 6)
                    fc(i - 1, 0, front)
                    fc(i - 1, 1, front)
                if front:
                    proj_gate(i, 1)
                    conv(i, 1)
                if mid:
                    out_proj(i - 1, 0)
                if route:
                    turn_h2(i - 2, mid)
                if front:
                    proj_gate(i, 2)
                    conv(i, 2)
                if route:
                    logits(i - 2)
                if mid:
                    out_proj(i - 1, 1)
                if front:
                    proj_gate(i, 3)
                if route:
                    ranks(i - 2)
                if pre:
                    turn_x(i + 1, range(KD - 1))
                if front:
                    conv(i, 3)
                if mid:
                    out_proj(i - 1, 2)
                if pre:
                    turn_x(i + 1, range(KD - 1, KD))
                if mid:
                    out_proj(i - 1, 3)

            pe.wait_ge(S["silu_c_done"], 1)
            pe.wait_ge(S["ident_ready"], 4)
            for s in range(2):
                for m in range(KD):
                    o = (s * KD + m) * NB
                    for k in range(KD):
                        w = k * 6 * D + s * D + m * P
                        mm = pe.matmul(bank[4][:, o:o + NB], wmod_f[:, w:w + P], silu_c[:, k * NB:(k + 1) * NB],
                                       start=(k == 0), stop=(k == KD - 1))
            mm.then_inc(S["modT_ps"], 1)
            for r, bk in ((0, 5), (1, 3)):
                for k in range(KD):
                    w = k * 6 * D + (2 + 2 * r) * D
                    mm = pe.matmul(bank[bk][0:NB, 0:2 * D], silu_c[:, k * NB:(k + 1) * NB], wmod_f[:, w:w + 2 * D],
                                   start=(k == 0), stop=(k == KD - 1))
            mm.then_inc(S["modrow_ps"], 1)
            turn_x(0)
            pe.wait_ge(S["out_loaded"], 16)
            pe.wait_ge(S["cpb_ready"], 1)
            for k in range(KI):
                pe.matmul(bank[0][:, 0:D], ones_f[:, :], out_f[:, k * D:(k + 1) * D], start=(k == 0), stop=(k == KI - 1))
            for k in range(KI):
                mm = pe.matmul(bank[0][0:64, D:2 * D], cpb_rep[:, k * 64:(k + 1) * 64], out_f[:, k * D:(k + 1) * D],
                               start=(k == 0), stop=(k == KI - 1))
            mm.then_inc(S["colsum_ps"], 1)
            pe.wait_ge(S["cproj_loaded"], 16)
            for m in range(KD):
                for k in range(KI):
                    w = k * D + m * P
                    mm = pe.matmul(bank[1][:, m * D:(m + 1) * D], cproj_f[:, w:w + P], out_f[:, k * D:(k + 1) * D],
                                   start=(k == 0), stop=(k == KI - 1))
            mm.then_inc(S["comp_ps"], 1)
            pe.wait_ge(S["fc_loaded"], 16)
            for m in range(KD):
                for k in range(KI):
                    w = k * D + m * P
                    mm = pe.matmul(bank[2][:, m:m + 1], fc_f[:, w:w + P], cols[:, KI + k:KI + k + 1],
                                   start=(k == 0), stop=(k == KI - 1))
            mm.then_inc(S["fb_ps"], 1)
            pe.wait_ge(S["w_lo"], 6)
            pe.wait_ge(S["modrow_done"], 1)
            run(pe, body)

            def turn_m(g):
                pe.wait_ge(S["xm_loaded"], (g + 1) * 16)
                for j in range(TS):
                    for k in range(KD):
                        o = k * T + j * P
                        mm = pe.transpose(bank[6][:, o:o + P], xm[:, j, k * P:(k + 1) * P], ident[:, :])
                mm.then_inc(S["xmT_ps"], 1)

            pe.nop().then_inc(S["y_ps"], 1)
            pe.wait_ge(S["tables_ready"], 1)
            turn_m(0)

            def expert(e, buf, has_next, has_after):
                first = pe.value_load(tab_g0[0:1, e:e + 1] if isinstance(e, int) else tab_g0[0:1, bass.ds(e, 1)],
                                      min_val=0, max_val=MAXT - 2)
                n = pe.value_load(tab_nt[0:1, e:e + 1] if isinstance(e, int) else tab_nt[0:1, bass.ds(e, 1)],
                                  min_val=1, max_val=MAXT - 2)
                wait_alone(pe, S["w_ready"], (e + 1) * WQ)

                def w1(hl, k, c):
                    o = k * FF + c * P
                    return split_w[:, buf, hl, o:o + P]

                def w2(hl, c):
                    o = KD * FF + c * D
                    return split_w[:, buf, hl, o:o + D]

                with pe.Fori(0, n) as t:
                    g = pe.snap(first + t)
                    pe.wait_ge(S["xmT_lo"], g + 1)
                    for c in range(KF):
                        if c == 0:
                            pe.wait_ge(S["hf_done"], g * KF + 1)
                        for k in range(KD):
                            mm = three(pe, bank[c // 2][:, (c % 2) * T:(c % 2 + 1) * T],
                                       (w1(0, k, c), w1(1, k, c)), (xmT[:, 0, k, :], xmT[:, 1, k, :]),
                                       k == 0, k == KD - 1)
                        if c % 2 == 1:
                            mm.then_inc(S["l1_ps"], 1)
                    turn_m(g + 1)
                    pe.wait_ge(S["yw_done"], g * TS + 1)
                    for c in range(KF):
                        pe.wait_ge(S["hm_lo"], g * (KF // 2) + c // 2 + 2)
                        for j in range(TS):
                            mm = three(pe, bank[4 + j][:, 0:D],
                                       (hm[:, 0, c, j * P:(j + 1) * P], hm[:, 1, c, j * P:(j + 1) * P]),
                                       (w2(0, c), w2(1, c)), c == 0, c == KF - 1)
                    mm.then_inc(S["y_ps"], 1)

            expert_pairs(pe, expert)


_LAYOUT = {
    "x": lambda d: d["L0_attn_hidden_states"],
    "in_wT": lambda d: d["L0_attn_in_proj_w"].T,
    "convT": lambda d: d["L0_attn_conv_w"].reshape(4, 2, 64, 64, 4).transpose(0, 1, 3, 4, 2),
    "conv_b": lambda d: d["L0_attn_conv_b"],
    "ln_g": lambda d: d["L0_attn_ln_g"].reshape(-1, 128).T,
    "ln_b": lambda d: d["L0_attn_ln_b"].reshape(-1, 128).T,
    "fcT": lambda d: d["L0_attn_fc_w"].T,
    "fc_b": lambda d: d["L0_attn_fc_b"].reshape(-1, 128).T,
    "cproj": lambda d: d["L0_attn_cproj_w"],
    "cproj_b": lambda d: d["L0_attn_cproj_b"].reshape(-1, 128).T,
    "outT": lambda d: d["L0_attn_out_w"].T,
    "WrT": lambda d: d["L0_ffn_Wr"].T,
    "br": lambda d: d["L0_ffn_br"],
    "W1T": lambda d: d["L0_ffn_W1"].transpose(0, 2, 1),
    "b1": lambda d: d["L0_ffn_b1"].reshape(-1, 128).T,
    "W2T": lambda d: d["L0_ffn_W2"].transpose(0, 2, 1),
    "b2": lambda d: d["L0_ffn_b2"].reshape(-1),
    "gamma": lambda d: d["L0_ffn_gamma"],
    "beta": lambda d: d["L0_ffn_beta"],
    "cT": lambda d: d["L0_c"].T.reshape(2, 128, 8).transpose(1, 0, 2).reshape(128, 16),
    "wmod": lambda d: d["L0_wmod"],
}


def kernel(**inputs):
    import numpy as np
    import concourse.bacc as bacc
    from concourse.bass_utils import run_bass_kernel_spmd

    nc = bacc.Bacc("TRN2", target_bir_lowering=False, num_devices=1)
    arrays, args = {}, {}
    for name, lay in _LAYOUT.items():
        a = np.ascontiguousarray(lay({k: np.asarray(v) for k, v in inputs.items()}))
        arrays[f"in_{name}"] = a
        args[name] = nc.dram_tensor(f"in_{name}", a.shape, F32, kind="ExternalInput").ap()
    shape = tuple(inputs["L0_attn_hidden_states"].shape)
    args["out"] = nc.dram_tensor("out_x", shape, F32, kind="ExternalOutput").ap()
    adaln_kernel(nc, **args)
    r = run_bass_kernel_spmd(nc, [arrays], core_ids=[0])
    return r.results[0]["out_x"]
```

```python
from contextlib import ExitStack

import concourse.bass as bass
from concourse import mybir

F32 = mybir.dt.float32
F16 = mybir.dt.float16
I32 = mybir.dt.int32
U32 = mybir.dt.uint32
ALU = mybir.AluOpType
ACT = mybir.ActivationFunctionType
AX = mybir.AxisListType.X

P = 128
EPS = 1e-5
WS = 16.0
GATE_MIN = 0.25
RSQRT_MAGIC = float(0x5F3759DF)
NEWTON = 3
MASKED = -3.0e38


def adaln_kernel(nc, x, in_wT, convT, conv_b, ln_g, ln_b, fcT, fc_b, cproj, cproj_b, outT,
                 WrT, br, W1T, b1, W2T, b2, gamma, beta, cT, wmod, out):
    NB, SEQ, D = x.shape
    INNER = outT.shape[0]
    NE, _, FF = W1T.shape
    TAPS = convT.shape[3]
    G = convT.shape[2]
    KD, KI, KF, SUB = D // P, INNER // P, FF // P, SEQ // P
    PAD = TAPS - 1
    TOKENS = NB * SEQ
    T = 256
    TS = T // P
    REGION = TOKENS + T
    MAXT = 48
    assert 2 * TOKENS // T + NE < MAXT and KF * T == SUB * INNER
    C_ID, C_W, RW = D, D + 1, D + 8
    WE = KD * FF + KF * D
    WQ = 4
    BIAS_K = 33

    gathered = nc.dram_tensor("expert_lists", (NE * REGION, RW), F32, kind="Internal").ap()
    moe_acc = nc.dram_tensor("moe_sum", (TOKENS + T, D), F32, kind="Internal").ap()
    modd = nc.dram_tensor("modulation_rows", (NB, 5, D), F32, kind="Internal").ap()

    with ExitStack() as ctx:
        def sb(name, shape, dt=F32):
            return ctx.enter_context(nc.sbuf_tensor(name, shape, dt))

        def sem(name):
            return ctx.enter_context(nc.semaphore(name))

        bank = [ctx.enter_context(nc.psum_tensor(f"bank{i}", [P, 512], F32)) for i in range(8)]

        pool_f = sb("weight_pool", [P, WE + 2 * WE])
        at = 0

        def part(n):
            nonlocal at
            at += n
            return pool_f[:, at - n:at]

        in_f = part(KD * 2 * INNER)
        conv_f = part(KI * TAPS * P)
        fc_f = part(KI * D)
        out_f = part(KI * D)
        cproj_f = part(KI * D)
        wmod_f = part(KD * 6 * D)
        convb_f = part(INNER)
        cpb_rep = part(KI * 64)
        assert at <= 3 * WE
        stage_w = pool_f[:, 0:WE]
        split_w = pool_f[:, WE:3 * WE].bitcast(F16).rearrange("p (b h n) -> p b h n", b=2, h=2)

        in_w = sb("in_w", [P, 2, KD * 2 * INNER], F16)
        conv_w = sb("conv_w", [P, 2, KI * TAPS * P], F16)
        fc_w = sb("fc_w", [P, 2, KI * D], F16)
        out_w = sb("out_w", [P, 2, KI * D], F16)
        comp_w = sb("comp_w", [P, 2, KD * D], F16)
        bias_rows = sb("bias_rows", [64, INNER + D], F16)
        bias_hi = sb("bias_hi", [64, INNER + D], F16)
        bias_lo = sb("bias_lo", [64, INNER + D], F16)
        router_w = sb("router_w", [P, KD, NE])
        cols = sb("cols", [P, 3 * KI + KD])
        g16 = sb("g16", [P, KI])
        fc_bias = sb("fc_bias", [P, KD])
        b1c = sb("b1c", [P, NE * KF])
        b2r = sb("b2r", [P, NE, D])
        br4 = sb("br4", [P, SUB, NE])
        silu_c = sb("silu_c", [P, KD * NB])
        c_sb = sb("c_sb", [P, KD * NB])
        shiftT = sb("shiftT", [P, KD, NB])
        scaleT = sb("scaleT", [P, KD, NB])
        modrow = sb("modrow", [NB, 5, D])
        mtmp = sb("mtmp", [NB, 4, D])
        gb_row = sb("gamma_beta", [NB, 2, D])
        colsum = sb("colsum", [P, D])

        ident = sb("ident", [P, P])
        ones_f = sb("ones_f", [P, P])
        ones16 = sb("ones16", [P, P], F16)
        before = sb("before", [P, P], F16)
        iota_i = sb("iota_i", [P, SUB * NE + NE + SUB + TS], I32)
        iota_f = sb("iota_f", [P, SUB * NE + NE + SUB + TS])
        rev = iota_f[:, 0:SUB * NE].rearrange("p (j e) -> p j e", j=SUB)
        region0 = iota_f[:, SUB * NE:SUB * NE + NE]
        token0 = iota_f[:, SUB * NE + NE:SUB * NE + NE + SUB]
        fill_id = iota_f[:, SUB * NE + NE + SUB:]
        filler = sb("filler", [P, TS, RW])

        xa = sb("xa", [P, SUB, D])
        xr = sb("xr", [P, SUB, D])
        xn = sb("xn", [P, SUB, D])
        xT_f = sb("xT_f", [P, KD, SEQ])
        xT = sb("xT", [P, 2, KD, SEQ], F16)
        hT_all = sb("hT", [P, 2 * KI * (PAD + SEQ)], F16)
        hT = hT_all[:, :].rearrange("p (h k n) -> p h k n", h=2, k=KI)
        gate_sb = sb("gate_sb", [P, INNER])
        r_sb = sb("r_sb", [P, SUB, INNER])
        hnT = sb("hnT", [P, 2, KI, SEQ], F16)
        s_f = sb("s_f", [P, KD, SEQ])
        sT = sb("sT", [P, 2, KD, SEQ], F16)
        tmp = sb("tmp", [P, SUB, D])
        x1 = sb("x1", [P, SUB, D])
        xn2 = sb("xn2", [P, SUB, D])
        x1p = sb("x1p", [P, SUB, D])
        h2x = sb("h2x", [P, SUB, RW])
        h2T = sb("h2T", [P, KD, SEQ])
        h2x_last = r_sb[:, :, 0:RW]
        ga_row = sb("ga_row", [P, D])
        rt_row = sb("rt_row", [P, 3, D])
        st_in = sb("bn_inner", [P, SUB, 6])
        mv_in = sb("mv_inner", [P, SUB, 2])
        nw_in = sb("newton_inner", [P, 4, SUB])
        rstd_in = sb("rstd_inner", [P, SUB])
        nbias_in = sb("nbias_inner", [P, SUB])
        st_12 = sb("bn_12", [P, 2, SUB, 6])
        mv_12 = sb("mv_12", [P, 2 * SUB, 2])
        nw_12 = sb("newton_12", [P, 4, 2 * SUB])
        rstd_12 = sb("rstd_12", [P, 2 * SUB])
        nbias_12 = sb("nbias_12", [P, 2 * SUB])
        std = sb("std", [P, SUB])
        m16 = sb("m16", [P, SUB])
        lg = sb("lg", [P, SUB, NE])
        lg2 = sb("lg2", [P, SUB, NE])
        eq = sb("eq", [P, SUB, NE])
        sc = sb("sc", [P, SUB, NE])
        top = sb("top", [P, 4, SUB])
        onehot = sb("onehot", [P, 2, SUB, NE])
        chosen = sb("chosen", [P, SUB, NE], F16)
        rank = sb("rank", [P, SUB, NE])
        pick = sb("pick", [P, 2, SUB, NE])
        slot_f = sb("slot_f", [P, 2, SUB])
        slot_u = sb("slot_u", [P, 2, SUB], U32)
        dlt = sb("dlt", [P, SUB])
        weights = sb("weights", [P, 2, SUB])
        base = sb("base", [P, NE])
        ids = sb("ids", [P, SUB])
        cnt = sb("cnt", [P, NE])
        cnt_i = sb("cnt_i", [P, NE], I32)
        cnt_s = sb("cnt_s", [P, NE], I32)
        nt = sb("nt", [P, NE])
        g0 = sb("g0", [P, NE + 1])
        tab_nt = sb("tab_nt", [P, NE], I32)
        tab_g0 = sb("tab_g0", [P, NE + 1], I32)
        tab_fill = sb("tab_fill", [P, NE], I32)
        xm = sb("xm", [P, TS, RW])
        xmT = sb("xmT", [P, 2, KD, T], F16)
        hf = r_sb[:, :, :].rearrange("p j (a t) -> p (j a) t", t=T)
        hm = hnT[:, :, :, :].rearrange("p h k (a t) -> p h (k a) t", t=T)
        meta = sb("meta", [P, TS, 2])
        wcur = sb("wcur", [P, TS])
        idcur = sb("idcur", [P, TS], U32)
        b2w = sb("b2w", [P, TS, D])
        y_w = sb("y_w", [P, TS, D])

        fin_v = [t.rearrange("p (j d) -> p j d", j=SUB) for t in (
            s_f[:, :, :].rearrange("p k n -> p (k n)"), h2T[:, :, :].rearrange("p k n -> p (k n)"),
            *(in_w[:, h, :].bitcast(F32) for h in range(2)), *(conv_w[:, h, :].bitcast(F32) for h in range(2)),
            fc_w[:, :, :].rearrange("p h n -> p (h n)").bitcast(F32),
            out_w[:, :, :].rearrange("p h n -> p (h n)").bitcast(F32))]
        fin_g = hT_all[:, 0:2 * NB * D].bitcast(F32).rearrange("p (b d) -> p b d", b=NB)
        GATED_BY_POOL = (0, 2, 4, 5)
        fin_std = sb("fin_std", [P, NB, SUB])
        fin_rstd = sb("fin_rstd", [P, NB, SUB])
        fin_nbias = sb("fin_nbias", [P, NB, SUB])
        fin_st = sb("fin_st", [P, NB, SUB, 6])
        fin_mv = sb("fin_mv", [P, NB, SUB, 2])

        names = """
        zeroed ident_ready consts_ready iota_ready iota_conv cond_loaded wmod_first_loaded
        wmod_rest_loaded cols_loaded in_loaded conv_loaded fc_loaded out_loaded cproj_loaded
        rows_loaded router_loaded g16_ready cpb_ready silu_c_done modT_ps modT_read modrow_ps
        modrow_step modrow_done mod_stored colsum_ps fb_ps comp_ps w_hi w_lo xa_loaded ln1_step
        ln2_step ln_aggr ln_step ln_ready xn_done xT_ps xT_f32 xT_hi xT_lo h_ps h_hi h_lo
        gate_ps gate_done conv_ps r_done bn_in_step lnin_step lnin_ready hn_done hnT_ps hnT_hi
        hnT_lo u_ps s_f32 s_hi s_lo o_ps o_step t_done xr_loaded ga_loaded x1_step x1_done
        xn2_done rt_loaded h2_step h2_last_step x1p_done row_done row_stored h2T_ps h2T_done
        lg_ps mask_step mask_done weights_done rank_ps slot_step slots_done fill_rows_ready
        payload_copy payload scattered base_ready table_step tables_ready filled xm_loaded
        xmT_ps xmT_hi xmT_lo w_loaded w_conv w_ready b2_loaded l1_ps hf_done hm_hi hm_lo y_ps
        meta_done meta_used b2_scaled b2w_done yw_done acc_added rows_added wait_passed
        acc_filled fin_g_loaded fin_step fin_var fin_sqrt fin_recip fin_norm fin_ready fin_mul
        fin_mul_pool out_added
        """.split()
        S = {n: sem(n) for n in names}
        FIN_LOADED = [sem(f"fin_loaded_{b}") for b in range(NB)]

        def rows_of(t, b):
            if isinstance(b, int):
                return t[b * SEQ:(b + 1) * SEQ, :].rearrange("(j p) d -> p j d", p=P)
            return t[bass.ds(b * SEQ, SEQ), :].rearrange("(j p) d -> p j d", p=P)

        def fin_rows(t, b):
            return t[b * SEQ:(b + 1) * SEQ, :].rearrange("(p j) d -> p j d", j=SUB)

        x_rows = x.rearrange("b s d -> (b s) d")
        out_rows = out.rearrange("b s d -> (b s) d")

        def mod_bc(b, lo, hi):
            src = modd[b:b + 1, lo:hi, :] if isinstance(b, int) else modd[bass.ds(b, 1), lo:hi, :]
            return src.rearrange("a r d -> a (r d)").partition_broadcast(P)

        def col(t, b):
            return t[:, b:b + 1] if isinstance(b, int) else t[:, bass.ds(b, 1)]

        def three(pe, ps, stat, mov, first, last, lo_first=False):
            sh, sl = stat
            mh, ml = mov
            pe.matmul(ps, sh, mh, start=first, stop=False)
            pe.matmul(ps, sh, ml, start=False, stop=False)
            return pe.matmul(ps, sl, mh, start=False, stop=last)

        block = ctx.enter_context(nc.Block())

        STAGES = [(i, 0 <= i < NB, 0 <= i - 1 < NB, 0 <= i - 2 < NB, i + 1 < NB)
                  for i in range(NB + 2)]

        def run(eng, body):
            full = [s[0] for s in STAGES if all(s[1:]) and s[0] > 2]
            for s in STAGES:
                if s[0] == full[0]:
                    with eng.Fori(full[0], full[-1] + 1) as i:
                        body(i, True, True, True, True)
                elif s[0] not in full:
                    body(*s)

        def load_w(eng, e):
            w1, w2 = (W1T[e:e + 1], W2T[e:e + 1]) if isinstance(e, int) else (W1T[bass.ds(e, 1)], W2T[bass.ds(e, 1)])
            eng.dma_start(stage_w[:, 0:KD * FF].rearrange("p (k n) -> p k n", k=KD),
                          w1.rearrange("a (k p) n -> p (a k) n", p=P)).then_inc(S["w_loaded"], 16)
            eng.dma_start(stage_w[:, KD * FF:WE].rearrange("p (k n) -> p k n", k=KF),
                          w2.rearrange("a (k p) n -> p (a k) n", p=P)).then_inc(S["w_loaded"], 16)

        def wait_alone(eng, semaphore, value):
            eng.wait_ge(semaphore, value)
            eng.nop().then_inc(S["wait_passed"], 1)

        def expert_pairs(eng, expert):
            with eng.Fori(0, NE // 2 - 1) as pair:
                expert(pair * 2, 0, True, True)
                expert(pair * 2 + 1, 1, True, True)
            expert(NE - 2, 0, True, False)
            expert(NE - 1, 1, False, False)

        @block.sync
        def _(sp):
            sp.dma_start(c_sb[:, :], cT).then_inc(S["cond_loaded"], 16)
            sp.dma_start(xa[:, :, :], rows_of(x_rows, 0)).then_inc(S["xa_loaded"], 16)
            wmod_to = wmod_f.rearrange("p (k n) -> p k n", k=KD)
            wmod_from = wmod.rearrange("(k p) n -> p k n", p=P)
            sp.dma_start(wmod_to[:, :, 0:2 * D], wmod_from[:, :, 0:2 * D]).then_inc(S["wmod_first_loaded"], 16)
            sp.dma_start(in_f.rearrange("p (k n) -> p k n", k=KD),
                         in_wT.rearrange("(k p) n -> p k n", p=P)).then_inc(S["in_loaded"], 16)
            sp.dma_start(wmod_to[:, :, 2 * D:], wmod_from[:, :, 2 * D:]).then_inc(S["wmod_rest_loaded"], 16)
            for n, (src, w) in enumerate([(ln_g, KI), (ln_b, KI), (cproj_b, KI), (fc_b, KD)]):
                sp.dma_start(cols[:, n * KI:n * KI + w], src).then_inc(S["cols_loaded"], 16)
            sp.dma_start(b1c[:, :], b1).then_inc(S["cols_loaded"], 16)
            sp.wait_ge(S["zeroed"], 1)
            for g in range(P // G):
                for c in range(KI):
                    dst = conv_f[g * G:(g + 1) * G, :].rearrange(
                        "p (c t m) -> p c t m", c=KI, t=TAPS)[:, c, :, g * G:(g + 1) * G]
                    sp.dma_start(dst, convT[c, g]).then_inc(S["conv_loaded"], 16)
            sp.dma_start(convb_f[0:64, :], conv_b.partition_broadcast(64)).then_inc(S["rows_loaded"], 16)
            for n, src in enumerate([gamma, beta]):
                sp.dma_start(gb_row[:, n, :], src.partition_broadcast(NB)).then_inc(S["rows_loaded"], 16)
            for dst, src, s in [(out_f, outT, "out_loaded"), (cproj_f, cproj, "cproj_loaded"),
                                (fc_f, fcT, "fc_loaded")]:
                sp.dma_start(dst.rearrange("p (k n) -> p k n", k=KI),
                             src.rearrange("(k p) n -> p k n", p=P)).then_inc(S[s], 16)
            sp.dma_start(router_w[:, :, :], WrT.rearrange("(k p) e -> p k e", p=P)).then_inc(S["router_loaded"], 16)
            for j in range(SUB):
                sp.dma_start(br4[:, j, :], br.partition_broadcast(P)).then_inc(S["router_loaded"], 16)
            sp.dma_start(b2r[:, :, :].rearrange("p e d -> p (e d)"),
                         b2.partition_broadcast(P)).then_inc(S["b2_loaded"], 16)
            sp.wait_ge(S["xn_done"], 1)
            sp.dma_start(xa[:, :, :], rows_of(x_rows, 1)).then_inc(S["xa_loaded"], 16)
            sp.wait_ge(S["modrow_done"], 1)
            sp.dma_start(modd, modrow[:, :, :]).then_inc(S["mod_stored"], 16)
            sp.wait_ge(S["mod_stored"], 16)
            sp.dma_start(rt_row[:, :, :].rearrange("p r d -> p (r d)"), mod_bc(0, 1, 4)).then_inc(S["rt_loaded"], 16)
            sp.wait_ge(S["consts_ready"], 3)
            sp.dma_start(moe_acc[TOKENS:TOKENS + T, :].rearrange("(p j) d -> p j d", j=TS),
                         filler[:, :, 0:D]).then_inc(S["acc_filled"], 16)

            def body(i, front, mid, route, pre):
                if mid:
                    if not (isinstance(i, int) and i == 1):
                        sp.wait_ge(S["x1_done"], (i - 1) * SUB)
                    sp.dma_start(xr[:, :, :], rows_of(x_rows, i - 1)).then_inc(S["xr_loaded"], 16)
                    sp.dma_start(ga_row[:, :], mod_bc(i - 1, 0, 1)).then_inc(S["ga_loaded"], 16)
                if pre and not (isinstance(i, int) and i == 0):
                    sp.wait_ge(S["xn_done"], i + 1)
                    sp.dma_start(xa[:, :, :], rows_of(x_rows, i + 1)).then_inc(S["xa_loaded"], 16)
                if route:
                    b = i - 2
                    sp.wait_ge(S["row_done"], b * SUB + SUB)
                    rows = h2x if mid else h2x_last
                    sp.dma_start(rows_of(moe_acc, b), rows[:, :, 0:D]).then_inc(S["row_stored"], 16)
                    sp.wait_ge(S["x1p_done"], b * SUB + SUB)
                    sp.dma_start(rows_of(out_rows, b), x1p[:, :, :]).then_inc(S["row_stored"], 16)
                    if not (isinstance(b, int) and b == NB - 1):
                        sp.dma_start(rt_row[:, :, :].rearrange("p r d -> p (r d)"),
                                     mod_bc(b + 1, 1, 4)).then_inc(S["rt_loaded"], 16)
                if isinstance(i, int) and i == NB:
                    load_w(sp, 0)
                    sp.wait_ge(S["fill_rows_ready"], 1)
                    for e in range(NE):
                        at = sp.value_load(tab_fill[0:1, e:e + 1], min_val=0, max_val=NE * REGION - SEQ - T)
                        for n in range(0, SEQ + T, T):
                            sp.dma_start(gathered[bass.ds(at + n, T), :].rearrange("(p j) c -> p j c", j=TS),
                                         filler[:, :, :]).then_inc(S["filled"], 16)

            run(sp, body)

            def load_tile(row):
                sp.dma_start(xm[:, :, :], gathered[bass.ds(row, T), :].rearrange("(p j) c -> p j c", j=TS))\
                  .then_inc(S["xm_loaded"], 16)

            def expert(e, buf, has_next, has_after):
                first = sp.value_load(tab_g0[0:1, e:e + 1] if isinstance(e, int) else tab_g0[0:1, bass.ds(e, 1)],
                                      min_val=0, max_val=MAXT - 2)
                n = sp.value_load(tab_nt[0:1, e:e + 1] if isinstance(e, int) else tab_nt[0:1, bass.ds(e, 1)],
                                  min_val=1, max_val=MAXT - 2)
                with sp.Fori(0, n) as t:
                    g = sp.snap(first + t)
                    sp.wait_ge(S["xmT_ps"], g + 1)
                    sp.wait_ge(S["meta_done"], g + 1)
                    load_tile(nc.s_assert_within(e * REGION + t * T, 0, NE * REGION - T))

            sp.wait_ge(S["tables_ready"], 1)
            sp.wait_ge(S["scattered"], 16 * 2 * SUB * NB)
            sp.wait_ge(S["row_stored"], 32 * NB)
            expert_pairs(sp, expert)
            total = sp.value_load(tab_g0[0:1, NE:NE + 1], min_val=1, max_val=MAXT - 2)
            sp.wait_ge(S["xmT_ps"], total + 1)
            sp.wait_ge(S["meta_done"], total + 1)
            load_tile(0)
            sp.dma_start(fin_g, modd[:, 4:5, :].rearrange("b r d -> r b d").partition_broadcast(P))\
                .then_inc(S["fin_g_loaded"], 16)
            wait_alone(sp, S["xm_loaded"], total * 16 + 16)
            sp.wait_ge(S["acc_added"], total * (16 * TS))
            for b in range(NB):
                sp.dma_start(fin_v[b], fin_rows(moe_acc, b)).then_inc(FIN_LOADED[b], 16)
            sp.wait_ge(S["out_added"], 16 * NB)
            sp.wait_ge(S["acc_filled"], 16)

        @block.gpsimd
        def _(pool):
            pool.memset(ident[:, :], 0.0).then_inc(S["ident_ready"], 1)
            pool.memset(before[:, :], 0.0).then_inc(S["ident_ready"], 1)
            pool.wait_ge(S["ident_ready"], 2)
            pool.affine_select(out=ident[:, :], in_=ident[:, :], compare_op=ALU.not_equal, fill=1.0,
                               base=0, pattern=[[-1, P]], channel_multiplier=1).then_inc(S["ident_ready"], 1)
            pool.affine_select(out=before[:, :], in_=before[:, :], compare_op=ALU.is_ge, fill=1.0,
                               base=0, pattern=[[-1, P]], channel_multiplier=1).then_inc(S["ident_ready"], 1)
            o = 0
            for pattern, base_, mult, n in [([[0, SUB], [-1, NE]], NE, 0, SUB * NE),
                                            ([[REGION, NE]], 0, 0, NE), ([[P, SUB]], 0, 1, SUB),
                                            ([[1, TS]], TOKENS, TS, TS)]:
                pool.iota(iota_i[:, o:o + n], pattern, base=base_, channel_multiplier=mult)\
                    .then_inc(S["iota_ready"], 1)
                o += n
            pool.wait_ge(S["iota_ready"], 4)
            pool.tensor_copy(iota_f[:, :], iota_i[:, :]).then_inc(S["iota_conv"], 1)
            pool.memset(filler[:, :, :], 0.0).then_inc(S["consts_ready"], 1)
            pool.memset(h2x[:, :, C_W + 1:RW], 0.0).then_inc(S["consts_ready"], 1)
            pool.wait_ge(S["consts_ready"], 2)
            pool.wait_ge(S["iota_conv"], 1)
            pool.tensor_copy(filler[:, :, C_ID], fill_id).then_inc(S["consts_ready"], 1)
            pool.tensor_copy(ids[:, :], token0).then_inc(S["consts_ready"], 1)
            pool.tensor_copy(base[:, :], region0).then_inc(S["base_ready"], 1)
            pool.wait_ge(S["consts_ready"], 4)

            def xT_lo(b):
                for k in range(KD):
                    pool.wait_ge(S["xT_hi"], b * KD + k + 1)
                    pool.tensor_tensor(xT[:, 1, k, :], xT_f[:, k, :], xT[:, 0, k, :], ALU.subtract)\
                        .then_inc(S["xT_lo"], 1)

            def x1_add(b, j):
                pool.wait_ge(S["t_done"], b * SUB + j + 1)
                if j == 0:
                    pool.wait_ge(S["ga_loaded"], (b + 1) * 16)
                    pool.wait_ge(S["xr_loaded"], (b + 1) * 16)
                    if not (isinstance(b, int) and b == 0):
                        pool.wait_ge(S["xn2_done"], b * SUB)
                        pool.wait_ge(S["x1p_done"], b * SUB)
                pool.tensor_tensor(tmp[:, j, :], tmp[:, j, :], ga_row[:, :], ALU.mult).then_inc(S["x1_step"], 1)
                pool.wait_ge(S["x1_step"], b * SUB + j + 1)
                pool.tensor_tensor(x1[:, j, :], tmp[:, j, :], xr[:, j, :], ALU.add).then_inc(S["x1_done"], 1)

            def payload(b, k, rows):
                if k == 0:
                    if not (isinstance(b, int) and b == 0):
                        wait_alone(pool, S["payload"], b * 5)
                    wait_alone(pool, S["slots_done"], b + 1)
                    wait_alone(pool, S["weights_done"], b + 1)
                pool.tensor_copy(rows[:, :, C_ID], ids[:, :]).then_inc(S["payload"], 1)
                pool.tensor_scalar(rows[:, :, C_W], weights[:, k, :], 1 / WS, None, ALU.mult)\
                    .then_inc(S["payload"], 1)

            def scatter(b, k, rows):
                wait_alone(pool, S["payload"], b * 5 + 2 * k + 2)
                for j in range(SUB):
                    pool.indirect_dma_start(
                        out=gathered, out_offset=bass.IndirectOffsetOnAxis(ap=slot_u[:, k, j:j + 1], axis=0),
                        in_=rows[:, j, :], in_offset=None).then_inc(S["scattered"], 16)

            def route_first(b):
                payload(b, 0, h2x)
                scatter(b, 0, h2x)

            def route_second(b):
                wait_alone(pool, S["scattered"], (b * 2 + 1) * (16 * SUB))
                payload(b, 1, h2x)
                scatter(b, 1, h2x)
                next_ids(b)

            def next_ids(b):
                wait_alone(pool, S["payload"], b * 5 + 4)
                pool.tensor_scalar(ids[:, :], ids[:, :], float(SEQ), None, ALU.add).then_inc(S["payload"], 1)

            def route_last(b):
                payload(b, 0, h2x_last)
                payload(b, 1, h2x)
                pool.wait_ge(S["payload_copy"], 1)
                pool.wait_ge(S["filled"], 16 * NE * (SEQ // T + 1))
                scatter(b, 0, h2x_last)
                scatter(b, 1, h2x)

            def body(i, front, mid, route, pre):
                if route:
                    b = i - 2
                    pool.wait_ge(S["rt_loaded"], (b + 1) * 16)
                    if not (isinstance(b, int) and b == 0):
                        pool.wait_ge(S["row_stored"], b * 32)
                        if mid:
                            pool.wait_ge(S["scattered"], b * (32 * SUB))
                    for j in range(SUB if mid else 0):
                        pool.wait_ge(S["xn2_done"], b * SUB + j + 1)
                        pool.tensor_tensor(h2x[:, j, 0:D], xn2[:, j, :], rt_row[:, 0, :], ALU.mult)\
                            .then_inc(S["h2_step"], 1)
                        pool.wait_ge(S["h2_step"], b * SUB + j + 1)
                        pool.tensor_tensor(h2x[:, j, 0:D], h2x[:, j, 0:D], rt_row[:, 1, :], ALU.add)\
                            .then_inc(S["row_done"], 1)
                    for j in range(SUB):
                        pool.tensor_tensor(x1p[:, j, :], x1[:, j, :], rt_row[:, 2, :], ALU.add)\
                            .then_inc(S["x1p_done"], 1)
                if mid:
                    x1_add(i - 1, 0)
                    x1_add(i - 1, 1)
                if route and mid:
                    route_first(i - 2)
                if pre:
                    xT_lo(i + 1)
                if mid:
                    x1_add(i - 1, 2)
                    x1_add(i - 1, 3)
                if route and mid:
                    route_second(i - 2)
                if route and not mid:
                    route_last(i - 2)

            xT_lo(0)
            pool.wait_ge(S["b2_loaded"], 16)
            pool.tensor_scalar(b2r[:, :, :], b2r[:, :, :], WS, None, ALU.mult).then_inc(S["b2_scaled"], 1)
            run(pool, body)

            pool.wait_ge(S["b2_scaled"], 1)
            pool.nop().then_inc(S["rows_added"], 1)
            pool.wait_ge(S["row_stored"], 32 * NB)
            pool.nop().then_inc(S["meta_done"], 1)
            pool.wait_ge(S["acc_filled"], 16)
            pool.wait_ge(S["tables_ready"], 1)

            def take_meta(g):
                wait_alone(pool, S["xm_loaded"], (g + 1) * 16)
                pool.tensor_copy(meta[:, :, :], xm[:, :, C_ID:C_W + 1]).then_inc(S["meta_done"], 1)

            take_meta(0)

            def expert(e, buf, has_next, has_after):
                first = pool.value_load(tab_g0[0:1, e:e + 1] if isinstance(e, int) else tab_g0[0:1, bass.ds(e, 1)],
                                        min_val=0, max_val=MAXT - 2)
                n = pool.value_load(tab_nt[0:1, e:e + 1] if isinstance(e, int) else tab_nt[0:1, bass.ds(e, 1)],
                                    min_val=1, max_val=MAXT - 2)
                b2e = b2r[:, e:e + 1, :] if isinstance(e, int) else b2r[:, bass.ds(e, 1), :]
                with pool.Fori(0, n) as t:
                    g = pool.snap(first + t)
                    wait_alone(pool, S["meta_done"], g + 2)
                    pool.tensor_copy(idcur[:, :], meta[:, :, 0]).then_inc(S["meta_used"], 1)
                    pool.tensor_copy(wcur[:, :], meta[:, :, 1]).then_inc(S["meta_used"], 1)
                    pool.wait_ge(S["meta_used"], g * 2 + 2)
                    pool.tensor_tensor(b2w[:, :, :], b2e.to_broadcast([P, TS, D]),
                                       wcur[:, :].unsqueeze(2).to_broadcast([P, TS, D]), ALU.mult)\
                        .then_inc(S["b2w_done"], 1)
                    take_meta(g + 1)
                    wait_alone(pool, S["yw_done"], g * TS + TS + 1)
                    for j in range(TS):
                        pool.indirect_dma_start(
                            out=moe_acc, out_offset=bass.IndirectOffsetOnAxis(ap=idcur[:, j:j + 1], axis=0),
                            in_=y_w[:, j, :], in_offset=None, compute_op=ALU.add).then_inc(S["acc_added"], 16)
                    pool.wait_ge(S["acc_added"], (g + 1) * (16 * TS))
                    pool.nop().then_inc(S["rows_added"], 1)

            expert_pairs(pool, expert)

            pool.wait_ge(S["fin_g_loaded"], 16)
            def add_out(b):
                pool.dma_start(fin_rows(out_rows, b), fin_v[b], accum_op=ALU.add).then_inc(S["out_added"], 16)

            for b in range(NB):
                if b in GATED_BY_POOL:
                    pool.wait_ge(S["fin_norm"], b + 1)
                    pool.tensor_tensor(fin_v[b], fin_v[b], fin_g[:, b:b + 1, :].to_broadcast([P, SUB, D]),
                                       ALU.mult).then_inc(S["fin_mul_pool"], 1)
                    pool.wait_ge(S["fin_mul_pool"], GATED_BY_POOL.index(b) + 1)
                else:
                    pool.wait_ge(S["fin_mul"], b + 1 - sum(a < b for a in GATED_BY_POOL))
                add_out(b)

        @block.scalar
        def _(act):
            def split_hi(dst, src, scale=WS):
                act.activation(dst, src, ACT.Copy, scale=scale).then_inc(S["w_hi"], 1)

            def xn_norm(b):
                act.wait_ge(S["ln_ready"], b + 1)
                if not (isinstance(b, int) and b == 0):
                    act.wait_ge(S["xT_ps"], b * KD)
                for j in range(SUB):
                    a = act.activation(xn[:, j, :], xa[:, j, :], ACT.Identity,
                                       bias=nbias_12[:, j:j + 1], scale=rstd_12[:, j:j + 1])
                a.then_inc(S["xn_done"], 1)

            def xT_split(b):
                for k in range(KD):
                    act.wait_ge(S["xT_ps"], b * KD + k + 1)
                    if k == 0 and not (isinstance(b, int) and b == 0):
                        act.wait_ge(S["xT_lo"], b * KD)
                    act.activation(xT_f[:, k, :], bank[6 + k][:, :], ACT.Identity,
                                   bias=col(shiftT[:, k, :], b), scale=col(scaleT[:, k, :], b))\
                        .then_inc(S["xT_f32"], 1)
                    act.wait_ge(S["xT_f32"], b * KD + k + 1)
                    act.activation(xT[:, 0, k, :], xT_f[:, k, :], ACT.Copy).then_inc(S["xT_hi"], 1)

            def h_hi(b, m):
                act.wait_ge(S["h_ps"], b * KI + m + 1)
                act.activation(hT[:, 0, m, PAD:], bank[m % 2][:, :], ACT.Copy, scale=1 / WS)\
                    .then_inc(S["h_hi"], 1)

            def gate(b, j):
                act.wait_ge(S["gate_ps"], b * SUB + j + 1)
                if not (isinstance(b, int) and b * SUB + j == 0):
                    act.wait_ge(S["r_done"], b * SUB + j)
                act.activation(gate_sb[:, :], bank[2][:, :], ACT.Silu, scale=1 / WS).then_inc(S["gate_done"], 1)

            def hnT_hi(b, j):
                act.wait_ge(S["hnT_ps"], b * SUB + j + 1)
                act.activation(hnT[:, 0, :, j * P:(j + 1) * P],
                               bank[6 + j % 2][:, :].rearrange("p (k t) -> p k t", k=KI), ACT.Copy)\
                    .then_inc(S["hnT_hi"], 1)

            def mixer_weights_hi():
                act.wait_ge(S["g16_ready"], 1)
                act.wait_ge(S["fc_loaded"], 16)
                for k in range(KI):
                    a = act.activation(fc_w[:, 0, k * D:(k + 1) * D], fc_f[:, k * D:(k + 1) * D], ACT.Copy,
                                       scale=g16[:, k:k + 1])
                a.then_inc(S["w_hi"], 1)
                act.wait_ge(S["out_loaded"], 16)
                split_hi(out_w[:, 0, :], out_f)
                act.wait_ge(S["comp_ps"], 1)
                split_hi(comp_w[:, 0, :], bank[5][:, :])
                act.wait_ge(S["colsum_ps"], 1)
                split_hi(bias_hi[:, INNER:], bank[4][0:64, D:2 * D])

            def body(i, front, mid, route, pre):
                if front:
                    h_hi(i, 0)
                    h_hi(i, 1)
                    gate(i, 0)
                if mid:
                    hnT_hi(i - 1, 0)
                    hnT_hi(i - 1, 1)
                if front:
                    h_hi(i, 2)
                if mid:
                    hnT_hi(i - 1, 2)
                if front:
                    h_hi(i, 3)
                if mid:
                    hnT_hi(i - 1, 3)
                if route:
                    b = i - 2
                    act.wait_ge(S["ln_ready"], b + 4)
                    if not (isinstance(b, int) and b == 0):
                        act.wait_ge(S["row_done"], b * SUB)
                    for j in range(SUB):
                        act.activation(xn2[:, j, :], x1[:, j, :], ACT.Identity,
                                       bias=nbias_12[:, SUB + j:SUB + j + 1],
                                       scale=rstd_12[:, SUB + j:SUB + j + 1])\
                            .then_inc(S["xn2_done"], 1)
                if mid:
                    b = i - 1
                    for m in range(KD):
                        act.wait_ge(S["u_ps"], b * KD + m + 1)
                        if m == 0 and not (isinstance(b, int) and b == 0):
                            act.wait_ge(S["s_lo"], b * KD)
                        act.activation(s_f[:, m, :], bank[m][:, :], ACT.Silu, bias=fc_bias[:, m:m + 1],
                                       scale=1 / WS).then_inc(S["s_f32"], 1)
                        act.wait_ge(S["s_f32"], b * KD + m + 1)
                        act.activation(sT[:, 0, m, :], s_f[:, m, :], ACT.Copy).then_inc(S["s_hi"], 1)
                if isinstance(i, int) and i == 0:
                    mixer_weights_hi()
                if front:
                    gate(i, 1)
                if route:
                    for k in range(KD):
                        act.wait_ge(S["h2T_ps"], (i - 2) * KD + k + 1)
                        act.activation(h2T[:, k, :], bank[6 + k][:, :], ACT.Copy).then_inc(S["h2T_done"], 1)
                if route and not mid:
                    act.wait_ge(S["row_done"], NB * SUB)
                    act.wait_ge(S["scattered"], (NB - 1) * (32 * SUB))
                    act.wait_ge(S["row_stored"], (NB - 1) * 32)
                    act.activation(h2x[:, :, 0:D], h2x_last[:, :, 0:D], ACT.Copy).then_inc(S["payload_copy"], 1)
                if pre:
                    xn_norm(i + 1)
                if front:
                    gate(i, 2)
                if front:
                    gate(i, 3)
                if route:
                    b = i - 2
                    act.wait_ge(S["mask_done"], b + 1)
                    if not (isinstance(b, int) and b == 0):
                        act.wait_ge(S["payload"], b * 5)
                    act.activation(weights[:, 0, :], dlt[:, :], ACT.Sigmoid, scale=-1.0)
                    act.activation(weights[:, 1, :], dlt[:, :], ACT.Sigmoid).then_inc(S["weights_done"], 1)
                if pre:
                    xT_split(i + 1)
                if front:
                    act.wait_ge(S["lnin_ready"], i + 1)
                    for j in range(SUB):
                        act.activation(r_sb[:, j, :], r_sb[:, j, :], ACT.Identity,
                                       bias=nbias_in[:, j:j + 1], scale=rstd_in[:, j:j + 1])\
                            .then_inc(S["hn_done"], 1)

            act.wait_ge(S["cond_loaded"], 16)
            act.activation(silu_c[:, :], c_sb[:, :], ACT.Silu).then_inc(S["silu_c_done"], 1)
            xn_norm(0)
            act.wait_ge(S["in_loaded"], 16)
            split_hi(in_w[:, 0, :], in_f)
            act.wait_ge(S["modT_read"], 2)
            xT_split(0)
            act.wait_ge(S["conv_loaded"], 16 * KI * (P // G))
            split_hi(conv_w[:, 0, :], conv_f)
            act.wait_ge(S["rows_loaded"], 48)
            split_hi(bias_hi[:, 0:INNER], convb_f[0:64, :])
            run(act, body)

            def w_split(n, buf):
                act.wait_ge(S["w_loaded"], n * 32)
                for q in range(WQ):
                    c = slice(q * (WE // WQ), (q + 1) * (WE // WQ))
                    act.activation(split_w[:, buf, 0, c], stage_w[:, c], ACT.Copy, scale=WS)\
                        .then_inc(S["w_conv"], 1)

            def xmT_hi(g):
                act.wait_ge(S["xmT_ps"], g + 2)
                act.activation(xmT[:, 0, :, :].rearrange("p k t -> p (k t)"), bank[6][:, :], ACT.Copy)\
                    .then_inc(S["xmT_hi"], 1)

            act.nop().then_inc(S["hf_done"], 1)
            w_split(1, 0)
            act.wait_ge(S["tables_ready"], 1)
            xmT_hi(0)
            act.wait_ge(S["w_ready"], WQ)
            load_w(act, 1)

            def expert(e, buf, has_next, has_after):
                first = act.value_load(tab_g0[0:1, e:e + 1] if isinstance(e, int) else tab_g0[0:1, bass.ds(e, 1)],
                                       min_val=0, max_val=MAXT - 2)
                n = act.value_load(tab_nt[0:1, e:e + 1] if isinstance(e, int) else tab_nt[0:1, bass.ds(e, 1)],
                                   min_val=1, max_val=MAXT - 2)
                with act.Fori(0, n) as t:
                    g = act.snap(first + t)
                    for c in range(KF):
                        if c % 2 == 0:
                            if c == 0:
                                act.wait_ge(S["hm_lo"], g * (KF // 2) + 1)
                            act.wait_ge(S["l1_ps"], g * (KF // 2) + c // 2 + 1)
                        act.activation(hf[:, c, :], bank[c // 2][:, (c % 2) * T:(c % 2 + 1) * T], ACT.Relu,
                                       bias=col(b1c, e * KF + c), scale=1 / WS).then_inc(S["hf_done"], 1)
                    xmT_hi(g + 1)
                    if has_next:
                        with act.If(t == 0):
                            act.wait_ge(S["y_ps"], first + 1)
                            w_split(e + 2, 1 - buf)
                    if has_after:
                        with act.If(t == 0):
                            act.wait_ge(S["w_ready"], (e + 2) * WQ)
                            load_w(act, e + 2)

            expert_pairs(act, expert)

            def norm(b):
                act.wait_ge(S["fin_ready"], b + 1)
                for j in range(SUB):
                    a = act.activation(fin_v[b][:, j, :], fin_v[b][:, j, :], ACT.Identity,
                                       bias=fin_nbias[:, b, j:j + 1], scale=fin_rstd[:, b, j:j + 1])
                a.then_inc(S["fin_norm"], 1)

            for b in range(NB):
                act.wait_ge(S["fin_var"], b + 1)
                act.activation(fin_std[:, b, :], fin_mv[:, b, :, 1], ACT.Sqrt).then_inc(S["fin_sqrt"], 1)
                if b >= 1:
                    norm(b - 1)
            norm(NB - 1)

        @block.vector
        def _(dve):
            def rsqrt(mv, nw, rstd, nbias, s, at):
                ve, y, a, yi = (nw[:, k, :] for k in range(4))
                var, mean = mv[:, :, 1], mv[:, :, 0]
                c = 0

                def do(ins, last=False):
                    nonlocal c
                    c += 1
                    ins.then_inc(S[s], 1)
                    if not last:
                        dve.wait_ge(S[s], at + c)

                do(dve.tensor_scalar(ve, var, EPS, None, ALU.add))
                do(dve.tensor_scalar(yi.bitcast(I32), ve.bitcast(I32), 1, None, ALU.logical_shift_right))
                do(dve.tensor_scalar(y.bitcast(I32), yi.bitcast(I32), -1.0, RSQRT_MAGIC, ALU.mult, ALU.add))
                for it in range(NEWTON):
                    do(dve.scalar_tensor_tensor(out=a, in0=y, scalar=-0.5, in1=y, op0=ALU.mult, op1=ALU.mult))
                    do(dve.tensor_tensor(a, a, ve, ALU.mult))
                    to = rstd[:, :] if it == NEWTON - 1 else y
                    do(dve.scalar_tensor_tensor(out=to, in0=a, scalar=1.5, in1=y, op0=ALU.add, op1=ALU.mult))
                do(dve.scalar_tensor_tensor(out=nbias[:, :], in0=mean, scalar=-1.0, in1=rstd[:, :],
                                            op0=ALU.mult, op1=ALU.mult))
                return c

            RSQRT_STEPS = 4 + 3 * NEWTON

            def ln1_stats(b):
                dve.wait_ge(S["xa_loaded"], (b + 1) * 16)
                for j in range(SUB):
                    dve.bn_stats(st_12[:, 0, j, :], xa[:, j, :]).then_inc(S["ln1_step"], 1)

            def ln2_stats(b, j):
                dve.wait_ge(S["x1_done"], b * SUB + j + 1)
                dve.bn_stats(st_12[:, 1, j, :], x1[:, j, :]).then_inc(S["ln2_step"], 1)

            def ln12(i, pre, route):
                if pre:
                    wait_alone(dve, S["ln1_step"], (i + 2) * SUB)
                    for j in range(SUB):
                        dve.bn_aggr(mv_12[:, j, :], st_12[:, 0, j, :]).then_inc(S["ln_aggr"], 1)
                if route:
                    wait_alone(dve, S["ln2_step"], (i - 1) * SUB)
                    for j in range(SUB):
                        dve.bn_aggr(mv_12[:, SUB + j, :], st_12[:, 1, j, :]).then_inc(S["ln_aggr"], 1)
                dve.wait_ge(S["ln_aggr"], (min(i + 2, NB) + max(i - 1, 0)) * SUB if isinstance(i, int)
                            else i * (2 * SUB) + SUB)
                if not (isinstance(i, int) and i < 0):
                    dve.wait_ge(S["xn_done"], min(i + 1, NB) if isinstance(i, int) else i + 1)
                if not (isinstance(i, int) and i <= 2):
                    dve.wait_ge(S["xn2_done"], (i - 2) * SUB)
                at = (i + 1) * RSQRT_STEPS
                rsqrt(mv_12, nw_12, rstd_12, nbias_12, "ln_step", at)
                dve.wait_ge(S["ln_step"], at + RSQRT_STEPS)
                dve.nop().then_inc(S["ln_ready"], 1)

            def split_lo(dst, src, hi, n, scale=WS):
                dve.wait_ge(S["w_hi"], n)
                dve.scalar_tensor_tensor(out=dst, in0=src, scalar=scale, in1=hi, op0=ALU.mult,
                                         op1=ALU.subtract)

            def h_lo(b, m):
                dve.wait_ge(S["h_hi"], b * KI + m + 1)
                dve.scalar_tensor_tensor(out=hT[:, 1, m, PAD:], in0=bank[m % 2][:, :], scalar=1 / WS,
                                         in1=hT[:, 0, m, PAD:], op0=ALU.mult, op1=ALU.subtract)\
                    .then_inc(S["h_lo"], 1)

            def hnT_lo(b, j):
                dve.wait_ge(S["hnT_hi"], b * SUB + j + 1)
                dve.tensor_tensor(hnT[:, 1, :, j * P:(j + 1) * P],
                                  bank[6 + j % 2][:, :].rearrange("p (k t) -> p k t", k=KI),
                                  hnT[:, 0, :, j * P:(j + 1) * P], ALU.subtract).then_inc(S["hnT_lo"], 1)

            def r_tile(b, j):
                dve.wait_ge(S["conv_ps"], b * SUB + j + 1)
                dve.wait_ge(S["gate_done"], b * SUB + j + 1)
                if not (isinstance(b, int) and b == 0):
                    dve.wait_ge(S["hnT_ps"], (b - 1) * SUB + j + 1)
                dve.scalar_tensor_tensor(out=r_sb[:, j, :], in0=bank[3][:, :], scalar=1 / WS, in1=gate_sb[:, :],
                                         op0=ALU.mult, op1=ALU.mult).then_inc(S["r_done"], 1)
                dve.wait_ge(S["r_done"], b * SUB + j + 1)
                dve.bn_stats(st_in[:, j, :], r_sb[:, j, :]).then_inc(S["bn_in_step"], 1)

            def ln_inner(b):
                wait_alone(dve, S["bn_in_step"], b * (2 * SUB) + SUB)
                for j in range(SUB):
                    dve.bn_aggr(mv_in[:, j, :], st_in[:, j, :]).then_inc(S["bn_in_step"], 1)
                dve.wait_ge(S["bn_in_step"], (b + 1) * (2 * SUB))
                if not (isinstance(b, int) and b == 0):
                    dve.wait_ge(S["hn_done"], b * SUB)
                at = b * RSQRT_STEPS
                rsqrt(mv_in, nw_in, rstd_in, nbias_in, "lnin_step", at)
                dve.wait_ge(S["lnin_step"], at + RSQRT_STEPS)
                dve.nop().then_inc(S["lnin_ready"], 1)

            def inner_stats(b):
                if not (isinstance(b, int) and b == 0):
                    dve.wait_ge(S["t_done"], b * SUB)
                dve.tensor_tensor(std[:, :], nw_in[:, 0, :], rstd_in[:, :], ALU.mult).then_inc(S["o_step"], 1)
                dve.tensor_scalar(m16[:, :], mv_in[:, :, 0], WS, None, ALU.mult).then_inc(S["o_step"], 1)

            def o_tile(b, j):
                if j == 0:
                    dve.wait_ge(S["o_step"], b * (2 + SUB) + 2)
                    if not (isinstance(b, int) and b == 0):
                        dve.wait_ge(S["x1_done"], b * SUB)
                dve.wait_ge(S["o_ps"], b * SUB + j + 1)
                dve.scalar_tensor_tensor(out=tmp[:, j, :], in0=colsum[:, :], scalar=m16[:, j:j + 1],
                                         in1=bank[5][:, D:2 * D], op0=ALU.mult, op1=ALU.add)\
                    .then_inc(S["o_step"], 1)
                dve.wait_ge(S["o_step"], b * (2 + SUB) + 3 + j)
                dve.scalar_tensor_tensor(out=tmp[:, j, :], in0=bank[5][:, 0:D], scalar=std[:, j:j + 1],
                                         in1=tmp[:, j, :], op0=ALU.mult, op1=ALU.add).then_inc(S["t_done"], 1)

            MASK_STEPS = 14

            def top2(b):
                c = 0

                def do(ins):
                    nonlocal c
                    c += 1
                    ins.then_inc(S["mask_step"], 1)
                    dve.wait_ge(S["mask_step"], b * MASK_STEPS + c)

                def bc(a):
                    return a.unsqueeze(2).to_broadcast([P, SUB, NE])

                dve.wait_ge(S["lg_ps"], b + 1)
                do(dve.tensor_tensor(lg[:, :, :], bank[4][:, 0:SUB * NE].rearrange("p (j e) -> p j e", j=SUB),
                                     br4[:, :, :], ALU.add))
                src = lg
                for k in range(2):
                    v, mx = top[:, k, :], top[:, 2 + k, :]
                    do(dve.tensor_reduce(v, src[:, :, :], AX, ALU.max))
                    do(dve.tensor_tensor(eq[:, :, :], src[:, :, :], bc(v), ALU.is_equal))
                    do(dve.tensor_tensor(sc[:, :, :], eq[:, :, :], rev, ALU.mult))
                    do(dve.tensor_reduce(mx, sc[:, :, :], AX, ALU.max))
                    do(dve.tensor_tensor(onehot[:, k, :, :], sc[:, :, :], bc(mx), ALU.is_equal))
                    if k == 0:
                        do(dve.scalar_tensor_tensor(out=lg2[:, :, :], in0=onehot[:, 0, :, :], scalar=MASKED,
                                                    in1=lg[:, :, :], op0=ALU.mult, op1=ALU.add))
                        src = lg2
                if not (isinstance(b, int) and b == 0):
                    dve.wait_ge(S["weights_done"], b)
                do(dve.tensor_tensor(dlt[:, :], top[:, 1, :], top[:, 0, :], ALU.subtract))
                do(dve.tensor_tensor(chosen[:, :, :], onehot[:, 0, :, :], onehot[:, 1, :, :], ALU.add))
                assert c == MASK_STEPS
                dve.nop().then_inc(S["mask_done"], 1)

            def h2_last(b):
                dve.wait_ge(S["rt_loaded"], (b + 1) * 16)
                for j in range(SUB):
                    dve.wait_ge(S["xn2_done"], b * SUB + j + 1)
                    dve.tensor_tensor(h2x_last[:, j, 0:D], xn2[:, j, :], rt_row[:, 0, :], ALU.mult)\
                        .then_inc(S["h2_last_step"], 1)
                for j in range(SUB):
                    dve.wait_ge(S["h2_last_step"], j + 1)
                    dve.tensor_tensor(h2x_last[:, j, 0:D], h2x_last[:, j, 0:D], rt_row[:, 1, :], ALU.add)\
                        .then_inc(S["row_done"], 1)

            def slots(b):
                c = 0

                def do(ins):
                    nonlocal c
                    c += 1
                    ins.then_inc(S["slot_step"], 1)
                    dve.wait_ge(S["slot_step"], b * 5 + c)

                dve.wait_ge(S["rank_ps"], b + 1)
                R0 = SUB * NE
                if isinstance(b, int) and b == NB - 1:
                    dve.wait_ge(S["fill_rows_ready"], 1)
                do(dve.tensor_tensor(rank[:, :, :], bank[4][:, R0:2 * R0].rearrange("p (j e) -> p j e", j=SUB),
                                     base[:, :].unsqueeze(1).to_broadcast([P, SUB, NE]), ALU.add))
                do(dve.tensor_tensor(base[:, :], bank[4][:, 2 * R0:2 * R0 + NE], base[:, :], ALU.add))
                if isinstance(b, int) and b == NB - 2:
                    dve.tensor_copy(tab_fill[:, :], base[:, :]).then_inc(S["fill_rows_ready"], 1)
                for k in range(2):
                    ins = dve.tensor_tensor(pick[:, k, :, :], onehot[:, k, :, :], rank[:, :, :], ALU.mult)
                do(ins)
                do(dve.tensor_reduce(slot_f[:, :, :], pick[:, :, :, :], AX, ALU.add))
                if not (isinstance(b, int) and b == 0):
                    dve.wait_ge(S["scattered"], b * (32 * SUB))
                do(dve.tensor_copy(slot_u[:, :, :], slot_f[:, :, :]))
                dve.nop().then_inc(S["slots_done"], 1)

            row_steps = 0

            def do_row(ins):
                nonlocal row_steps
                row_steps += 1
                ins.then_inc(S["modrow_step"], 1)
                dve.wait_ge(S["modrow_step"], row_steps)

            def mixer_weights_lo():
                gates = mtmp[:, 0:2, :]
                work = mtmp[:, 2:4, :]
                do_row(dve.scalar_tensor_tensor(out=work, in0=gates, scalar=-1.0, in1=gates,
                                                op0=ALU.mult, op1=ALU.max))
                do_row(dve.tensor_scalar(work, work, GATE_MIN, None, ALU.max))
                do_row(dve.tensor_scalar(gates, gates, 0.0, 2.0, ALU.is_ge, ALU.mult))
                do_row(dve.scalar_tensor_tensor(out=gates, in0=gates, scalar=-1.0, in1=work,
                                                op0=ALU.add, op1=ALU.mult))
                do_row(dve.tensor_scalar(modrow[:, 0, :], mtmp[:, 0, :], 1 / WS, None, ALU.mult))
                dve.wait_ge(S["rows_loaded"], 48)
                do_row(dve.tensor_tensor(modrow[:, 4, :], mtmp[:, 1, :], gb_row[:, 0, :], ALU.mult))
                do_row(dve.tensor_tensor(modrow[:, 3, :], mtmp[:, 1, :], gb_row[:, 1, :], ALU.mult))
                dve.nop().then_inc(S["modrow_done"], 1)

                for k in range(KI):
                    split_lo(fc_w[:, 1, k * D:(k + 1) * D], fc_f[:, k * D:(k + 1) * D],
                             fc_w[:, 0, k * D:(k + 1) * D], 4, g16[:, k:k + 1])
                dve.wait_ge(S["fb_ps"], 1)
                dve.tensor_tensor(fc_bias[:, :], bank[6][:, 0:KD], cols[:, 3 * KI:3 * KI + KD], ALU.add)
                dve.drain().then_inc(S["w_lo"], 1)
                split_lo(out_w[:, 1, :], out_f, out_w[:, 0, :], 5)
                split_lo(comp_w[:, 1, :], bank[5][:, :], comp_w[:, 0, :], 6)
                split_lo(bias_lo[:, INNER:], bank[4][0:64, D:2 * D], bias_hi[:, INNER:], 7)
                dve.tensor_copy(colsum[:, :], bank[4][:, 0:D])
                dve.drain().then_inc(S["w_lo"], 1)
                dve.wait_ge(S["w_lo"], 5)
                dve.tensor_copy(bias_rows[0:1, INNER:], bias_hi[0:1, INNER:])
                dve.tensor_copy(bias_rows[32:33, INNER:], bias_lo[32:33, INNER:]).then_inc(S["w_lo"], 1)

            def body(i, front, mid, route, pre):
                if mid:
                    inner_stats(i - 1)
                if front:
                    h_lo(i, 0)
                    h_lo(i, 1)
                if mid:
                    hnT_lo(i - 1, 0)
                    hnT_lo(i - 1, 1)
                if pre:
                    ln1_stats(i + 1)
                if front:
                    h_lo(i, 2)
                if mid:
                    hnT_lo(i - 1, 2)
                if front:
                    h_lo(i, 3)
                if mid:
                    hnT_lo(i - 1, 3)
                if route:
                    ln2_stats(i - 2, 3)
                ln12(i, pre, route)
                if isinstance(i, int) and i == 0:
                    mixer_weights_lo()
                if front:
                    r_tile(i, 0)
                if mid:
                    for m in range(KD):
                        dve.wait_ge(S["s_hi"], (i - 1) * KD + m + 1)
                        dve.tensor_tensor(sT[:, 1, m, :], s_f[:, m, :], sT[:, 0, m, :], ALU.subtract)\
                            .then_inc(S["s_lo"], 1)
                if front:
                    r_tile(i, 1)
                if mid:
                    o_tile(i - 1, 0)
                if front:
                    r_tile(i, 2)
                if route and not mid:
                    h2_last(i - 2)
                if route:
                    top2(i - 2)
                if mid:
                    o_tile(i - 1, 1)
                if route:
                    slots(i - 2)
                if front:
                    r_tile(i, 3)
                if mid:
                    ln2_stats(i - 1, 0)
                    o_tile(i - 1, 2)
                if front:
                    ln_inner(i)
                if mid:
                    ln2_stats(i - 1, 1)
                    o_tile(i - 1, 3)
                    ln2_stats(i - 1, 2)

            dve.memset(conv_f, 0.0).then_inc(S["zeroed"], 1)
            dve.memset(hT[:, :, :, 0:PAD], 0.0)
            dve.memset(ones_f[:, :], 1.0)
            dve.memset(ones16[:, :], 1.0)
            dve.memset(mv_12[:, :, :], 1.0).then_inc(S["zeroed"], 1)
            dve.memset(bias_rows[:, :], 0.0).then_inc(S["zeroed"], 1)
            ln1_stats(0)
            dve.wait_ge(S["zeroed"], 3)
            ln12(-1, True, False)
            dve.wait_ge(S["cols_loaded"], 80)
            dve.tensor_scalar(g16[:, :], cols[:, 0:KI], WS, None, ALU.mult).then_inc(S["g16_ready"], 1)
            for k in range(KI):
                ins = dve.tensor_scalar(cpb_rep[:, k * 64:(k + 1) * 64], ones_f[:, 0:64],
                                        cols[:, 2 * KI + k:2 * KI + k + 1], None, ALU.mult)
            ins.then_inc(S["cpb_ready"], 1)
            dve.wait_ge(S["modT_ps"], 1)
            modT = bank[4][:, 0:4 * NB].rearrange("p (s k b) -> p s k b", s=2, k=KD)
            dve.tensor_copy(shiftT[:, :, :], modT[:, 0]).then_inc(S["modT_read"], 1)
            dve.tensor_scalar(scaleT[:, :, :], modT[:, 1], 1.0, None, ALU.add).then_inc(S["modT_read"], 1)
            split_lo(in_w[:, 1, :], in_f, in_w[:, 0, :], 1)
            dve.drain().then_inc(S["w_lo"], 1)
            dve.wait_ge(S["modrow_ps"], 1)

            do_row(dve.tensor_copy(mtmp[:, 0, :], bank[5][0:NB, 0:D]))
            do_row(dve.tensor_copy(modrow[:, 2, :], bank[5][0:NB, D:2 * D]))
            do_row(dve.tensor_scalar(modrow[:, 1, :], bank[3][0:NB, 0:D], 1.0, None, ALU.add))
            do_row(dve.tensor_copy(mtmp[:, 1, :], bank[3][0:NB, D:2 * D]))
            split_lo(conv_w[:, 1, :], conv_f, conv_w[:, 0, :], 2)
            split_lo(bias_lo[:, 0:INNER], convb_f[0:64, :], bias_hi[:, 0:INNER], 3)
            dve.drain().then_inc(S["w_lo"], 1)
            dve.wait_ge(S["w_lo"], 2)
            dve.tensor_copy(bias_rows[0:1, 0:INNER], bias_hi[0:1, 0:INNER])
            dve.tensor_copy(bias_rows[32:33, 0:INNER], bias_lo[32:33, 0:INNER]).then_inc(S["w_lo"], 1)

            dve.wait_ge(S["base_ready"], 1)
            dve.wait_ge(S["router_loaded"], 16 * (1 + SUB))

            run(dve, body)

            c2 = 0

            def do2(ins):
                nonlocal c2
                c2 += 1
                ins.then_inc(S["table_step"], 1)
                dve.wait_ge(S["table_step"], c2)

            do2(dve.tensor_tensor(cnt[:, :], base[:, :], region0, ALU.subtract))
            do2(dve.tensor_scalar(cnt[:, :], cnt[:, :], float(T - 1), None, ALU.add))
            do2(dve.tensor_copy(cnt_i[:, :], cnt[:, :]))
            do2(dve.tensor_scalar(cnt_s[:, :], cnt_i[:, :], T.bit_length() - 1, None, ALU.logical_shift_right))
            do2(dve.tensor_copy(nt[:, :], cnt_s[:, :]))
            do2(dve.tensor_scalar(nt[:, :], nt[:, :], 1.0, None, ALU.max))
            do2(dve.memset(g0[:, 0:1], 0.0))
            for e in range(NE):
                do2(dve.tensor_tensor(g0[:, e + 1:e + 2], g0[:, e:e + 1], nt[:, e:e + 1], ALU.add))
            do2(dve.tensor_copy(tab_nt[:, :], nt[:, :]))
            do2(dve.tensor_copy(tab_g0[:, :], g0[:, :]))
            dve.nop().then_inc(S["tables_ready"], 1)

            def w_split(n, buf):
                for q in range(WQ):
                    c = slice(q * (WE // WQ), (q + 1) * (WE // WQ))
                    dve.wait_ge(S["w_conv"], (n - 1) * WQ + q + 1)
                    dve.scalar_tensor_tensor(out=split_w[:, buf, 1, c], in0=stage_w[:, c], scalar=WS,
                                             in1=split_w[:, buf, 0, c], op0=ALU.mult, op1=ALU.subtract)\
                        .then_inc(S["w_ready"], 1)

            def xmT_lo(g):
                dve.wait_ge(S["xmT_hi"], g + 1)
                dve.tensor_tensor(xmT[:, 1, :, :].rearrange("p k t -> p (k t)"), bank[6][:, :],
                                  xmT[:, 0, :, :].rearrange("p k t -> p (k t)"), ALU.subtract)\
                    .then_inc(S["xmT_lo"], 1)

            dve.nop().then_inc(S["hm_lo"], 1)
            dve.nop().then_inc(S["yw_done"], 1)
            w_split(1, 0)
            xmT_lo(0)

            def expert(e, buf, has_next, has_after):
                first = dve.value_load(tab_g0[0:1, e:e + 1] if isinstance(e, int) else tab_g0[0:1, bass.ds(e, 1)],
                                       min_val=0, max_val=MAXT - 2)
                n = dve.value_load(tab_nt[0:1, e:e + 1] if isinstance(e, int) else tab_nt[0:1, bass.ds(e, 1)],
                                   min_val=1, max_val=MAXT - 2)
                with dve.Fori(0, n) as t:
                    g = dve.snap(first + t)
                    for q in range(KF // 2):
                        dve.wait_ge(S["hf_done"], g * KF + 2 * q + 3)
                        pair = hf[:, 2 * q:2 * q + 2, :]
                        dve.tensor_copy(hm[:, 0, 2 * q:2 * q + 2, :], pair).then_inc(S["hm_hi"], 1)
                        dve.wait_ge(S["hm_hi"], g * (KF // 2) + q + 1)
                        dve.tensor_tensor(hm[:, 1, 2 * q:2 * q + 2, :], pair, hm[:, 0, 2 * q:2 * q + 2, :],
                                          ALU.subtract).then_inc(S["hm_lo"], 1)
                    xmT_lo(g + 1)
                    if has_next:
                        with dve.If(t == 0):
                            w_split(e + 2, 1 - buf)
                    dve.wait_ge(S["b2w_done"], g + 1)
                    dve.wait_ge(S["rows_added"], g + 1)
                    dve.wait_ge(S["y_ps"], g + 2)
                    for j in range(TS):
                        dve.scalar_tensor_tensor(out=y_w[:, j, :], in0=bank[4 + j][:, 0:D],
                                                 scalar=wcur[:, j:j + 1], in1=b2w[:, j, :],
                                                 op0=ALU.mult, op1=ALU.add).then_inc(S["yw_done"], 1)

            expert_pairs(dve, expert)

            def stats(b):
                dve.wait_ge(FIN_LOADED[b], 16)
                for j in range(SUB):
                    dve.bn_stats(fin_st[:, b, j, :], fin_v[b][:, j, :]).then_inc(S["fin_step"], 1)
                for j in range(SUB):
                    dve.wait_ge(S["fin_step"], b * (2 * SUB) + j + 1)
                    dve.bn_aggr(fin_mv[:, b, j, :], fin_st[:, b, j, :]).then_inc(S["fin_step"], 1)
                dve.wait_ge(S["fin_step"], (b + 1) * (2 * SUB))
                dve.tensor_scalar(fin_mv[:, b, :, 1], fin_mv[:, b, :, 1], EPS, None, ALU.add)\
                    .then_inc(S["fin_var"], 1)

            def scale(b):
                dve.wait_ge(S["fin_sqrt"], b + 1)
                dve.reciprocal(fin_rstd[:, b, :], fin_std[:, b, :]).then_inc(S["fin_recip"], 1)
                dve.wait_ge(S["fin_recip"], b + 1)
                dve.scalar_tensor_tensor(out=fin_nbias[:, b, :], in0=fin_mv[:, b, :, 0], scalar=-1.0,
                                         in1=fin_rstd[:, b, :], op0=ALU.mult, op1=ALU.mult)\
                    .then_inc(S["fin_ready"], 1)

            def gate_rows(b):
                dve.wait_ge(S["fin_norm"], b + 1)
                dve.wait_ge(S["fin_g_loaded"], 16)
                dve.tensor_tensor(fin_v[b], fin_v[b], fin_g[:, b:b + 1, :].to_broadcast([P, SUB, D]), ALU.mult)\
                    .then_inc(S["fin_mul"], 1)

            LAG = 1
            stats(0)
            for b in range(NB):
                if b + 1 < NB:
                    stats(b + 1)
                scale(b)
                if b >= LAG and b - LAG not in GATED_BY_POOL:
                    gate_rows(b - LAG)
            for b in range(NB - LAG, NB):
                if b not in GATED_BY_POOL:
                    gate_rows(b)

        @block.tensor
        def _(pe):
            def win(hl, k, lo, n):
                return in_w[:, hl, k * 2 * INNER + lo:k * 2 * INNER + lo + n]

            def turn_x(b, chunks=range(KD)):
                for k in chunks:
                    if not (isinstance(b, int) and b == 0):
                        if isinstance(b, int) and b <= 1:
                            pe.wait_ge(S["xT_f32"], KD * b)
                        elif isinstance(b, int) and b == 2:
                            pe.wait_ge(S["hnT_lo"], SUB)
                        else:
                            pe.wait_ge(S["h2T_done"], (b - 3) * KD + k + 1)
                    if k == 0:
                        pe.wait_ge(S["xn_done"], b + 1)
                    for j in range(SUB):
                        mm = pe.transpose(bank[6 + k][:, j * P:(j + 1) * P], xn[:, j, k * P:(k + 1) * P],
                                          ident[:, :])
                    mm.then_inc(S["xT_ps"], 1)

            def proj_h(b, m):
                if m == 0:
                    pe.wait_ge(S["xT_lo"], (b + 1) * KD)
                if m < 2:
                    if isinstance(b, int) and b == 1:
                        pe.wait_ge(S["h_lo"], KI)
                    elif not (isinstance(b, int) and b == 0):
                        pe.wait_ge(S["s_f32"], (b - 2) * KD + m + 1)
                else:
                    pe.wait_ge(S["h_lo"], b * KI + m - 1)
                for k in range(KD):
                    mm = three(pe, bank[m % 2][:, :], (win(0, k, m * P, P), win(1, k, m * P, P)),
                               (xT[:, 0, k, :], xT[:, 1, k, :]), k == 0, k == KD - 1)
                mm.then_inc(S["h_ps"], 1)

            def proj_gate(b, j):
                if not (isinstance(b, int) and b * SUB + j == 0):
                    pe.wait_ge(S["gate_done"], b * SUB + j)
                t = slice(j * P, (j + 1) * P)
                for k in range(KD):
                    mm = three(pe, bank[2][:, :], (xT[:, 0, k, t], xT[:, 1, k, t]),
                               (win(0, k, INNER, INNER), win(1, k, INNER, INNER)), k == 0, k == KD - 1)
                mm.then_inc(S["gate_ps"], 1)

            def conv(b, j):
                if not (isinstance(b, int) and b * SUB + j == 0):
                    pe.wait_ge(S["r_done"], b * SUB + j)
                pe.matmul(bank[3][:, :], ones16[0:BIAS_K, :], bias_rows[0:BIAS_K, 0:INNER],
                          start=True, stop=False)
                for c in range(KI):
                    if j == 0:
                        pe.wait_ge(S["h_lo"], b * KI + c + 1)
                    for t in range(TAPS):
                        w = (c * TAPS + t) * P
                        tt = slice(j * P + t, j * P + t + P)
                        mm = three(pe, bank[3][:, c * P:(c + 1) * P], (hT[:, 0, c, tt], hT[:, 1, c, tt]),
                                   (conv_w[:, 0, w:w + P], conv_w[:, 1, w:w + P]), False,
                                   c == KI - 1 and t == TAPS - 1)
                mm.then_inc(S["conv_ps"], 1)

            def turn_hn(b, j):
                if j < 2:
                    if isinstance(b, int) and b == NB - 1:
                        pe.wait_ge(S["h2T_done"], (b - 1) * KD)
                    else:
                        pe.wait_ge(S["xT_f32"], (b + 1) * KD + j + 1)
                else:
                    pe.wait_ge(S["hnT_lo"], b * SUB + j - 1)
                pe.wait_ge(S["hn_done"], b * SUB + j + 1)
                for k in range(KI):
                    mm = pe.transpose(bank[6 + j % 2][:, k * P:(k + 1) * P], r_sb[:, j, k * P:(k + 1) * P],
                                      ident[:, :])
                mm.then_inc(S["hnT_ps"], 1)

            def fc(b, m, front):
                if m == 0:
                    pe.wait_ge(S["hnT_lo"], (b + 1) * SUB)
                if front:
                    pe.wait_ge(S["h_lo"], (b + 1) * KI + 3 + m)
                for k in range(KI):
                    w = k * D + m * P
                    mm = three(pe, bank[m][:, :], (fc_w[:, 0, w:w + P], fc_w[:, 1, w:w + P]),
                               (hnT[:, 0, k, :], hnT[:, 1, k, :]), k == 0, k == KI - 1)
                mm.then_inc(S["u_ps"], 1)

            def out_proj(b, j):
                if not (isinstance(b, int) and b * SUB + j == 0):
                    pe.wait_ge(S["t_done"], b * SUB + j)
                if j == 0:
                    pe.wait_ge(S["s_lo"], (b + 1) * KD)
                t = slice(j * P, (j + 1) * P)
                for k in range(KI):
                    three(pe, bank[5][:, 0:D], (hnT[:, 0, k, t], hnT[:, 1, k, t]),
                          (out_w[:, 0, k * D:(k + 1) * D], out_w[:, 1, k * D:(k + 1) * D]), k == 0, k == KI - 1)
                pe.matmul(bank[5][:, D:2 * D], ones16[0:BIAS_K, :], bias_rows[0:BIAS_K, INNER:],
                          start=True, stop=False)
                for k in range(KD):
                    mm = three(pe, bank[5][:, D:2 * D], (sT[:, 0, k, t], sT[:, 1, k, t]),
                               (comp_w[:, 0, k * D:(k + 1) * D], comp_w[:, 1, k * D:(k + 1) * D]),
                               False, k == KD - 1)
                mm.then_inc(S["o_ps"], 1)

            def turn_h2(b, mid):
                rows = h2x if mid else h2x_last
                pe.wait_ge(S["row_done"], (b + 1) * SUB)
                for k in range(KD):
                    if mid:
                        pe.wait_ge(S["hnT_lo"], (b + 1) * SUB + 3 + k)
                    else:
                        pe.wait_ge(S["h2T_done"], b * KD)
                    for j in range(SUB):
                        mm = pe.transpose(bank[6 + k][:, j * P:(j + 1) * P], rows[:, j, k * P:(k + 1) * P],
                                          ident[:, :])
                    mm.then_inc(S["h2T_ps"], 1)

            def logits(b):
                pe.wait_ge(S["h2T_done"], (b + 1) * KD)
                if not (isinstance(b, int) and b == 0):
                    pe.wait_ge(S["slots_done"], b)
                for j in range(SUB):
                    for k in range(KD):
                        mm = pe.matmul(bank[4][:, j * NE:(j + 1) * NE], h2T[:, k, j * P:(j + 1) * P],
                                       router_w[:, k, :], start=(k == 0), stop=(k == KD - 1))
                mm.then_inc(S["lg_ps"], 1)

            def ranks(b):
                pe.wait_ge(S["mask_done"], b + 1)
                R0 = SUB * NE
                pe.matmul(bank[4][:, R0:2 * R0], before[:, :], chosen[:, :, :].rearrange("p j e -> p (j e)"),
                          start=True, stop=False)
                for j in range(SUB - 1):
                    pe.matmul(bank[4][:, R0 + (j + 1) * NE:2 * R0], ones16[:, :],
                              chosen[:, j:j + 1, :].to_broadcast([P, SUB - 1 - j, NE]),
                              start=False, stop=(j == SUB - 2))
                for j in range(SUB):
                    mm = pe.matmul(bank[4][:, 2 * R0:2 * R0 + NE], ones16[:, :], chosen[:, j, :],
                                   start=(j == 0), stop=(j == SUB - 1))
                mm.then_inc(S["rank_ps"], 1)

            def mixer_products():
                pe.wait_ge(S["modT_read"], 2)
                pe.wait_ge(S["out_loaded"], 16)
                pe.wait_ge(S["cpb_ready"], 1)
                for k in range(KI):
                    pe.matmul(bank[4][:, 0:D], ones_f[:, :], out_f[:, k * D:(k + 1) * D],
                              start=(k == 0), stop=(k == KI - 1))
                for k in range(KI):
                    mm = pe.matmul(bank[4][0:64, D:2 * D], cpb_rep[:, k * 64:(k + 1) * 64], out_f[:, k * D:(k + 1) * D],
                                   start=(k == 0), stop=(k == KI - 1))
                mm.then_inc(S["colsum_ps"], 1)
                pe.wait_ge(S["cproj_loaded"], 16)
                pe.wait_ge(S["modrow_step"], 4)
                for m in range(KD):
                    for k in range(KI):
                        w = k * D + m * P
                        mm = pe.matmul(bank[5][:, m * D:(m + 1) * D], cproj_f[:, w:w + P], out_f[:, k * D:(k + 1) * D],
                                       start=(k == 0), stop=(k == KI - 1))
                mm.then_inc(S["comp_ps"], 1)
                pe.wait_ge(S["fc_loaded"], 16)
                pe.wait_ge(S["xT_f32"], KD)
                for m in range(KD):
                    for k in range(KI):
                        w = k * D + m * P
                        mm = pe.matmul(bank[6][:, m:m + 1], fc_f[:, w:w + P], cols[:, KI + k:KI + k + 1],
                                       start=(k == 0), stop=(k == KI - 1))
                mm.then_inc(S["fb_ps"], 1)

            def body(i, front, mid, route, pre):
                if isinstance(i, int) and i == 0:
                    pe.wait_ge(S["w_lo"], 1)
                if front:
                    proj_h(i, 0)
                    proj_h(i, 1)
                    proj_gate(i, 0)
                if mid:
                    turn_hn(i - 1, 0)
                    turn_hn(i - 1, 1)
                if front:
                    proj_h(i, 2)
                if mid:
                    turn_hn(i - 1, 2)
                if front:
                    proj_h(i, 3)
                if mid:
                    turn_hn(i - 1, 3)
                if front:
                    if isinstance(i, int) and i == 0:
                        mixer_products()
                        pe.wait_ge(S["w_lo"], 3)
                    conv(i, 0)
                if mid:
                    if isinstance(i, int) and i == 1:
                        pe.wait_ge(S["w_lo"], 6)
                    fc(i - 1, 0, front)
                    fc(i - 1, 1, front)
                if front:
                    proj_gate(i, 1)
                    conv(i, 1)
                if mid:
                    out_proj(i - 1, 0)
                if route:
                    turn_h2(i - 2, mid)
                if front:
                    proj_gate(i, 2)
                    conv(i, 2)
                if route:
                    logits(i - 2)
                if mid:
                    out_proj(i - 1, 1)
                if front:
                    proj_gate(i, 3)
                if route:
                    ranks(i - 2)
                if isinstance(i, int) and i == 0:
                    pe.wait_ge(S["w_lo"], 4)
                if pre:
                    turn_x(i + 1, range(KD - 1))
                if front:
                    conv(i, 3)
                if mid:
                    out_proj(i - 1, 2)
                if pre:
                    turn_x(i + 1, range(KD - 1, KD))
                if mid:
                    out_proj(i - 1, 3)

            pe.wait_ge(S["silu_c_done"], 1)
            pe.wait_ge(S["ident_ready"], 4)
            pe.wait_ge(S["wmod_first_loaded"], 16)
            for s in range(2):
                for m in range(KD):
                    o = (s * KD + m) * NB
                    for k in range(KD):
                        w = k * 6 * D + s * D + m * P
                        mm = pe.matmul(bank[4][:, o:o + NB], wmod_f[:, w:w + P], silu_c[:, k * NB:(k + 1) * NB],
                                       start=(k == 0), stop=(k == KD - 1))
            mm.then_inc(S["modT_ps"], 1)
            turn_x(0)
            pe.wait_ge(S["wmod_rest_loaded"], 16)
            for r, bk in ((0, 5), (1, 3)):
                for k in range(KD):
                    w = k * 6 * D + (2 + 2 * r) * D
                    mm = pe.matmul(bank[bk][0:NB, 0:2 * D], silu_c[:, k * NB:(k + 1) * NB], wmod_f[:, w:w + 2 * D],
                                   start=(k == 0), stop=(k == KD - 1))
            mm.then_inc(S["modrow_ps"], 1)
            run(pe, body)

            def turn_m(g):
                pe.wait_ge(S["xm_loaded"], (g + 1) * 16)
                for j in range(TS):
                    for k in range(KD):
                        o = k * T + j * P
                        mm = pe.transpose(bank[6][:, o:o + P], xm[:, j, k * P:(k + 1) * P], ident[:, :])
                mm.then_inc(S["xmT_ps"], 1)

            pe.nop().then_inc(S["y_ps"], 1)
            pe.nop().then_inc(S["xmT_ps"], 1)
            pe.wait_ge(S["tables_ready"], 1)
            turn_m(0)

            def expert(e, buf, has_next, has_after):
                first = pe.value_load(tab_g0[0:1, e:e + 1] if isinstance(e, int) else tab_g0[0:1, bass.ds(e, 1)],
                                      min_val=0, max_val=MAXT - 2)
                n = pe.value_load(tab_nt[0:1, e:e + 1] if isinstance(e, int) else tab_nt[0:1, bass.ds(e, 1)],
                                  min_val=1, max_val=MAXT - 2)
                wait_alone(pe, S["w_ready"], (e + 1) * WQ)

                def w1(hl, k, c):
                    o = k * FF + c * P
                    return split_w[:, buf, hl, o:o + P]

                def w2(hl, c):
                    o = KD * FF + c * D
                    return split_w[:, buf, hl, o:o + D]

                with pe.Fori(0, n) as t:
                    g = pe.snap(first + t)
                    pe.wait_ge(S["xmT_lo"], g + 1)
                    for c in range(KF):
                        if c == 0:
                            pe.wait_ge(S["hf_done"], g * KF + 1)
                        for k in range(KD):
                            mm = three(pe, bank[c // 2][:, (c % 2) * T:(c % 2 + 1) * T],
                                       (w1(0, k, c), w1(1, k, c)), (xmT[:, 0, k, :], xmT[:, 1, k, :]),
                                       k == 0, k == KD - 1)
                        if c % 2 == 1:
                            mm.then_inc(S["l1_ps"], 1)
                    turn_m(g + 1)
                    pe.wait_ge(S["yw_done"], g * TS + 1)
                    for c in range(KF):
                        pe.wait_ge(S["hm_lo"], g * (KF // 2) + c // 2 + 2)
                        for j in range(TS):
                            mm = three(pe, bank[4 + j][:, 0:D],
                                       (hm[:, 0, c, j * P:(j + 1) * P], hm[:, 1, c, j * P:(j + 1) * P]),
                                       (w2(0, c), w2(1, c)), c == 0, c == KF - 1)
                    mm.then_inc(S["y_ps"], 1)

            expert_pairs(pe, expert)


_LAYOUT = {
    "x": lambda d: d["L0_attn_hidden_states"],
    "in_wT": lambda d: d["L0_attn_in_proj_w"].T,
    "convT": lambda d: d["L0_attn_conv_w"].reshape(4, 2, 64, 64, 4).transpose(0, 1, 3, 4, 2),
    "conv_b": lambda d: d["L0_attn_conv_b"],
    "ln_g": lambda d: d["L0_attn_ln_g"].reshape(-1, 128).T,
    "ln_b": lambda d: d["L0_attn_ln_b"].reshape(-1, 128).T,
    "fcT": lambda d: d["L0_attn_fc_w"].T,
    "fc_b": lambda d: d["L0_attn_fc_b"].reshape(-1, 128).T,
    "cproj": lambda d: d["L0_attn_cproj_w"],
    "cproj_b": lambda d: d["L0_attn_cproj_b"].reshape(-1, 128).T,
    "outT": lambda d: d["L0_attn_out_w"].T,
    "WrT": lambda d: d["L0_ffn_Wr"].T,
    "br": lambda d: d["L0_ffn_br"],
    "W1T": lambda d: d["L0_ffn_W1"].transpose(0, 2, 1),
    "b1": lambda d: d["L0_ffn_b1"].reshape(-1, 128).T,
    "W2T": lambda d: d["L0_ffn_W2"].transpose(0, 2, 1),
    "b2": lambda d: d["L0_ffn_b2"].reshape(-1),
    "gamma": lambda d: d["L0_ffn_gamma"],
    "beta": lambda d: d["L0_ffn_beta"],
    "cT": lambda d: d["L0_c"].T.reshape(2, 128, 8).transpose(1, 0, 2).reshape(128, 16),
    "wmod": lambda d: d["L0_wmod"],
}


def kernel(**inputs):
    import numpy as np
    import concourse.bacc as bacc
    from concourse.bass_utils import run_bass_kernel_spmd

    nc = bacc.Bacc("TRN2", target_bir_lowering=False, num_devices=1)
    arrays, args = {}, {}
    for name, lay in _LAYOUT.items():
        a = np.ascontiguousarray(lay({k: np.asarray(v) for k, v in inputs.items()}))
        arrays[f"in_{name}"] = a
        args[name] = nc.dram_tensor(f"in_{name}", a.shape, F32, kind="ExternalInput").ap()
    shape = tuple(inputs["L0_attn_hidden_states"].shape)
    args["out"] = nc.dram_tensor("out_x", shape, F32, kind="ExternalOutput").ap()
    adaln_kernel(nc, **args)
    r = run_bass_kernel_spmd(nc, [arrays], core_ids=[0])
    return r.results[0]["out_x"]
```
